# Optimizing a Trainium2 kernel written in Bass

```python
import numpy as np
import jax
import jax.numpy as jnp

def _softmax(x, axis=-1):
    return jax.nn.softmax(x, axis=axis)

def _gelu(x):
    return jax.nn.gelu(x, approximate=True)

def _silu(x):
    return jax.nn.silu(x)

def _sigmoid(x):
    return jax.nn.sigmoid(x)

def _layernorm(x, axis=-1, eps=1e-05):
    m = jnp.mean(x, axis=axis, keepdims=True)
    v = jnp.var(x, axis=axis, keepdims=True)
    return (x - m) / jnp.sqrt(v + eps)

def _scatter_add(tgt, idx, src, axis=0):
    return tgt.at[idx].add(src)

def _segment_sum(src, seg, n):
    return jax.ops.segment_sum(src, seg, n)
kernel_name = 'mk_decoder_preln_d1_seqx_r4_13e25a'

def setup_inputs(seed: int=0):
    np.random.seed(seed)
    _w = jnp.asarray

    def _rec_inputs():
        import jax
        import jax.numpy as jnp
        _rk = jax.random.key(seed)
        x = -0.0002928 + 1 * jax.random.normal(jax.random.fold_in(_rk, 1), (16, 256, 256), jnp.float32)
        _lenS = 256 - jax.random.randint(jax.random.fold_in(_rk, 7), (16,), 0, max(1, 256 // 4) + 1, jnp.int32)
        _lenS2 = 77 - jax.random.randint(jax.random.fold_in(_rk, 8), (16,), 0, max(1, 77 // 4) + 1, jnp.int32)
        _ctx_1024P = jax.random.normal(jax.random.fold_in(_rk, 11), (16, 16, 256), jnp.float32)
        _ctx_1024c = jax.random.dirichlet(jax.random.fold_in(_rk, 511), 0.3 * jnp.ones((16,), jnp.float32), (16, 77))
        _ctx_1024t = jnp.einsum('bsk,bkd->bsd', _ctx_1024c, _ctx_1024P)
        _ctx_1024t = _ctx_1024t * jax.lax.rsqrt(jnp.mean(jnp.square(_ctx_1024t)) + 1e-12) * 0.953939
        ctx_1024 = -1.39393e-06 + 0.999914 * (_ctx_1024t + 0.3 * jax.random.normal(jax.random.fold_in(_rk, 611), (16, 77, 256), jnp.float32))
        _validS = jnp.arange(256)[None, :] < _lenS[:, None]
        _validS2 = jnp.arange(77)[None, :] < _lenS2[:, None]
        _causal = jnp.tril(jnp.ones((256, 256), dtype=bool))
        mask_Bx1x1xS2_if1 = jnp.where(jnp.ones((16, 1, 1, 77), dtype=bool), 1, 0).astype(jnp.int32)
        return (x, ctx_1024, mask_Bx1x1xS2_if1)
    x, ctx_1024, mask_Bx1x1xS2_if1 = _rec_inputs()

    def _L0_attn_setup():
        import jax, jax.numpy as jnp
        import numpy as np
        B, N, F, H = (2, 512, 256, 16)
        HD = F // H
        SQRT_D = float(np.sqrt(F))
        key = jax.random.key(seed)
        ks = jax.random.split(key, 9)
        s = 1.0 / np.sqrt(F)
        mk = lambda k: jax.random.uniform(k, (F, F), jnp.float32, -s, s)
        mb = lambda k: jax.random.uniform(k, (F,), jnp.float32, -s, s)
        return {'x': jax.random.normal(ks[0], (B, N, F), jnp.float32), 'Wq': mk(ks[1]), 'bq': mb(ks[2]), 'Wk': mk(ks[3]), 'bk': mb(ks[4]), 'Wv': mk(ks[5]), 'bv': mb(ks[6]), 'Wo': mk(ks[7]), 'bo': mb(ks[8])}
    _L0_attn_all = _L0_attn_setup()
    _L0_attn_in = {k: v for k, v in _L0_attn_all.items() if k in ('Wq', 'bq', 'Wk', 'bk', 'Wv', 'bv', 'Wo', 'bo')}
    del _L0_attn_all

    def _L0_xattn_setup():
        import jax, jax.numpy as jnp
        import numpy as np
        D_MODEL = 256
        N_HEAD = 16

        def _split(x, n_head):
            B, S, D = x.shape
            return x.reshape(B, S, n_head, D // n_head).transpose(0, 2, 1, 3)
        key = jax.random.key(seed)
        ks = jax.random.split(key, 12)
        B, S, D = (2, 512, D_MODEL)
        std = 1.0 / np.sqrt(D)
        inp = {'Q': jax.random.normal(ks[0], (B, S, D), jnp.float32), 'K': jax.random.normal(ks[1], (B, S, D), jnp.float32), 'V': jax.random.normal(ks[2], (B, S, D), jnp.float32), 'mask': jnp.ones((B, 1, 1, S), jnp.int32), 'Wq': jax.random.normal(ks[3], (D, D), jnp.float32) * std, 'bq': jax.random.normal(ks[4], (D,), jnp.float32) * std, 'Wk': jax.random.normal(ks[5], (D, D), jnp.float32) * std, 'bk': jax.random.normal(ks[6], (D,), jnp.float32) * std, 'Wv': jax.random.normal(ks[7], (D, D), jnp.float32) * std, 'bv': jax.random.normal(ks[8], (D,), jnp.float32) * std, 'Wo': jax.random.normal(ks[9], (D, D), jnp.float32) * std, 'bo': jax.random.normal(ks[10], (D,), jnp.float32) * std}
        return inp
    _L0_xattn_all = _L0_xattn_setup()
    _L0_xattn_in = {k: v for k, v in _L0_xattn_all.items() if k in ('Wq', 'bq', 'Wk', 'bk', 'Wv', 'bv', 'Wo', 'bo')}
    del _L0_xattn_all

    def _L0_ffn_setup():
        import jax, jax.numpy as jnp
        import numpy as np
        EPS = 1e-12

        def rms_norm(t, gamma):
            n = jnp.maximum(jnp.linalg.norm(t, axis=-1, keepdims=True), EPS)
            scale = jnp.sqrt(jnp.asarray(t.shape[-1], t.dtype))
            return t / n * scale * gamma
        key = jax.random.key(seed)
        ks = jax.random.split(key, 4)
        b, s, d = (4, 1024, 256)
        e, t = (8, 128)
        hidden = 4 * d
        return {'x': jax.random.normal(ks[0], (b, s, d), dtype=jnp.float32), 'gamma_x': jnp.ones((d,), dtype=jnp.float32), 'gamma_slot': jnp.ones((d,), dtype=jnp.float32), 'slot_embeds': jax.random.normal(ks[1], (e, t, d), dtype=jnp.float32), 'w1': jax.random.normal(ks[2], (d, hidden), dtype=jnp.float32) * (1.0 / np.sqrt(d)), 'w2': jax.random.normal(ks[3], (hidden, d), dtype=jnp.float32) * (1.0 / np.sqrt(hidden))}
    _L0_ffn_all = _L0_ffn_setup()
    _L0_ffn_in = {k: v for k, v in _L0_ffn_all.items() if k in ('gamma_x', 'gamma_slot', 'slot_embeds', 'w1', 'w2')}
    del _L0_ffn_all
    return {'x': x, 'ctx_1024': ctx_1024, 'mask_Bx1x1xS2_if1': mask_Bx1x1xS2_if1, 'L0_attn_Wq': _L0_attn_in['Wq'], 'L0_attn_bq': _L0_attn_in['bq'], 'L0_attn_Wk': _L0_attn_in['Wk'], 'L0_attn_bk': _L0_attn_in['bk'], 'L0_attn_Wv': _L0_attn_in['Wv'], 'L0_attn_bv': _L0_attn_in['bv'], 'L0_attn_Wo': _L0_attn_in['Wo'], 'L0_attn_bo': _L0_attn_in['bo'], 'L0_xattn_Wq': _L0_xattn_in['Wq'], 'L0_xattn_bq': _L0_xattn_in['bq'], 'L0_xattn_Wk': _L0_xattn_in['Wk'], 'L0_xattn_bk': _L0_xattn_in['bk'], 'L0_xattn_Wv': _L0_xattn_in['Wv'], 'L0_xattn_bv': _L0_xattn_in['bv'], 'L0_xattn_Wo': _L0_xattn_in['Wo'], 'L0_xattn_bo': _L0_xattn_in['bo'], 'L0_ffn_gamma_x': _L0_ffn_in['gamma_x'], 'L0_ffn_gamma_slot': _L0_ffn_in['gamma_slot'], 'L0_ffn_slot_embeds': _L0_ffn_in['slot_embeds'], 'L0_ffn_w1': _L0_ffn_in['w1'], 'L0_ffn_w2': _L0_ffn_in['w2']}

def reference(x, ctx_1024, mask_Bx1x1xS2_if1, L0_attn_Wq, L0_attn_bq, L0_attn_Wk, L0_attn_bk, L0_attn_Wv, L0_attn_bv, L0_attn_Wo, L0_attn_bo, L0_xattn_Wq, L0_xattn_bq, L0_xattn_Wk, L0_xattn_bk, L0_xattn_Wv, L0_xattn_bv, L0_xattn_Wo, L0_xattn_bo, L0_ffn_gamma_x, L0_ffn_gamma_slot, L0_ffn_slot_embeds, L0_ffn_w1, L0_ffn_w2):
    import jax
    import jax.numpy as jnp

    def _L0_attn_ref(x, Wq, bq, Wk, bk, Wv, bv, Wo, bo):
        import jax, jax.numpy as jnp
        import numpy as np
        B, N, F, H = (2, 512, 256, 16)
        HD = F // H
        SQRT_D = float(np.sqrt(F))
        b, n, f = x.shape
        q = (x @ Wq.T + bq).reshape(b, n, H, HD)
        k = (x @ Wk.T + bk).reshape(b, n, H, HD)
        v = (x @ Wv.T + bv).reshape(b, n, H, HD)
        score = jnp.einsum('bihd,bjhd->bhij', q, k)
        attn = jax.nn.softmax(score / SQRT_D, axis=-1)
        o = jnp.einsum('bhij,bjhd->bihd', attn, v).reshape(b, n, f)
        return o @ Wo.T + bo

    def _L0_xattn_ref(Q, K, V, mask, Wq, bq, Wk, bk, Wv, bv, Wo, bo):
        import jax, jax.numpy as jnp
        import numpy as np
        D_MODEL = 256
        N_HEAD = 16

        def _split(x, n_head):
            B, S, D = x.shape
            return x.reshape(B, S, n_head, D // n_head).transpose(0, 2, 1, 3)
        q = _split(Q @ Wq.T + bq, N_HEAD)
        k = _split(K @ Wk.T + bk, N_HEAD)
        v = _split(V @ Wv.T + bv, N_HEAD)
        d_head = k.shape[-1]
        scale = 1.0 / jnp.sqrt(jnp.asarray(d_head, q.dtype))
        score = jnp.einsum('bhqd,bhkd->bhqk', q, k) * scale
        score = jnp.where(mask == 0, -jnp.inf, score)
        attn = jax.nn.softmax(score, axis=-1)
        out = jnp.einsum('bhqk,bhkd->bhqd', attn, v)
        B, H, S, dh = out.shape
        out = out.transpose(0, 2, 1, 3).reshape(B, S, H * dh)
        return out @ Wo.T + bo

    def _L0_ffn_ref(x, gamma_x, gamma_slot, slot_embeds, w1, w2):
        import jax, jax.numpy as jnp
        import numpy as np
        EPS = 1e-12

        def rms_norm(t, gamma):
            n = jnp.maximum(jnp.linalg.norm(t, axis=-1, keepdims=True), EPS)
            scale = jnp.sqrt(jnp.asarray(t.shape[-1], t.dtype))
            return t / n * scale * gamma
        b, s, d = x.shape
        e, t, _ = slot_embeds.shape
        xn = rms_norm(x, gamma_x)
        se = rms_norm(slot_embeds, gamma_slot)
        logits = jnp.einsum('bsd,etd->bset', xn, se)
        dispatch = jax.nn.softmax(logits, axis=1)
        slots = jnp.einsum('bsd,bset->betd', xn, dispatch)
        h = jax.nn.gelu(slots @ w1, approximate=False)
        processed = h @ w2
        combine = jax.nn.softmax(logits.reshape(b, s, e * t), axis=-1)
        out = jnp.einsum('bnd,bsn->bsd', processed.reshape(b, e * t, d), combine)
        return out
    x = x + _L0_attn_ref(_layernorm(x, axis=-1), L0_attn_Wq, L0_attn_bq, L0_attn_Wk, L0_attn_bk, L0_attn_Wv, L0_attn_bv, L0_attn_Wo, L0_attn_bo)
    x = x + _L0_xattn_ref(_layernorm(x, axis=-1), ctx_1024, ctx_1024, mask_Bx1x1xS2_if1, L0_xattn_Wq, L0_xattn_bq, L0_xattn_Wk, L0_xattn_bk, L0_xattn_Wv, L0_xattn_bv, L0_xattn_Wo, L0_xattn_bo)
    x = x + _L0_ffn_ref(_layernorm(x, axis=-1), L0_ffn_gamma_x, L0_ffn_gamma_slot, L0_ffn_slot_embeds, L0_ffn_w1, L0_ffn_w2)
    return x

_drawn_inputs = setup_inputs


def setup_inputs(seed=0):
    import zlib

    import numpy as np

    out = dict(_drawn_inputs(seed))
    spreads = {'L0_ffn_gamma_x': (1.0, 0.2), 'L0_ffn_gamma_slot': (1.0, 0.2)}
    factors = {'L0_attn_Wq': 8.0,
     'L0_attn_bq': 8.0,
     'L0_attn_Wk': 8.0,
     'L0_attn_bk': 64.0,
     'L0_xattn_bk': 64.0,
     'L0_xattn_bq': 2.681}
    for name, (base, spread) in spreads.items():
        noise = np.random.default_rng([zlib.crc32(name.encode()), seed]).standard_normal(out[name].shape)
        drawn = base * np.exp(spread * noise) if base else spread * noise
        out[name] = jnp.asarray(drawn.astype(out[name].dtype))
    for name, factor in factors.items():
        out[name] = (out[name] * factor).astype(out[name].dtype)
    return out
```

```python
import concourse.bass as bass
from concourse import mybir
from concourse.alu_op_type import AluOpType as ALU
from contextlib import ExitStack
import numpy as np

B, S, D = 16, 256, 256
H, HD = 16, 16
CTX = 77
E, TS, HID = 8, 128, 1024
SLOTS = E * TS
P = 128
NT = S // P
ND = D // P
G, R = 4, 4
PADW = 160
CHUNK = 256
NC = SLOTS // CHUNK
NS = SLOTS // P
NM = HID // P
LN_EPS, RMS_EPS = 1e-5, 1e-12
BM, NMASK, EXPO, BQ, BK, BQ2, NCOLS = 0, 4, 5, 8, 12, 16, 20
ATTN_SCALE, XATTN_SCALE = 1.0 / 16.0, 1.0 / 4.0

PER = dict(
    x_in=16, ctx_in=16, mask_in=16, out=16,
    ln1_st=1, ln1_mv=1, ln1_rs=2, ln1_xh=1, xt1_ps=1, xt1_hi=1, xt1_lo=1,
    ln2_st=1, ln2_mv=1, ln2_rs=2, ln2_xh=1, xt2_ps=1, xt2_hi=1, xt2_lo=1,
    ln3_st=1, ln3_mv=1, ln3_rs=8, ln3_xh=1, xt3_ps=1, xt3_hi=1, xt3_lo=1,
    x_bo=1, v_ps=1, v_sb=1, vg_hi=4, vg_lo=4, qk_ps=4, qk_sb=4, qk_hi=4, qk_lo=4,
    s_ps=16, mx=16, ex=16, rl=16, pn=16, t_ps=16, pt_hi=16, pt_lo=16, pv=16, ot_hi=4, ot_lo=4,
    o_ps=1, x1=1, ct_hi=1, ct_lo=1, kv_ps=1, kd_sb=1, v2_sb=1, k2t_ps=1, k2_f=1, k2_hi=1, k2_lo=1,
    q2_ps=2, q2_sb=2, q2_hi=2, q2_a=2, mk=2, s2_ps=2, s2_sb=2, mx2=2, sh2=2, ex2=2, sm2=2, rl2=2,
    pn2=2, t2_ps=4, pt2_hi=4, pt2_lo=4, vg2_hi=4, vg2_lo=4, pv2=4, ot2_hi=4, ot2_lo=4,
    o2_ps=1, x1_bo=1, x2=1, xs_hi=1, xs_lo=1, lg_ps=2, lg_sb=2, rm=2, ec=2, rr=1,
    lt_ps=4, cm=4, ed=4, rc=4, edn=4, cb_ps=4, cb_hi=4, cb_lo=4, ds_ps=4, ds_hi=4, ds_lo=4,
    sl_ps=4, sl_hi=4, sl_lo=4,
    h_ps=16, ge=16, h_hi=16, h_lo=16, pr_ps=4, pr_hi=4, pr_lo=4, d_ps=4, y=4,
)

WEIGHTS = ("wqk", "wv", "wo", "wkv2", "wq2", "wo2", "w1", "w2")


def decoder_layer(nc, t_in, out):
    f32, f32r, i32 = mybir.dt.float32, mybir.dt.float32r, mybir.dt.int32
    ACT = mybir.ActivationFunctionType
    AX = mybir.AxisListType.X
    KB = 1024

    ctx = ExitStack()
    with ctx:
        base = [nc.sbuf_base + (-nc.sbuf_base) % 64]
        end = nc.sbuf_usable_end

        def region(nbytes):
            at = base[0]
            base[0] = at + nbytes + (-nbytes) % 32
            assert base[0] <= end, (base[0], end)
            return at

        def at(name, shape, dt, offset):
            return nc.alloc_sbuf_tensor_at(name, shape, dt, offset=offset)

        def sb(name, shape, dt=f32):
            return at(name, shape, dt, region(4 * int(np.prod(shape[1:]))))

        def pair(name, shape):
            return sb(name + "_hi", shape, f32r), sb(name + "_lo", shape, f32r)

        W = dict(
            wqk=pair("wqk", [P, ND, 2 * 512]), wv=pair("wv", [P, ND, D]), wo=pair("wo", [P, G, D]),
            wkv2=pair("wkv2", [P, ND, 2 * D]), wq2=pair("wq2", [P, ND, 512]), wo2=pair("wo2", [P, G, D]),
            w1=pair("w1", [P, ND, HID]), w2=pair("w2", [P, NM, D]), se=pair("se", [P, ND, SLOTS]),
        )
        r_slots = region(16 * KB)
        sl_hi = at("sl_hi", [P, ND, SLOTS], f32r, r_slots)
        sl_lo = at("sl_lo", [P, ND, SLOTS], f32r, r_slots + 8 * KB)
        s2 = at("s2", [P, NT, H * CTX], f32, r_slots)
        r_comb = region(16 * KB)
        cb_hi = at("cb_hi", [P, NS, S], f32r, r_comb)
        cb_lo = at("cb_lo", [P, NS, S], f32r, r_comb + 8 * KB)
        lg = at("lg", [P, NT, SLOTS], f32, r_comb)
        ecomb = at("ecomb", [P, NT, SLOTS], f32, r_comb + 8 * KB)
        k2_hi = at("k2_hi", [P, G, R * CTX], f32r, r_comb)
        k2_lo = at("k2_lo", [P, G, R * CTX], f32r, r_comb + 5 * KB)
        k2_f = at("k2_f", [P, G, R * CTX], f32, r_comb + 5 * KB)
        r_hid = region(16 * KB)
        h_hi = at("h_hi", [P, NM, CHUNK], f32r, r_hid)
        h_lo = at("h_lo", [P, NM, CHUNK], f32r, r_hid + 8 * KB)
        h_f = at("h_f", [P, NM, CHUNK], f32, r_hid + 8 * KB)
        ds_hi = at("ds_hi", [P, NT, SLOTS], f32r, r_hid)
        ds_lo = at("ds_lo", [P, NT, SLOTS], f32r, r_hid + 8 * KB)
        q2_a = at("q2_a", [P, G, S], f32r, r_hid)
        q2_f = at("q2_f", [P, G, S], f32, r_hid)
        q2_h = at("q2_h", [P, G, S], f32r, r_hid + 4 * KB)
        pt2_hi = at("pt2_hi", [CTX, R, S], f32r, r_hid + 8 * KB)
        pt2_lo = at("pt2_lo", [CTX, R, S], f32r, r_hid + 12 * KB)
        r_proc = region(8 * KB)
        pr_hi = at("pr_hi", [P, 2, D], f32r, r_proc)
        pr_lo = at("pr_lo", [P, 2, D], f32r, r_proc + 2 * KB)
        edt = at("edt", [P, NS, S], f32, r_proc)
        k2d = at("k2d", [CTX, H, 2, HD], f32, r_proc)
        v2_f = at("v2_f", [CTX, D], f32, r_proc + 2 * KB)
        x = sb("x", [P, NT, D])
        x2 = sb("x2", [P, NT, D])
        xt_hi, xt_lo = pair("xt", [P, ND, S])
        r_qk = region(2 * KB)
        qk_f = at("qk_f", [P, 2, S], f32, r_qk)
        qk_l = at("qk_l", [P, 2, S], f32r, r_qk)
        qk_h = sb("qk_h", [P, 2, S], f32r)
        v_f = sb("v_f", [P, NT, D])
        vg = sb("vg", [P, NT, R, PADW], f32r)
        r_p = region(4 * KB)
        p_sb = at("p_sb", [P, 2, NT, S], f32, r_p)
        x1 = at("x1", [P, NT, D], f32, r_p)
        xh = at("xh", [P, NT, D], f32, r_p + 2 * KB)
        r_pt = region(8 * KB)
        pt_hi = at("pt_hi", [P, 2, NT, S], f32r, r_pt)
        pt_lo = at("pt_lo", [P, 2, NT, S], f32r, r_pt + 4 * KB)
        xs_hi = at("xs_hi", [P, NT, D], f32r, r_pt)
        xs_lo = at("xs_lo", [P, NT, D], f32r, r_pt + 2 * KB)
        ot_hi, ot_lo = pair("ot", [P, G, S])
        cx = sb("cx", [P, ND, CTX])
        cx_hi, cx_lo = pair("cxs", [P, ND, CTX])
        mk_i = sb("mk_i", [P, CTX], i32)
        mk_f = sb("mk_f", [P, CTX])
        consts = sb("consts", [P, P + NCOLS])
        ident = consts[:, 0:P]
        cols = consts[:, P:P + NCOLS]
        biases = sb("biases", [P, 5 * D])
        bv, bo, bo2 = (biases[:, i * D:(i + 1) * D] for i in (0, 1, 4))
        bkv2 = biases[0:CTX, 2 * D:4 * D]
        st = sb("st", [P, NT, 6])
        mv = sb("mv", [P, NT, 2])
        rs = sb("rs", [P, 6, NT])
        mx = sb("mx", [P, H, NT])
        ls = sb("ls", [P, H, NT])
        rl = sb("rl", [P, H, NT])
        mx2 = sb("mx2", [P, NT, H])
        ls2 = sb("ls2", [P, NT, H])
        rl2 = sb("rl2", [P, NT, H])
        rm = sb("rm", [P, NT])
        rsum = sb("rsum", [P, NT])
        rrec = sb("rrec", [P, NT])
        cm = sb("cm", [P, NS])
        csum = sb("csum", [P, NS])
        crec = sb("crec", [P, NS])
        gam = sb("gam", [P, 2, ND])
        gxs = sb("gxs", [P, ND])
        stage = dict(
            wqk=at("g_wqk", [P, ND, 1024], f32, r_slots), wv=at("g_wv", [P, ND, D], f32, r_slots + 8 * KB),
            wo=at("g_wo", [P, G, D], f32, r_slots + 10 * KB), wkv2=at("g_wkv2", [P, ND, 512], f32, r_comb),
            wq2=at("g_wq2", [P, ND, 512], f32, r_comb + 4 * KB), wo2=at("g_wo2", [P, G, D], f32, r_comb + 8 * KB),
            w1=at("g_w1", [P, ND, HID], f32, r_hid), w2=at("g_w2", [P, NM, D], f32, r_hid + 8 * KB),
        )
        g_se = at("g_se", [P, NS, D], f32, r_proc)
        se_t = at("se_t", [P, ND, SLOTS], f32, r_pt)
        se_sq = at("se_sq", [P, NS, D], f32, r_pt)
        se_ss, se_n, se_i, se_sc = (sb(n, [P, NS]) for n in ("se_ss", "se_n", "se_i", "se_sc"))
        ps = ctx.enter_context(nc.psum_tensor("ps", [P, 8, 512], f32))

        s = {n: ctx.enter_context(nc.semaphore("s_" + n)) for n in PER}
        for n in ("i_const", "i_bias", "pool_held", "dve_held", "i_cols", "i_vz", "i_se", "i_gam", "i_gxs", "i_hi", "i_lo", "i_w1g",
                  "i_st", "i_sq", "i_sr", "i_xn", "i_sps", "i_sg", "i_shi", "i_slo"):
            s[n] = ctx.enter_context(nc.semaphore("s_" + n))
        for n in WEIGHTS:
            s["i_" + n] = ctx.enter_context(nc.semaphore("s_i_" + n))

        def nth(name, b, k):
            return b * PER[name] + k

        def later(b):
            return not isinstance(b, int) or b > 0

        block = ctx.enter_context(nc.Block())

        @block.tensor
        def _(pe):
            te = nc.tensor

            def three(o, lhs, rhs, first, last):
                te.matmul(o, lhs[0], rhs[0], start=first, stop=False)
                te.matmul(o, lhs[1], rhs[0], start=False, stop=False)
                return te.matmul(o, lhs[0], rhs[1], start=False, stop=last)

            def both(t, *ix):
                return tuple(u.__getitem__(ix) for u in t)

            full = slice(None)
            XT, OT, SL, CB, DS, HH, PR, XS, CX = ((xt_hi, xt_lo), (ot_hi, ot_lo), (sl_hi, sl_lo), (cb_hi, cb_lo),
                                                  (ds_hi, ds_lo), (h_hi, h_lo), (pr_hi, pr_lo), (xs_hi, xs_lo),
                                                  (cx_hi, cx_lo))

            def xt(b, n):
                pe.wait_ge(s[f"ln{n}_xh"], nth(f"ln{n}_xh", b, 1))
                for dk in range(ND):
                    for t in range(NT):
                        last = te.transpose(ps[:, 0, dk * S + t * P:dk * S + (t + 1) * P],
                                            xh[:, t, dk * P:(dk + 1) * P], ident[:, :])
                last.then_inc(s[f"xt{n}_ps"], 1)

            def v_proj(b):
                pe.wait_ge(s["xt1_lo"], nth("xt1_lo", b, 1))
                for t in range(NT):
                    for dk in range(ND):
                        last = three(ps[:, 1, t * D:(t + 1) * D], both(XT, full, dk, slice(t * P, t * P + P)),
                                     both(W["wv"], full, dk), dk == 0, dk == ND - 1)
                last.then_inc(s["v_ps"], 1)

            def qk_proj(b, g, woven):
                pe.wait_ge(s["xt1_lo"], nth("xt1_lo", b, 1))
                if g:
                    pe.wait_ge(s["qk_sb"], nth("qk_sb", b, g))
                    if woven is not None:
                        pe.wait_ge(s["y"], nth("y", woven, g))
                for i in range(2):
                    for dk in range(ND):
                        c0 = i * 512 + g * P
                        last = three(ps[:, 7, i * S:(i + 1) * S], both(W["wqk"], full, dk, slice(c0, c0 + P)),
                                     both(XT, full, dk), dk == 0, dk == ND - 1)
                last.then_inc(s["qk_ps"], 1)

            def scores(b, h):
                g, r = divmod(h, R)
                rows = slice(32 * r, 32 * r + 32)
                pe.wait_ge(s["qk_lo"], nth("qk_lo", b, g + 1))
                if h >= 2:
                    pe.wait_ge(s["ex"], nth("ex", b, h - 1))
                if h == 0:
                    pe.wait_ge(s["v_sb"], nth("v_sb", b, 1))
                for t in range(NT):
                    for k, keys in enumerate((qk_h, qk_l)):
                        last = te.matmul(ps[:, 1 + h % 2, t * S:(t + 1) * S], qk_l[rows, 0, t * P:(t + 1) * P],
                                         keys[rows, 1, :], start=k == 0, stop=k == 1)
                last.then_inc(s["s_ps"], 1)

            def transp(b, h):
                pe.wait_ge(s["pn"], nth("pn", b, h + 1))
                if h >= 2:
                    pe.wait_ge(s["pt_lo"], nth("pt_lo", b, h - 1))
                for j in range(NT):
                    for t in range(NT):
                        last = te.transpose(ps[:, 3 + h % 2, j * S + t * P:j * S + (t + 1) * P],
                                            p_sb[:, h % 2, t, j * P:(j + 1) * P], ident[:, :])
                last.then_inc(s["t_ps"], 1)

            def pv(b, h):
                g, r = divmod(h, R)
                pe.wait_ge(s["pt_lo"], nth("pt_lo", b, h + 1))
                pe.wait_ge(s["vg_lo"], nth("vg_lo", b, g + 1))
                if g and r == 0:
                    pe.wait_ge(s["ot_lo"], nth("ot_lo", b, g))
                for j in range(NT):
                    v = vg[:, j, :, :].rearrange("p r w -> p (r w)")[:, r * P:(r + 1) * P]
                    for k, pt in enumerate((pt_hi, pt_lo)):
                        last = te.matmul(ps[:, 0, 0:S], v, pt[:, h % 2, j, :], start=r == 0 and j == 0 and k == 0,
                                         stop=r == R - 1 and j == NT - 1 and k == 1)
                last.then_inc(s["pv"], 1)

            def hidden(b, c, q):
                n = c * 4 + q
                if n == 0:
                    pe.wait_ge(s["sl_lo"], nth("sl_lo", b, 4))
                    pe.wait_ge(s["ds_lo"], nth("ds_lo", b, 4))
                if n >= 2:
                    pe.wait_ge(s["ge"], nth("ge", b, n - 1))
                for i in range(2):
                    m = 2 * q + i
                    for dk in range(ND):
                        last = three(ps[:, 5 + n % 2, i * CHUNK:(i + 1) * CHUNK],
                                     both(W["w1"], full, dk, slice(m * P, m * P + P)),
                                     both(SL, full, dk, slice(c * CHUNK, (c + 1) * CHUNK)), dk == 0, dk == ND - 1)
                last.then_inc(s["h_ps"], 1)

            def processed(b, c, e, woven):
                if e == 0:
                    pe.wait_ge(s["h_lo"], nth("h_lo", b, 4 * c + 4))
                    if woven is not None:
                        pe.wait_ge(s["qk_sb"], nth("qk_sb", woven, c + 1))
                    if c:
                        pe.wait_ge(s["y"], nth("y", b, c))
                for k in range(NM):
                    last = three(ps[:, 7, e * D:(e + 1) * D], both(HH, full, k, slice(e * P, e * P + P)),
                                 both(W["w2"], full, k), k == 0, k == NM - 1)
                if e == 1:
                    last.then_inc(s["pr_ps"], 1)

            def combine(b, c):
                pe.wait_ge(s["pr_lo"], nth("pr_lo", b, c + 1))
                for t in range(NT):
                    for e in range(2):
                        last = three(ps[:, 7, t * D:(t + 1) * D], both(CB, full, 2 * c + e, slice(t * P, t * P + P)),
                                     both(PR, full, e), e == 0, e == 1)
                last.then_inc(s["d_ps"], 1)

            def stage_a(a):
                xt(a, 1)
                v_proj(a)

            def group(c, b=None, a=None):
                h = 4 * c
                if a is not None:
                    qk_proj(a, c, b)
                if b is not None:
                    for q in range(4):
                        hidden(b, c, q)
                if a is not None:
                    if c:
                        pv(a, h - 2)
                        pv(a, h - 1)
                    scores(a, h)
                    scores(a, h + 1)
                if b is not None:
                    processed(b, c, 0, a)
                if a is not None:
                    transp(a, h)
                    transp(a, h + 1)
                    scores(a, h + 2)
                    scores(a, h + 3)
                if b is not None:
                    processed(b, c, 1, a)
                if a is not None:
                    pv(a, h)
                    pv(a, h + 1)
                    transp(a, h + 2)
                    transp(a, h + 3)
                if b is not None:
                    combine(b, c)

            def stage_b(b):
                pe.wait_ge(s["ct_lo"], nth("ct_lo", b, 1))
                if later(b):
                    pe.wait_ge(s["h_lo"], nth("h_lo", b - 1, 16))
                for dk in range(ND):
                    last = three(ps[0:CTX, 5, :], both(CX, full, dk), both(W["wkv2"], full, dk), dk == 0, dk == ND - 1)
                last.then_inc(s["kv_ps"], 1)
                pe.wait_ge(s["kd_sb"], nth("kd_sb", b, 1))
                for g in range(G):
                    kd = k2d[:, :, :, :].rearrange("p h e d -> p (h e d)")[:, g * P:(g + 1) * P]
                    last = te.transpose(ps[:, 6, g * CTX:(g + 1) * CTX], kd, ident[0:CTX, 0:CTX])
                last.then_inc(s["k2t_ps"], 1)
                pv(b, H - 2)
                pv(b, H - 1)
                pe.wait_ge(s["ex"], nth("ex", b, H))
                pe.wait_ge(s["ot_lo"], nth("ot_lo", b, G))
                for t in range(NT):
                    for g in range(G):
                        last = three(ps[:, 1, t * D:(t + 1) * D], both(OT, full, g, slice(t * P, t * P + P)),
                                     both(W["wo"], full, g), g == 0, g == G - 1)
                last.then_inc(s["o_ps"], 1)
                xt(b, 2)
                pe.wait_ge(s["xt2_lo"], nth("xt2_lo", b, 1))
                for g in range(G):
                    for dk in range(ND):
                        last = three(ps[:, 2 + g // 2, (g % 2) * S:(g % 2 + 1) * S],
                                     both(W["wq2"], full, dk, slice(g * P, g * P + P)), both(XT, full, dk),
                                     dk == 0, dk == ND - 1)
                    if g % 2:
                        last.then_inc(s["q2_ps"], 1)
                pe.wait_ge(s["q2_a"], nth("q2_a", b, 2))
                pe.wait_ge(s["k2_lo"], nth("k2_lo", b, 1))
                pe.wait_ge(s["x1"], nth("x1", b, 1))
                if later(b):
                    pe.wait_ge(s["y"], nth("y", b - 1, 4))
                for t in range(NT):
                    for g in range(G):
                        for k, keys in enumerate((k2_hi, k2_lo)):
                            last = te.matmul(ps[:, 4 * t + g, 0:R * CTX], q2_a[:, g, t * P:(t + 1) * P], keys[:, g, :],
                                             start=k == 0, stop=k == 1)
                    last.then_inc(s["s2_ps"], 1)
                def transp2(g):
                    if g == 0:
                        pe.wait_ge(s["pn2"], nth("pn2", b, 2))
                    if g >= 2:
                        pe.wait_ge(s["pt2_lo"], nth("pt2_lo", b, g - 1))
                    for r in range(R):
                        for t in range(NT):
                            c0 = (g * R + r) * CTX
                            last = te.transpose(ps[0:CTX, 2 * (g % 2) + r // 2, (r % 2) * S + t * P:(r % 2) * S + (t + 1) * P],
                                                s2[:, t, c0:c0 + CTX], ident[:, :])
                    last.then_inc(s["t2_ps"], 1)

                transp2(0)
                for g in range(G):
                    if g + 1 < G:
                        transp2(g + 1)
                    pe.wait_ge(s["pt2_lo"], nth("pt2_lo", b, g + 1))
                    pe.wait_ge(s["vg2_lo"], nth("vg2_lo", b, g + 1))
                    if g >= 2:
                        pe.wait_ge(s["ot2_lo"], nth("ot2_lo", b, g - 1))
                    for r in range(R):
                        v = vg[0:CTX, g % 2, :, :].rearrange("p r w -> p (r w)")[:, r * P:(r + 1) * P]
                        for k, pt in enumerate((pt2_hi, pt2_lo)):
                            last = te.matmul(ps[:, 4 + g % 2, 0:S], v, pt[:, r, :], start=r == 0 and k == 0,
                                             stop=r == R - 1 and k == 1)
                    last.then_inc(s["pv2"], 1)
                pe.wait_ge(s["ot2_lo"], nth("ot2_lo", b, G))
                for t in range(NT):
                    for g in range(G):
                        last = three(ps[:, 6, t * D:(t + 1) * D], both(OT, full, g, slice(t * P, t * P + P)),
                                     both(W["wo2"], full, g), g == 0, g == G - 1)
                last.then_inc(s["o2_ps"], 1)
                xt(b, 3)
                pe.wait_ge(s["xt3_lo"], nth("xt3_lo", b, 1))
                for t in range(NT):
                    for u in range(2):
                        for dk in range(ND):
                            last = three(ps[:, 2 + 2 * t + u, :], both(XT, full, dk, slice(t * P, t * P + P)),
                                         both(W["se"], full, dk, slice(u * 512, u * 512 + 512)), dk == 0, dk == ND - 1)
                    last.then_inc(s["lg_ps"], 1)
                pe.wait_ge(s["lg_sb"], nth("lg_sb", b, 2))
                pe.wait_ge(s["x2"], nth("x2", b, 1))
                for k in range(4):
                    for e in (2 * k, 2 * k + 1):
                        for t in range(NT):
                            last = te.transpose(ps[:, (6 + k) % 8, (e % 2) * S + t * P:(e % 2) * S + (t + 1) * P],
                                                lg[:, t, e * P:(e + 1) * P], ident[:, :])
                    last.then_inc(s["lt_ps"], 1)
                pe.wait_ge(s["ec"], nth("ec", b, 2))
                for k in range(4):
                    for e in (2 * k, 2 * k + 1):
                        for t in range(NT):
                            last = te.transpose(ps[:, 2 + k, (e % 2) * S + t * P:(e % 2) * S + (t + 1) * P],
                                                ecomb[:, t, e * P:(e + 1) * P], ident[:, :])
                    last.then_inc(s["cb_ps"], 1)
                pe.wait_ge(s["edn"], nth("edn", b, 4))
                for t in range(NT):
                    for u in range(2):
                        for e in range(4 * u, 4 * u + 4):
                            last = te.transpose(ps[:, (6 + 2 * t + u) % 8, (e % 4) * P:(e % 4 + 1) * P],
                                                edt[:, e, t * P:(t + 1) * P], ident[:, :])
                        last.then_inc(s["ds_ps"], 1)
                pe.wait_ge(s["cb_lo"], nth("cb_lo", b, 4))
                pe.wait_ge(s["ds_lo"], nth("ds_lo", b, 4))
                pe.wait_ge(s["xs_lo"], nth("xs_lo", b, 1))
                for dk in range(ND):
                    for u in range(2):
                        for t in range(NT):
                            last = three(ps[:, 2 + 2 * dk + u, :], both(XS, full, t, slice(dk * P, dk * P + P)),
                                         both(DS, full, t, slice(u * 512, u * 512 + 512)), t == 0, t == NT - 1)
                        last.then_inc(s["sl_ps"], 1)

            pe.wait_ge(s["i_const"], 16)
            pe.wait_ge(s["i_xn"], 1)
            for dk in range(ND):
                for e in range(NS):
                    last = te.transpose(ps[:, 2 * dk + e // 4, (e % 4) * P:(e % 4 + 1) * P],
                                        g_se[:, e, dk * P:(dk + 1) * P], ident[:, :])
            last.then_inc(s["i_sps"], 1)
            pe.wait_ge(s["i_slo"], 1)
            pe.wait_ge(s["i_lo"], len(WEIGHTS))
            stage_a(0)
            for c in range(NC):
                group(c, a=0)
            stage_b(0)
            with pe.Fori(0, B - 1) as b:
                stage_a(b + 1)
                for c in range(NC):
                    group(c, b, b + 1)
                stage_b(b + 1)
            for c in range(NC):
                group(c, b=B - 1)

        @block.scalar
        def _(act):
            def copy(o, i):
                return nc.scalar.activation(o, i, ACT.Copy)

            def xt(b, n):
                act.wait_ge(s[f"xt{n}_ps"], nth(f"xt{n}_ps", b, 1))
                if n == 1 and later(b):
                    act.wait_ge(s["lg_ps"], nth("lg_ps", b - 1, 2))
                copy(xt_hi[:, :, :], ps[:, 0, :].rearrange("p (k s) -> p k s", k=ND)).then_inc(s[f"xt{n}_hi"], 1)

            def qk_copy(b, g):
                act.wait_ge(s["qk_ps"], nth("qk_ps", b, g + 1))
                if g:
                    act.wait_ge(s["s_ps"], nth("s_ps", b, 4 * g))
                nc.scalar.activation(qk_f[:, 0, :], ps[:, 7, 0:S], ACT.Identity, scale=ATTN_SCALE,
                                     bias=cols[:, BQ + g:BQ + g + 1])
                nc.scalar.activation(qk_f[:, 1, :], ps[:, 7, S:2 * S], ACT.Identity,
                                     bias=cols[:, BK + g:BK + g + 1]).then_inc(s["qk_sb"], 1)

            def exps(b, h):
                act.wait_ge(s["mx"], nth("mx", b, h + 1))
                if h >= 2:
                    act.wait_ge(s["t_ps"], nth("t_ps", b, h - 1))
                for t in range(NT):
                    last = nc.scalar.activation(p_sb[:, h % 2, t, :], ps[:, 1 + h % 2, t * S:(t + 1) * S], ACT.Exp,
                                                bias=mx[:, h, t:t + 1], accum_out=ls[:, h, t:t + 1])
                last.then_inc(s["ex"], 1)

            def pt_split(b, h):
                act.wait_ge(s["t_ps"], nth("t_ps", b, h + 1))
                if h >= 2:
                    act.wait_ge(s["pv"], nth("pv", b, h - 1))
                copy(pt_hi[:, h % 2, :, :], ps[:, 3 + h % 2, :].rearrange("p (j s) -> p j s", j=NT))\
                    .then_inc(s["pt_hi"], 1)

            def ot_split(b, g):
                act.wait_ge(s["pv"], nth("pv", b, 4 * g + 4))
                copy(ot_hi[:, g, :], ps[:, 0, 0:S]).then_inc(s["ot_hi"], 1)

            def gelu(b, c, q):
                n = 4 * c + q
                act.wait_ge(s["h_ps"], nth("h_ps", b, n + 1))
                if c and q == 0:
                    act.wait_ge(s["pr_ps"], nth("pr_ps", b, c))
                nc.scalar.activation(h_f[:, 2 * q:2 * q + 2, :], ps[:, 5 + n % 2, :].rearrange("p (m s) -> p m s", m=2),
                                     ACT.Gelu).then_inc(s["ge"], 1)

            def pr_split(b, c):
                act.wait_ge(s["pr_ps"], nth("pr_ps", b, c + 1))
                if c:
                    act.wait_ge(s["d_ps"], nth("d_ps", b, c))
                copy(pr_hi[:, :, :], ps[:, 7, :].rearrange("p (e d) -> p e d", e=2)).then_inc(s["pr_hi"], 1)

            def group(c, b=None, a=None):
                h = 4 * c
                if a is not None:
                    if c:
                        pt_split(a, h - 2)
                        pt_split(a, h - 1)
                    qk_copy(a, c)
                if b is not None:
                    for q in range(4):
                        gelu(b, c, q)
                if a is not None:
                    if c:
                        ot_split(a, c - 1)
                    exps(a, h)
                    exps(a, h + 1)
                    pt_split(a, h)
                    pt_split(a, h + 1)
                    exps(a, h + 2)
                    exps(a, h + 3)
                if b is not None:
                    pr_split(b, c)

            def stage_b(b):
                pt_split(b, H - 2)
                pt_split(b, H - 1)
                ot_split(b, G - 1)
                act.wait_ge(s["k2_f"], nth("k2_f", b, 1))
                copy(k2_hi[:, :, :], k2_f[:, :, :]).then_inc(s["k2_hi"], 1)
                xt(b, 2)
                for u in range(2):
                    act.wait_ge(s["q2_ps"], nth("q2_ps", b, u + 1))
                    for g in (2 * u, 2 * u + 1):
                        last = nc.scalar.activation(q2_f[:, g, :], ps[:, 2 + u, (g % 2) * S:(g % 2 + 1) * S],
                                                    ACT.Identity, scale=XATTN_SCALE, bias=cols[:, BQ2 + g:BQ2 + g + 1])
                    last.then_inc(s["q2_sb"], 1)
                for t in range(NT):
                    act.wait_ge(s["sh2"], nth("sh2", b, t + 1))
                    nc.scalar.activation(s2[:, t, :], s2[:, t, :], ACT.Exp).then_inc(s["ex2"], 1)
                for g in range(G):
                    act.wait_ge(s["t2_ps"], nth("t2_ps", b, g + 1))
                    if g:
                        act.wait_ge(s["pv2"], nth("pv2", b, g))
                    copy(pt2_hi[:, :, :], ps[0:CTX, 2 * (g % 2):2 * (g % 2) + 2, :]
                         .rearrange("p k (r s) -> p (k r) s", r=2)).then_inc(s["pt2_hi"], 1)
                    if g == 0:
                        act.wait_ge(s["o_ps"], nth("o_ps", b, 1))
                    act.wait_ge(s["pv2"], nth("pv2", b, g + 1))
                    copy(ot_hi[:, g, :], ps[:, 4 + g % 2, 0:S]).then_inc(s["ot2_hi"], 1)
                xt(b, 3)
                for t in range(NT):
                    act.wait_ge(s["lg_ps"], nth("lg_ps", b, t + 1))
                    copy(lg[:, t, :], ps[:, 2 + 2 * t:4 + 2 * t, :].rearrange("p u n -> p (u n)"))\
                        .then_inc(s["lg_sb"], 1)
                for t in range(NT):
                    act.wait_ge(s["rm"], nth("rm", b, t + 1))
                    nc.scalar.activation(ecomb[:, t, :], lg[:, t, :], ACT.Exp, bias=rm[:, t:t + 1],
                                         accum_out=rsum[:, t:t + 1]).then_inc(s["ec"], 1)
                for k in range(4):
                    act.wait_ge(s["cm"], nth("cm", b, k + 1))
                    for e in (2 * k, 2 * k + 1):
                        last = nc.scalar.activation(edt[:, e, :], ps[:, (6 + k) % 8, (e % 2) * S:(e % 2 + 1) * S],
                                                    ACT.Exp, bias=cm[:, e:e + 1], accum_out=csum[:, e:e + 1])
                    last.then_inc(s["ed"], 1)
                act.wait_ge(s["cb_ps"], nth("cb_ps", b, 4))
                for k in range(4):
                    copy(cb_hi[:, 2 * k:2 * k + 2, :], ps[:, 2 + k, :].rearrange("p (e s) -> p e s", e=2))\
                        .then_inc(s["cb_hi"], 1)
                for t in range(NT):
                    for u in range(2):
                        act.wait_ge(s["ds_ps"], nth("ds_ps", b, 2 * t + u + 1))
                        copy(ds_hi[:, t, u * 512:(u + 1) * 512], ps[:, (6 + 2 * t + u) % 8, :])\
                            .then_inc(s["ds_hi"], 1)
                for dk in range(ND):
                    for u in range(2):
                        act.wait_ge(s["sl_ps"], nth("sl_ps", b, 2 * dk + u + 1))
                        copy(sl_hi[:, dk, u * 512:(u + 1) * 512], ps[:, 2 + 2 * dk + u, :]).then_inc(s["sl_hi"], 1)

            for n, name in enumerate(WEIGHTS):
                act.wait_ge(s["i_" + name], 16)
                if name == "w1":
                    act.wait_ge(s["i_w1g"], 1)
                copy(W[name][0][:, :, :], stage[name][:, :, :]).then_inc(s["i_hi"], 1)
            act.wait_ge(s["i_sg"], 2)
            copy(W["se"][0][:, :, :], se_t[:, :, :]).then_inc(s["i_shi"], 1)
            act.wait_ge(s["i_cols"], 1)
            xt(0, 1)
            for c in range(NC):
                group(c, a=0)
            stage_b(0)
            with act.Fori(0, B - 1) as b:
                xt(b + 1, 1)
                for c in range(NC):
                    group(c, b, b + 1)
                stage_b(b + 1)
            for c in range(NC):
                group(c, b=B - 1)

        @block.vector
        def _(dve):
            V = nc.vector

            def minus(o, a, hi):
                return V.tensor_tensor(o, a, hi.bitcast(f32), ALU.subtract)

            def norm(b, n, src):
                if n == 1:
                    dve.wait_ge(s["x_in"], nth("x_in", b, 16))
                if n == 2:
                    dve.wait_ge(s["x1"], nth("x1", b, 1))
                if n == 3:
                    dve.wait_ge(s["x2"], nth("x2", b, 1))
                for t in range(NT):
                    last = V.bn_stats(st[:, t, :], src[:, t, :])
                last.then_inc(s[f"ln{n}_st"], 1)
                dve.wait_ge(s[f"ln{n}_st"], nth(f"ln{n}_st", b, 1))
                dve.sem_inc(s["dve_held"], 1)
                for t in range(NT):
                    last = V.bn_aggr(mv[:, t, :], st[:, t, :])
                last.then_inc(s[f"ln{n}_mv"], 1)
                k = PER[f"ln{n}_rs"]
                dve.wait_ge(s[f"ln{n}_rs"], nth(f"ln{n}_rs", b, k))
                for t in range(NT):
                    last = V.tensor_scalar(xh[:, t, :], src[:, t, :], mv[:, t, 0:1], rs[:, 5, t:t + 1],
                                           ALU.subtract, ALU.mult)
                last.then_inc(s[f"ln{n}_xh"], 1)

            def xt(b, n):
                dve.wait_ge(s[f"xt{n}_hi"], nth(f"xt{n}_hi", b, 1))
                minus(xt_lo[:, :, :], ps[:, 0, :].rearrange("p (k s) -> p k s", k=ND), xt_hi[:, :, :])\
                    .then_inc(s[f"xt{n}_lo"], 1)

            def v_copy(b):
                dve.wait_ge(s["v_ps"], nth("v_ps", b, 1))
                V.tensor_tensor(v_f[:, :, :], ps[:, 1, :].rearrange("p (t d) -> p t d", t=NT),
                                bv[:, :].unsqueeze(1).broadcast_to([P, NT, D]), ALU.add).then_inc(s["v_sb"], 1)

            def qk_split(b, g):
                dve.wait_ge(s["qk_hi"], nth("qk_hi", b, g + 1))
                V.scalar_tensor_tensor(qk_l[:, 0, :], qk_h[:, 0, :].bitcast(f32), cols[:, NMASK:NMASK + 1],
                                       qk_f[:, 0, :], ALU.mult, ALU.add)
                minus(qk_l[:, 1, :], qk_f[:, 1, :], qk_h[:, 1, :]).then_inc(s["qk_lo"], 1)

            def maxima(b, h):
                dve.wait_ge(s["s_ps"], nth("s_ps", b, h + 1))
                V.tensor_reduce(mx[:, h, :], ps[:, 1 + h % 2, :].rearrange("p (t s) -> p t s", t=NT), AX, ALU.max,
                                negate=True).then_inc(s["mx"], 1)

            def recips(b, h):
                dve.wait_ge(s["ex"], nth("ex", b, h + 1))
                V.reciprocal(rl[:, h, :], ls[:, h, :]).then_inc(s["rl"], 1)

            def pt_split(b, h):
                dve.wait_ge(s["pt_hi"], nth("pt_hi", b, h + 1))
                minus(pt_lo[:, h % 2, :, :], ps[:, 3 + h % 2, :].rearrange("p (j s) -> p j s", j=NT),
                      pt_hi[:, h % 2, :, :]).then_inc(s["pt_lo"], 1)

            def ot_split(b, g):
                dve.wait_ge(s["ot_hi"], nth("ot_hi", b, g + 1))
                minus(ot_lo[:, g, :], ps[:, 0, 0:S], ot_hi[:, g, :]).then_inc(s["ot_lo"], 1)

            def h_split(b, c, q):
                n = 4 * c + q
                dve.wait_ge(s["h_hi"], nth("h_hi", b, n + 1))
                minus(h_lo[:, 2 * q:2 * q + 2, :], h_f[:, 2 * q:2 * q + 2, :], h_hi[:, 2 * q:2 * q + 2, :])\
                    .then_inc(s["h_lo"], 1)

            def pr_split(b, c):
                dve.wait_ge(s["pr_hi"], nth("pr_hi", b, c + 1))
                minus(pr_lo[:, :, :], ps[:, 7, :].rearrange("p (e d) -> p e d", e=2), pr_hi[:, :, :])\
                    .then_inc(s["pr_lo"], 1)

            def add_out(b, c):
                dve.wait_ge(s["d_ps"], nth("d_ps", b, c + 1))
                if c:
                    dve.wait_ge(s["y"], nth("y", b, c))
                for t in range(NT):
                    last = V.scalar_tensor_tensor(x2[:, t, :], ps[:, 7, t * D:(t + 1) * D], rrec[:, t:t + 1],
                                                  x2[:, t, :], ALU.mult, ALU.add)
                last.then_inc(s["y"], 1)

            def group(c, b=None, a=None):
                h = 4 * c
                if a is not None:
                    if c:
                        pt_split(a, h - 2)
                        pt_split(a, h - 1)
                    qk_split(a, c)
                if b is not None:
                    for q in range(4):
                        h_split(b, c, q)
                if a is not None:
                    maxima(a, h)
                    maxima(a, h + 1)
                    if c:
                        ot_split(a, c - 1)
                    recips(a, h)
                    recips(a, h + 1)
                    pt_split(a, h)
                    pt_split(a, h + 1)
                    maxima(a, h + 2)
                    maxima(a, h + 3)
                    recips(a, h + 2)
                    recips(a, h + 3)
                if b is not None:
                    pr_split(b, c)
                    add_out(b, c)

            def stage_a(a):
                norm(a, 1, x)
                xt(a, 1)
                v_copy(a)

            def stage_b(b):
                dve.wait_ge(s["kv_ps"], nth("kv_ps", b, 1))
                kin = ps[0:CTX, 5, 0:D].rearrange("p (h d) -> p h d", h=H)
                kb = bkv2[:, 0:D].rearrange("p (h d) -> p h d", h=H)
                for e in range(2):
                    last = V.tensor_tensor(k2d[:, :, e, :], kin, kb, ALU.add)
                last.then_inc(s["kd_sb"], 1)
                V.tensor_tensor(v2_f[:, :], ps[0:CTX, 5, D:2 * D], bkv2[:, D:2 * D], ALU.add).then_inc(s["v2_sb"], 1)
                dve.wait_ge(s["mask_in"], nth("mask_in", b, 16))
                V.tensor_scalar(mk_f[:, :], mk_i[:, :], 0.0, -3.0e38, ALU.is_equal, ALU.mult).then_inc(s["mk"], 1)
                dve.wait_ge(s["mk"], nth("mk", b, 1))
                V.tensor_scalar(mk_f[:, :], mk_f[:, :], 4.0, None, ALU.mult).then_inc(s["mk"], 1)
                pt_split(b, H - 2)
                pt_split(b, H - 1)
                ot_split(b, G - 1)
                dve.wait_ge(s["k2t_ps"], nth("k2t_ps", b, 1))
                kt = ps[:, 6, 0:G * CTX].rearrange("p (g c) -> p g c", g=G)
                for r in range(R):
                    last = V.tensor_scalar(k2_f[:, :, r * CTX:(r + 1) * CTX], kt, cols[:, BM + r:BM + r + 1], None, ALU.mult)
                last.then_inc(s["k2_f"], 1)
                dve.wait_ge(s["k2_hi"], nth("k2_hi", b, 1))
                minus(k2_lo[:, :, :], k2_f[:, :, :], k2_hi[:, :, :]).then_inc(s["k2_lo"], 1)
                dve.wait_ge(s["o_ps"], nth("o_ps", b, 1))
                dve.wait_ge(s["x_bo"], nth("x_bo", b, 1))
                V.tensor_tensor(x1[:, :, :], ps[:, 1, :].rearrange("p (t d) -> p t d", t=NT), x[:, :, :], ALU.add)\
                    .then_inc(s["x1"], 1)
                norm(b, 2, x1)
                xt(b, 2)
                for u in range(2):
                    dve.wait_ge(s["q2_hi"], nth("q2_hi", b, u + 1))
                    V.scalar_tensor_tensor(q2_a[:, 2 * u:2 * u + 2, :], q2_h[:, 2 * u:2 * u + 2, :].bitcast(f32),
                                           cols[:, NMASK:NMASK + 1], q2_f[:, 2 * u:2 * u + 2, :], ALU.mult, ALU.add)\
                        .then_inc(s["q2_a"], 1)
                dve.wait_ge(s["mk"], nth("mk", b, 2))
                for t in range(NT):
                    dve.wait_ge(s["s2_ps"], nth("s2_ps", b, t + 1))
                    for g in range(G):
                        last = V.tensor_tensor(s2[:, t, g * R * CTX:(g + 1) * R * CTX].rearrange("p (r c) -> p r c", r=R),
                                               ps[:, 4 * t + g, 0:R * CTX].rearrange("p (r c) -> p r c", r=R),
                                               mk_f[:, :].unsqueeze(1).broadcast_to([P, R, CTX]), ALU.add)
                    last.then_inc(s["s2_sb"], 1)
                    dve.wait_ge(s["s2_sb"], nth("s2_sb", b, t + 1))
                    V.tensor_reduce(mx2[:, t, :], s2[:, t, :].rearrange("p (h c) -> p h c", h=H), AX, ALU.max,
                                    negate=True).then_inc(s["mx2"], 1)
                    dve.wait_ge(s["mx2"], nth("mx2", b, t + 1))
                    v = s2[:, t, :].rearrange("p (h c) -> p h c", h=H)
                    V.tensor_tensor(v, v, mx2[:, t, :].unsqueeze(2).broadcast_to([P, H, CTX]), ALU.add)\
                        .then_inc(s["sh2"], 1)
                for t in range(NT):
                    dve.wait_ge(s["ex2"], nth("ex2", b, t + 1))
                    v = s2[:, t, :].rearrange("p (h c) -> p h c", h=H)
                    V.tensor_reduce(ls2[:, t, :], v, AX, ALU.add).then_inc(s["sm2"], 1)
                    dve.wait_ge(s["sm2"], nth("sm2", b, t + 1))
                    V.reciprocal(rl2[:, t, :], ls2[:, t, :]).then_inc(s["rl2"], 1)
                    dve.wait_ge(s["rl2"], nth("rl2", b, t + 1))
                    V.tensor_tensor(v, v, rl2[:, t, :].unsqueeze(2).broadcast_to([P, H, CTX]), ALU.mult)\
                        .then_inc(s["pn2"], 1)
                for g in range(G):
                    dve.wait_ge(s["pt2_hi"], nth("pt2_hi", b, g + 1))
                    minus(pt2_lo[:, :, :], ps[0:CTX, 2 * (g % 2):2 * (g % 2) + 2, :]
                          .rearrange("p k (r s) -> p (k r) s", r=2), pt2_hi[:, :, :]).then_inc(s["pt2_lo"], 1)
                    dve.wait_ge(s["ot2_hi"], nth("ot2_hi", b, g + 1))
                    minus(ot_lo[:, g, :], ps[:, 4 + g % 2, 0:S], ot_hi[:, g, :]).then_inc(s["ot2_lo"], 1)
                dve.wait_ge(s["o2_ps"], nth("o2_ps", b, 1))
                dve.wait_ge(s["x1_bo"], nth("x1_bo", b, 1))
                if later(b):
                    dve.wait_ge(s["out"], nth("out", b - 1, 16))
                V.tensor_tensor(x2[:, :, :], ps[:, 6, :].rearrange("p (t d) -> p t d", t=NT), x1[:, :, :], ALU.add)\
                    .then_inc(s["x2"], 1)
                norm(b, 3, x2)
                xt(b, 3)
                dve.wait_ge(s["xs_hi"], nth("xs_hi", b, 1))
                minus(xs_lo[:, :, :], xh[:, :, :], xs_hi[:, :, :]).then_inc(s["xs_lo"], 1)
                for t in range(NT):
                    dve.wait_ge(s["lg_sb"], nth("lg_sb", b, t + 1))
                    V.tensor_reduce(rm[:, t:t + 1], lg[:, t, :], AX, ALU.max, negate=True).then_inc(s["rm"], 1)
                for k in range(4):
                    dve.wait_ge(s["lt_ps"], nth("lt_ps", b, k + 1))
                    V.tensor_reduce(cm[:, 2 * k:2 * k + 2], ps[:, (6 + k) % 8, :].rearrange("p (e s) -> p e s", e=2),
                                    AX, ALU.max, negate=True).then_inc(s["cm"], 1)
                for k in range(4):
                    dve.wait_ge(s["ed"], nth("ed", b, k + 1))
                    V.reciprocal(crec[:, 2 * k:2 * k + 2], csum[:, 2 * k:2 * k + 2]).then_inc(s["rc"], 1)
                    dve.wait_ge(s["rc"], nth("rc", b, k + 1))
                    for e in (2 * k, 2 * k + 1):
                        last = V.tensor_scalar(edt[:, e, :], edt[:, e, :], crec[:, e:e + 1], None, ALU.mult)
                    last.then_inc(s["edn"], 1)
                dve.wait_ge(s["ec"], nth("ec", b, 2))
                V.reciprocal(rrec[:, :], rsum[:, :]).then_inc(s["rr"], 1)
                dve.wait_ge(s["rr"], nth("rr", b, 1))
                for k in range(4):
                    dve.wait_ge(s["cb_hi"], nth("cb_hi", b, k + 1))
                    minus(cb_lo[:, 2 * k:2 * k + 2, :], ps[:, 2 + k, :].rearrange("p (e s) -> p e s", e=2),
                          cb_hi[:, 2 * k:2 * k + 2, :]).then_inc(s["cb_lo"], 1)
                for t in range(NT):
                    for u in range(2):
                        dve.wait_ge(s["ds_hi"], nth("ds_hi", b, 2 * t + u + 1))
                        minus(ds_lo[:, t, u * 512:(u + 1) * 512], ps[:, (6 + 2 * t + u) % 8, :],
                              ds_hi[:, t, u * 512:(u + 1) * 512]).then_inc(s["ds_lo"], 1)
                for dk in range(ND):
                    for u in range(2):
                        dve.wait_ge(s["sl_hi"], nth("sl_hi", b, 2 * dk + u + 1))
                        minus(sl_lo[:, dk, u * 512:(u + 1) * 512], ps[:, 2 + 2 * dk + u, :],
                              sl_hi[:, dk, u * 512:(u + 1) * 512]).then_inc(s["sl_lo"], 1)

            dve.wait_ge(s["i_const"], 16)
            V.tensor_scalar(cols[:, BQ:BQ + G], cols[:, BQ:BQ + G], ATTN_SCALE, None, ALU.mult)
            V.tensor_scalar(cols[:, BQ2:BQ2 + G], cols[:, BQ2:BQ2 + G], XATTN_SCALE, None, ALU.mult)\
                .then_inc(s["i_cols"], 1)
            dve.wait_ge(s["i_bias"], 16)
            dve.wait_ge(s["i_se"], 16)
            V.tensor_tensor(se_sq[:, :, :], g_se[:, :, :], g_se[:, :, :], ALU.mult).then_inc(s["i_sq"], 1)
            dve.wait_ge(s["i_sq"], 1)
            V.tensor_reduce(se_ss[:, :], se_sq[:, :, :], AX, ALU.add).then_inc(s["i_st"], 1)
            dve.wait_ge(s["i_sr"], 4)
            for e in range(NS):
                last = V.tensor_scalar(g_se[:, e, :], g_se[:, e, :], se_sc[:, e:e + 1], None, ALU.mult)
            last.then_inc(s["i_xn"], 1)
            dve.wait_ge(s["i_gam"], 16)
            V.tensor_tensor(gxs[:, :], gam[:, 0, :], gam[:, 1, :], ALU.mult).then_inc(s["i_gxs"], 1)
            dve.wait_ge(s["i_w1"], 16)
            for dk in range(ND):
                last = V.tensor_scalar(stage["w1"][:, dk, :], stage["w1"][:, dk, :], gam[:, 0, dk:dk + 1], None, ALU.mult)
            last.then_inc(s["i_w1g"], 1)
            for n, name in enumerate(WEIGHTS):
                dve.wait_ge(s["i_hi"], n + 1)
                minus(W[name][1][:, :, :], stage[name][:, :, :], W[name][0][:, :, :]).then_inc(s["i_lo"], 1)
            dve.wait_ge(s["i_sps"], 1)
            dve.wait_ge(s["i_gxs"], 1)
            for dk in range(ND):
                V.tensor_scalar(se_t[:, dk, :], ps[:, 2 * dk:2 * dk + 2, :].rearrange("p u n -> p (u n)"),
                                gxs[:, dk:dk + 1], None, ALU.mult).then_inc(s["i_sg"], 1)
            dve.wait_ge(s["i_sg"], 2)
            dve.wait_ge(s["i_shi"], 1)
            minus(W["se"][1][:, :, :], se_t[:, :, :], W["se"][0][:, :, :]).then_inc(s["i_slo"], 1)
            stage_a(0)
            for c in range(NC):
                group(c, a=0)
            stage_b(0)
            with dve.Fori(0, B - 1) as b:
                stage_a(b + 1)
                for c in range(NC):
                    group(c, b, b + 1)
                stage_b(b + 1)
            for c in range(NC):
                group(c, b=B - 1)

        @block.gpsimd
        def _(pool):
            Q = nc.gpsimd

            def copy(o, i):
                return Q.tensor_scalar(o, i, 1.0, None, ALU.mult)

            def power(o, i, col):
                w = i.shape[1]
                return Q.tensor_tensor(o, i, cols[:, col:col + 1].broadcast_to([P, w]), ALU.pow)

            def rstd(b, n):
                name = f"ln{n}_rs"
                pool.wait_ge(s[f"ln{n}_mv"], nth(f"ln{n}_mv", b, 1))
                pool.sem_inc(s["pool_held"], 1)
                k = 0
                Q.tensor_scalar(rs[:, 0, :], mv[:, :, 1], LN_EPS, None, ALU.add).then_inc(s[name], 1)
                k += 1
                pool.wait_ge(s[name], nth(name, b, k))
                power(rs[:, 5 if n < 3 else 1, :], rs[:, 0, :], EXPO).then_inc(s[name], 1)
                if n < 3:
                    return
                power(rs[:, 2, :], mv[:, :, 1], EXPO + 1).then_inc(s[name], 1)
                k += 2
                pool.wait_ge(s[name], nth(name, b, k))
                Q.tensor_tensor(rs[:, 3, :], rs[:, 1, :], rs[:, 2, :], ALU.mult).then_inc(s[name], 1)
                k += 1
                pool.wait_ge(s[name], nth(name, b, k))
                pool.sem_inc(s["pool_held"], 1)
                Q.tensor_scalar(rs[:, 3, :], rs[:, 3, :], float(D) ** 0.5, RMS_EPS, ALU.mult, ALU.max).then_inc(s[name], 1)
                k += 1
                pool.wait_ge(s[name], nth(name, b, k))
                power(rs[:, 4, :], rs[:, 3, :], EXPO + 2).then_inc(s[name], 1)
                k += 1
                pool.wait_ge(s[name], nth(name, b, k))
                Q.tensor_tensor(rs[:, 0, :], rs[:, 4, :], rs[:, 1, :], ALU.mult).then_inc(s[name], 1)
                k += 1
                pool.wait_ge(s[name], nth(name, b, k))
                pool.sem_inc(s["pool_held"], 1)
                Q.tensor_scalar(rs[:, 5, :], rs[:, 0, :], float(D) ** 0.5, None, ALU.mult).then_inc(s[name], 1)

            def bias(o, bcol, b, ln, signal):
                pool.wait_ge(s[ln], nth(ln, b, 1))
                Q.tensor_tensor(o, o, bcol[:, :].unsqueeze(1).broadcast_to([P, NT, D]), ALU.add).then_inc(s[signal], 1)

            def qk_hi(b, g):
                pool.wait_ge(s["qk_sb"], nth("qk_sb", b, g + 1))
                pool.sem_inc(s["pool_held"], 1)
                copy(qk_h[:, :, :], qk_f[:, :, :]).then_inc(s["qk_hi"], 1)

            def place_v(b, g):
                pool.wait_ge(s["v_sb"], nth("v_sb", b, 1))
                if g:
                    pool.wait_ge(s["pv"], nth("pv", b, 4 * g))
                elif later(b):
                    pool.wait_ge(s["pv2"], nth("pv2", b - 1, G))
                    pool.sem_inc(s["pool_held"], 1)
                pool.sem_inc(s["pool_held"], 1)
                src = v_f[:, :, g * R * HD:(g + 1) * R * HD].rearrange("p t (r d) -> p t r d", r=R)
                copy(vg[:, :, :, 0:HD], src).then_inc(s["vg_hi"], 1)
                pool.wait_ge(s["vg_hi"], nth("vg_hi", b, g + 1))
                Q.tensor_tensor(vg[:, :, :, HD:2 * HD], src, vg[:, :, :, 0:HD].bitcast(f32), ALU.subtract)\
                    .then_inc(s["vg_lo"], 1)

            def h_hi_part(b, c, q):
                n = 4 * c + q
                pool.wait_ge(s["ge"], nth("ge", b, n + 1))
                pool.sem_inc(s["pool_held"], 1)
                copy(h_hi[:, 2 * q:2 * q + 2, :], h_f[:, 2 * q:2 * q + 2, :]).then_inc(s["h_hi"], 1)

            def normed(b, h):
                pool.wait_ge(s["rl"], nth("rl", b, h + 1))
                pool.sem_inc(s["pool_held"], 1)
                for t in range(NT):
                    last = Q.tensor_scalar(p_sb[:, h % 2, t, :], p_sb[:, h % 2, t, :], rl[:, h, t:t + 1], None, ALU.mult)
                last.then_inc(s["pn"], 1)

            def group(c, b=None, a=None):
                h = 4 * c
                if a is not None:
                    qk_hi(a, c)
                if b is not None:
                    for q in range(4):
                        h_hi_part(b, c, q)
                if a is not None:
                    place_v(a, c)
                    for i in range(R):
                        normed(a, h + i)

            def stage_a(a):
                rstd(a, 1)
                bias(x[:, :, :], bo, a, "ln1_xh", "x_bo")

            def stage_b(b):
                rstd(b, 2)
                bias(x1[:, :, :], bo2, b, "ln2_xh", "x1_bo")
                for u in range(2):
                    pool.wait_ge(s["q2_sb"], nth("q2_sb", b, u + 1))
                    pool.sem_inc(s["pool_held"], 1)
                    copy(q2_h[:, 2 * u:2 * u + 2, :], q2_f[:, 2 * u:2 * u + 2, :]).then_inc(s["q2_hi"], 1)
                pool.wait_ge(s["v2_sb"], nth("v2_sb", b, 1))
                pool.wait_ge(s["pv"], nth("pv", b, H))
                for g in range(G):
                    if g >= 2:
                        pool.wait_ge(s["pv2"], nth("pv2", b, g - 1))
                    pool.sem_inc(s["pool_held"], 1)
                    src = v2_f[:, g * R * HD:(g + 1) * R * HD].rearrange("p (r d) -> p r d", r=R)
                    copy(vg[0:CTX, g % 2, :, 0:HD], src).then_inc(s["vg2_hi"], 1)
                    pool.wait_ge(s["vg2_hi"], nth("vg2_hi", b, g + 1))
                    Q.tensor_tensor(vg[0:CTX, g % 2, :, HD:2 * HD], src, vg[0:CTX, g % 2, :, 0:HD].bitcast(f32),
                                    ALU.subtract).then_inc(s["vg2_lo"], 1)
                rstd(b, 3)
                pool.wait_ge(s["ln3_xh"], nth("ln3_xh", b, 1))
                pool.sem_inc(s["pool_held"], 1)
                copy(xs_hi[:, :, :], xh[:, :, :]).then_inc(s["xs_hi"], 1)

            def context(b):
                pool.wait_ge(s["ctx_in"], nth("ctx_in", b, 16))
                if later(b):
                    pool.wait_ge(s["kv_ps"], nth("kv_ps", b - 1, 1))
                    pool.sem_inc(s["pool_held"], 1)
                copy(cx_hi[:, :, :], cx[:, :, :]).then_inc(s["ct_hi"], 1)
                pool.wait_ge(s["ct_hi"], nth("ct_hi", b, 1))
                Q.tensor_tensor(cx_lo[:, :, :], cx[:, :, :], cx_hi[:, :, :].bitcast(f32), ALU.subtract)\
                    .then_inc(s["ct_lo"], 1)

            Q.memset(vg[:, :, :, :].bitcast(f32), 0.0).then_inc(s["i_vz"], 1)
            pool.wait_ge(s["i_vz"], 1)
            pool.wait_ge(s["i_const"], 16)
            pool.wait_ge(s["i_st"], 1)
            power(se_n[:, :], se_ss[:, :], EXPO + 1).then_inc(s["i_sr"], 1)
            pool.wait_ge(s["i_sr"], 1)
            pool.sem_inc(s["pool_held"], 1)
            Q.tensor_scalar(se_n[:, :], se_n[:, :], RMS_EPS, None, ALU.max).then_inc(s["i_sr"], 1)
            pool.wait_ge(s["i_sr"], 2)
            power(se_i[:, :], se_n[:, :], EXPO + 2).then_inc(s["i_sr"], 1)
            pool.wait_ge(s["i_sr"], 3)
            pool.sem_inc(s["pool_held"], 1)
            Q.tensor_scalar(se_sc[:, :], se_i[:, :], float(D) ** 0.5, None, ALU.mult).then_inc(s["i_sr"], 1)
            pool.wait_ge(s["i_bias"], 16)
            stage_a(0)
            context(0)
            for c in range(NC):
                group(c, a=0)
            stage_b(0)
            with pool.Fori(0, B - 1) as b:
                stage_a(b + 1)
                context(b + 1)
                for c in range(NC):
                    group(c, b, b + 1)
                stage_b(b + 1)
            for c in range(NC):
                group(c, b=B - 1)

        @block.sync
        def _(sp):
            def tokens(t, b):
                return t[bass.ds(b, 1), :, :].rearrange("o (t p) d -> p (o t) d", p=P)

            def load_x(b):
                if later(b):
                    sp.wait_ge(s["x1"], nth("x1", b - 1, 1))
                sp.dma_start(x[:, :, :], tokens(t_in["x"], b)).then_inc(s["x_in"], 16)

            def load_ctx(b):
                if later(b):
                    sp.wait_ge(s["ct_lo"], nth("ct_lo", b - 1, 1))
                    sp.wait_ge(s["mk"], nth("mk", b - 1, 2))
                sp.dma_start(cx[:, :, :], t_in["ctxT"][bass.ds(b, 1), :, :].rearrange("o (k p) c -> p (o k) c", p=P))\
                    .then_inc(s["ctx_in"], 16)
                sp.dma_start(mk_i[:, :], t_in["mask"][bass.ds(b, 1), :].broadcast_to([P, CTX])).then_inc(s["mask_in"], 16)

            def store(b):
                sp.wait_ge(s["y"], nth("y", b, NC))
                sp.dma_start(tokens(out, b), x2[:, :, :]).then_inc(s["out"], 16)

            sp.dma_start(consts[:, :], t_in["consts"]).then_inc(s["i_const"], 16)
            load_x(0)
            for name in WEIGHTS[:2]:
                sp.dma_start(stage[name][:, :, :], t_in[name]).then_inc(s["i_" + name], 16)
            sp.dma_start(g_se[:, :, :], t_in["se"].rearrange("(e p) d -> p e d", p=P)).then_inc(s["i_se"], 16)
            sp.dma_start(gam[:, :, :], t_in["gam"]).then_inc(s["i_gam"], 16)
            sp.dma_start(biases[:, :], t_in["bias"].broadcast_to([P, 5 * D])).then_inc(s["i_bias"], 16)
            load_ctx(0)
            for name in WEIGHTS[2:]:
                sp.dma_start(stage[name][:, :, :], t_in[name]).then_inc(s["i_" + name], 16)
            with sp.Fori(0, B - 1) as b:
                load_x(b + 1)
                load_ctx(b + 1)
                store(b)
            store(B - 1)
            sp.wait_ge(s["out"], 16 * B)


def kernel(**inputs):
    import numpy as _np
    import concourse.bacc as _bacc
    from concourse import mybir as _mybir
    from concourse.bass_utils import run_bass_kernel_spmd as _run

    a = {n: _np.asarray(v) for n, v in inputs.items()}
    sa, xa, ff = "L0_attn_", "L0_xattn_", "L0_ffn_"

    def twice(w, axis):
        shape = w.shape[:axis] + (H, HD) + w.shape[axis + 1:]
        w = w.reshape(shape)
        return _np.concatenate([w, w], axis=axis + 1).reshape(w.shape[:axis] + (2 * H * HD,) + w.shape[axis + 2:])

    def on_partitions(w):
        return w.reshape(-1, P, w.shape[-1]).transpose(1, 0, 2)

    def by_group(v):
        return twice(v, 0).reshape(G, P).T

    rows = _np.arange(P)
    consts = _np.zeros((P, P + NCOLS), _np.float32)
    consts[:, :P] = _np.eye(P, dtype=_np.float32)
    for r in range(R):
        consts[32 * r:32 * r + 32, P + BM + r] = 1.0
    consts[rows % 32 >= HD, P + NMASK] = -1.0
    consts[:, P + EXPO:P + EXPO + 3] = _np.array([-0.5, 0.5, -1.0], _np.float32)
    consts[:, P + BQ:P + BQ + G] = by_group(a[sa + "bq"])
    consts[:, P + BK:P + BK + G] = by_group(a[sa + "bk"])
    consts[:, P + BQ2:P + BQ2 + G] = by_group(a[xa + "bq"])
    host = {
        "x": a["x"],
        "ctxT": a["ctx_1024"].transpose(0, 2, 1),
        "mask": a["mask_Bx1x1xS2_if1"].reshape(B, CTX),
        "consts": consts,
        "bias": _np.concatenate([a[sa + "bv"], a[sa + "bo"], a[xa + "bk"], a[xa + "bv"], a[xa + "bo"]])[None, :],
        "gam": _np.stack([a[ff + "gamma_x"], a[ff + "gamma_slot"]]).reshape(2, ND, P).transpose(2, 0, 1),
        "se": a[ff + "slot_embeds"].reshape(SLOTS, D),
        "wqk": on_partitions(_np.concatenate([twice(a[sa + "Wq"].T, 1), twice(a[sa + "Wk"].T, 1)], axis=1)),
        "wv": on_partitions(a[sa + "Wv"].T),
        "wo": on_partitions(twice(a[sa + "Wo"].T, 0)),
        "wkv2": on_partitions(_np.concatenate([a[xa + "Wk"].T, a[xa + "Wv"].T], axis=1)),
        "wq2": on_partitions(twice(a[xa + "Wq"].T, 1)),
        "wo2": on_partitions(twice(a[xa + "Wo"].T, 0)),
        "w1": on_partitions(a[ff + "w1"]),
        "w2": on_partitions(a[ff + "w2"]),
    }
    nc = _bacc.Bacc("TRN2", target_bir_lowering=False, num_devices=1)
    arrays, t_in = {}, {}
    for name, v in host.items():
        v = _np.ascontiguousarray(v)
        arrays["in_" + name] = v
        t_in[name] = nc.dram_tensor("in_" + name, v.shape, _mybir.dt.from_np(v.dtype), kind="ExternalInput").ap()
    out = nc.dram_tensor("out_0", (B, S, D), _mybir.dt.float32, kind="ExternalOutput").ap()
    decoder_layer(nc, t_in, out)
    r = _run(nc, [arrays], core_ids=[0])
    return r.results[0]["out_0"]
```

```python
import concourse.bass as bass
from concourse import mybir
from concourse.alu_op_type import AluOpType as ALU
from contextlib import ExitStack
import numpy as np

B, S, D = 16, 256, 256
H, HD = 16, 16
CTX = 77
E, TS, HID = 8, 128, 1024
SLOTS = E * TS
P = 128
NT = S // P
ND = D // P
G, R = 4, 4
PADW = 160
CHUNK = 256
NC = SLOTS // CHUNK
NM = HID // P
NS = SLOTS // P
LN_EPS, RMS_EPS = 1e-5, 1e-12
BM, NMASK, EXPO, BQ, BK, BQ2, NCOLS = 0, 4, 5, 10, 14, 18, 22
ATTN_SCALE, XATTN_SCALE = 1.0 / 16.0, 1.0 / 4.0

PER = dict(
    x_in=16, ctx_in=16, mask_in=16, out=16,
    ln1_st=1, ln1_mv=1, ln1_ve=1, ln1_pw=1, ln1_xh=1, xt1_ps=1, xt1_hi=1, xt1_lo=1,
    ln2_st=1, ln2_mv=1, ln2_ve=1, ln2_pw=1, ln2_xh=1, xt2_ps=1, xt2_hi=1, xt2_lo=1,
    ln3_st=1, ln3_mv=1, ln3_ve=1, ln3_pw=1, ln3_sc=4, ln3_xh=1, xt3_ps=1, xt3_hi=1, xt3_lo=1,
    x_bo=1, v_ps=1, v_sb=1, vg_hi=4, vg_lo=4, qk_ps=4, qk_sb=4, qk_hi=4, qk_lo=4,
    s_ps=16, mx=16, ex=16, rl=16, pn=16, t_ps=16, pt_hi=16, pt_lo=16, pv=16, ot_hi=4, ot_lo=4,
    o_ps=1, x1=1, x1_bo=1, ct_hi=1, ct_lo=1, kv_ps=1, kd_sb=1, v2_sb=1, k2t_ps=1, k2_n=1, mk=2,
    k2_f=4, k2_hi=4, k2_lo=4, vg2_hi=4, vg2_lo=4, q2_ps=4, q2_sb=4, q2_hi=4, q2_a=4,
    s2_ps=4, s2_sb=4, mx2=4, sh2=4, ex2=4, sm2=4, rl2=4, pn2=4,
    t2_ps=8, pt2_hi=8, pt2_lo=8, pv2=8, ot2_hi=4, ot2_lo=4,
    o2_ps=1, x2=1, xs_hi=1, xs_lo=1, lg_ps=4, lg_sb=4,
    res=1, rm=2, lt_ps=4, cm=4, ed=4, rc=4, edn=4, ds_ps=4, ds_hi=4, ds_lo=4, sl_ps=4, sl_hi=4, sl_lo=4,
    ec=4, cb_ps=4, cb_hi=4, cb_lo=4, h_ps=16, ge=16, h_hi=16, h_lo=16, pr_ps=4, pr_hi=4, pr_lo=4,
    d_ps=4, acc=4, rs_sum=1, rr=1, y=1,
)

WEIGHTS = ("wqk", "wv", "wo", "wkv2", "wq2", "wo2", "w1", "w2")



def c(name, *k):
    return ("c", name, k)


def m(name, *k):
    return ("m", name, k)


def heads(g):
    h = R * g
    return [
        [c("scores", h), c("scores", h + 1)],
        [c("normed", h), c("transp", h), c("normed", h + 1), c("transp", h + 1)],
        [c("scores", h + 2), c("scores", h + 3)],
        [c("pv", h), c("pv", h + 1)],
        [c("normed", h + 2), c("transp", h + 2), c("normed", h + 3), c("transp", h + 3)],
        [c("pv", h + 2), c("pv", h + 3), c("ot", g)],
    ]


def pair_chunk(k, ga, gb):
    a, b = heads(ga), heads(gb)
    return ([c("qk", ga), m("hidden", k, 0), m("hidden", k, 1), m("hidden", k, 2), m("hidden", k, 3)]
            + a[0] + [m("lt", k + 1), m("edt", k + 1)] + a[1] + a[2] + [m("outer", k, 0)] + a[3] + a[4]
            + [m("ec", k), m("dispatch", k + 1)] + a[5] + [c("qk", gb), m("outer", k, 1)]
            + b[0] + [m("slots", k + 1)] + b[1] + b[2] + [m("comb", k)] + b[3] + b[4] + [m("combine", k)] + b[5])


WEAVE = (
    [m("begin"), c("norm", 1), m("lt", 0), m("edt", 0), c("xt", 1), c("v"), c("context"), m("dispatch", 0), m("slots", 0)]
    + pair_chunk(0, 0, 1)
    + pair_chunk(1, 2, 3)
    + [c("kv"), m("hidden", 2, 0), m("hidden", 2, 1), c("k2t"), c("k2", 0), c("v2", 0), m("hidden", 2, 2), m("hidden", 2, 3),
       c("oproj"), c("norm", 2), m("lt", 3), m("edt", 3), m("outer", 2, 0), c("xt", 2), m("ec", 2), m("dispatch", 3),
       m("outer", 2, 1), c("q2", 0), m("slots", 3), m("comb", 2), c("s2", 0), c("k2", 1), c("v2", 1), m("combine", 2),
       c("q2", 1), c("n2", 0), c("s2", 1), c("k2", 2),
       m("hidden", 3, 0), m("hidden", 3, 1), c("t2", 0, 0), m("hidden", 3, 2), c("t2", 0, 1), m("hidden", 3, 3),
       c("n2", 1), c("q2", 2), c("pv2", 0, 0), c("s2", 2), c("k2", 3), m("ec", 3), m("outer", 3, 0), c("t2", 1, 0),
       c("pv2", 0, 1), c("t2", 1, 1), c("v2", 2), c("q2", 3), c("n2", 2), c("pv2", 1, 0), c("s2", 3), m("comb", 3),
       c("pv2", 1, 1), c("t2", 2, 0), m("outer", 3, 1), c("t2", 2, 1), c("v2", 3), c("n2", 3), c("pv2", 2, 0),
       c("pv2", 2, 1), c("t2", 3, 0), c("t2", 3, 1), m("combine", 3), c("pv2", 3, 0), c("pv2", 3, 1), c("oproj2"),
       m("finish"), c("norm", 3), c("xt", 3), c("xs"), c("logits", 0), c("logits", 1), c("logits", 2), c("logits", 3)]
)


def run(steps, a=None, b=None):
    for kind, name, k in WEAVE:
        batch = a if kind == "c" else b
        if batch is not None and name in steps:
            steps[name](batch, *k)


def decoder_layer(nc, t_in, out):
    f32, f32r, i32 = mybir.dt.float32, mybir.dt.float32r, mybir.dt.int32
    ACT = mybir.ActivationFunctionType
    AX = mybir.AxisListType.X
    KB = 1024

    ctx = ExitStack()
    with ctx:
        base = [nc.sbuf_base + (-nc.sbuf_base) % 64]
        end = nc.sbuf_usable_end

        def region(nbytes):
            at = base[0]
            base[0] = at + nbytes + (-nbytes) % 32
            assert base[0] <= end, (base[0], end)
            return at

        def at(name, shape, dt, offset):
            return nc.alloc_sbuf_tensor_at(name, shape, dt, offset=offset)

        def sb(name, shape, dt=f32):
            return at(name, shape, dt, region(4 * int(np.prod(shape[1:]))))

        def pair(name, shape):
            return sb(name + "_hi", shape, f32r), sb(name + "_lo", shape, f32r)

        W = dict(
            wqk=pair("wqk", [P, ND, 2 * 512]), wv=pair("wv", [P, ND, D]), wo=pair("wo", [P, G, D]),
            wkv2=pair("wkv2", [P, ND, 2 * D]), wq2=pair("wq2", [P, ND, 512]), wo2=pair("wo2", [P, G, D]),
            w1=pair("w1", [P, ND, HID]), w2=pair("w2", [P, NM, D]), se=pair("se", [P, ND, SLOTS]),
        )
        r_lg = region(8 * KB)
        lg = at("lg", [P, NT, SLOTS], f32, r_lg)
        r_exp = region(4 * KB)
        edt = at("edt", [P, 2, S], f32, r_exp)
        ecomb = at("ecomb", [P, NT, CHUNK], f32, r_exp + 2 * KB)
        xs_hi, xs_lo = pair("xs", [P, NT, D])
        r_dc = region(4 * KB)
        ds_hi = at("ds_hi", [P, NT, CHUNK], f32r, r_dc)
        ds_lo = at("ds_lo", [P, NT, CHUNK], f32r, r_dc + 2 * KB)
        cb_hi = at("cb_hi", [P, 2, S], f32r, r_dc)
        cb_lo = at("cb_lo", [P, 2, S], f32r, r_dc + 2 * KB)
        sl_hi, sl_lo = pair("sl", [P, ND, CHUNK])
        r_hid = region(16 * KB)
        h_hi = at("h_hi", [P, NM, CHUNK], f32r, r_hid)
        h_lo = at("h_lo", [P, NM, CHUNK], f32r, r_hid + 8 * KB)
        h_f = at("h_f", [P, NM, CHUNK], f32, r_hid + 8 * KB)
        pr_hi, pr_lo = pair("pr", [P, 2, D])
        r_acc = region(2 * KB)
        acc = at("acc", [P, NT, D], f32, r_acc)
        res = sb("res", [P, NT, D])
        x = sb("x", [P, NT, D])
        x2 = sb("x2", [P, NT, D])
        xt_hi, xt_lo = pair("xt", [P, ND, S])
        r_qk = region(2 * KB)
        qk_f = at("qk_f", [P, 2, S], f32, r_qk)
        qk_l = at("qk_l", [P, 2, S], f32r, r_qk)
        qk_h = sb("qk_h", [P, 2, S], f32r)
        q2_f = at("q2_f", [P, 2, S], f32, r_qk)
        q2_a = at("q2_a", [P, 2, S], f32r, r_qk)
        r_v = region(2 * KB)
        v_f = at("v_f", [P, NT, D], f32, r_v)
        k2d = at("k2d", [CTX, H, 2, HD], f32, r_v)
        vg = sb("vg", [P, NT, R, PADW], f32r)
        r_p = region(4 * KB)
        p_sb = at("p_sb", [P, 2, NT, S], f32, r_p)
        x1 = at("x1", [P, NT, D], f32, r_p)
        xh = at("xh", [P, NT, D], f32, r_p + 2 * KB)
        r_pt = region(8 * KB)
        pt_hi = at("pt_hi", [P, 2, NT, S], f32r, r_pt)
        pt_lo = at("pt_lo", [P, 2, NT, S], f32r, r_pt + 4 * KB)
        pt2_hi = at("pt2_hi", [CTX, 2, 2, S], f32r, r_pt)
        pt2_lo = at("pt2_lo", [CTX, 2, 2, S], f32r, r_pt + 4 * KB)
        r_ot = region(8 * KB)
        ot_hi = at("ot_hi", [P, G, S], f32r, r_ot)
        ot_lo = at("ot_lo", [P, G, S], f32r, r_ot + 4 * KB)
        s2 = sb("s2", [P, 2, NT, R * CTX])
        v2_f = sb("v2_f", [CTX, D])
        k2_n = sb("k2_n", [P, G, CTX])
        r_k2 = region(4 * R * CTX)
        k2_f = at("k2_f", [P, R, CTX], f32, r_k2)
        k2_lo = at("k2_lo", [P, R * CTX], f32r, r_k2)
        k2_hi = sb("k2_hi", [P, R * CTX], f32r)
        r_cx = region(4 * ND * CTX)
        cx = at("cx", [P, ND, CTX], f32, r_cx)
        cx_lo = at("cx_lo", [P, ND, CTX], f32r, r_cx)
        cx_hi = sb("cx_hi", [P, ND, CTX], f32r)
        mk_i = sb("mk_i", [P, CTX], i32)
        mk_f = sb("mk_f", [P, CTX])
        consts = sb("consts", [P, P + NCOLS])
        ident = consts[:, 0:P]
        cols = consts[:, P:P + NCOLS]
        biases = sb("biases", [P, 5 * D])
        bv, bo, bo2 = (biases[:, i * D:(i + 1) * D] for i in (0, 1, 4))
        bkv2 = biases[0:CTX, 2 * D:4 * D]
        st = sb("st", [P, NT, 6])
        mv = sb("mv", [P, NT, 2])
        ve = sb("ve", [P, 2, NT])
        pw = sb("pw", [P, 2, NT])
        sc3 = sb("sc3", [P, 4, NT])
        mx = sb("mx", [P, H, NT])
        ls = sb("ls", [P, H, NT])
        rl = sb("rl", [P, H, NT])
        mx2 = sb("mx2", [P, G, NT, R])
        ls2 = sb("ls2", [P, G, NT, R])
        rl2 = sb("rl2", [P, G, NT, R])
        rm = sb("rm", [P, NT])
        rsum = sb("rsum", [P, NT, NC])
        rtot = sb("rtot", [P, NT])
        rrec = sb("rrec", [P, NT])
        cm = sb("cm", [P, NS])
        csum = sb("csum", [P, NS])
        crec = sb("crec", [P, NS])
        gam = sb("gam", [P, 2, ND])
        gxs = sb("gxs", [P, ND])
        stage = dict(
            wqk=at("g_wqk", [P, ND, 1024], f32, r_lg), w1=at("g_w1", [P, ND, HID], f32, r_hid),
            w2=at("g_w2", [P, NM, D], f32, r_hid + 8 * KB), wo2=at("g_wo2", [P, G, D], f32, r_ot),
            wq2=at("g_wq2", [P, ND, 512], f32, r_ot + 4 * KB), wv=at("g_wv", [P, ND, D], f32, r_exp),
            wo=at("g_wo", [P, G, D], f32, r_dc), wkv2=at("g_wkv2", [P, ND, 512], f32, r_p),
        )
        g_se = at("g_se", [P, NS, D], f32, r_acc)
        se_t = at("se_t", [P, ND, SLOTS], f32, r_pt)
        se_sq = at("se_sq", [P, NS, D], f32, r_pt)
        se_ss, se_n, se_i, se_sc = (sb(n, [P, NS]) for n in ("se_ss", "se_n", "se_i", "se_sc"))
        ps = ctx.enter_context(nc.psum_tensor("ps", [P, 8, 512], f32))

        s = {n: ctx.enter_context(nc.semaphore("s_" + n)) for n in PER}
        for n in ("i_const", "i_bias", "pool_held", "dve_held", "i_cols", "i_vz", "i_se", "i_gam", "i_gxs", "i_hi",
                  "i_lo", "i_w1g", "i_st", "i_sq", "i_sr", "i_xn", "i_sps", "i_sg", "i_shi", "i_slo"):
            s[n] = ctx.enter_context(nc.semaphore("s_" + n))
        for n in WEIGHTS:
            s["i_" + n] = ctx.enter_context(nc.semaphore("s_i_" + n))

        def nth(name, b, k):
            return b * PER[name] + k

        def later(b):
            return not isinstance(b, int) or b > 0

        block = ctx.enter_context(nc.Block())

        @block.tensor
        def _(pe):
            te = nc.tensor
            full = slice(None)
            XT, OT, SL, CB, DS = (xt_hi, xt_lo), (ot_hi, ot_lo), (sl_hi, sl_lo), (cb_hi, cb_lo), (ds_hi, ds_lo)
            HH, PR, XS, CX = (h_hi, h_lo), (pr_hi, pr_lo), (xs_hi, xs_lo), (cx_hi, cx_lo)

            def three(o, lhs, rhs, first, last):
                te.matmul(o, lhs[0], rhs[0], start=first, stop=False)
                te.matmul(o, lhs[1], rhs[0], start=False, stop=False)
                return te.matmul(o, lhs[0], rhs[1], start=False, stop=last)

            def both(t, *ix):
                return tuple(u.__getitem__(ix) for u in t)

            def xt(a, n):
                pe.wait_ge(s[f"ln{n}_xh"], nth(f"ln{n}_xh", a, 1))
                bank = 0 if n == 1 else 1
                if n == 2:
                    pe.wait_ge(s["v2_sb"], nth("v2_sb", a, 1))
                for dk in range(ND):
                    for t in range(NT):
                        last = te.transpose(ps[:, bank, dk * S + t * P:dk * S + (t + 1) * P],
                                            xh[:, t, dk * P:(dk + 1) * P], ident[:, :])
                last.then_inc(s[f"xt{n}_ps"], 1)

            def v(a):
                pe.wait_ge(s["xt1_lo"], nth("xt1_lo", a, 1))
                for t in range(NT):
                    for dk in range(ND):
                        last = three(ps[:, 1, t * D:(t + 1) * D], both(XT, full, dk, slice(t * P, t * P + P)),
                                     both(W["wv"], full, dk), dk == 0, dk == ND - 1)
                last.then_inc(s["v_ps"], 1)

            def qk(a, g):
                if g:
                    pe.wait_ge(s["ot_lo"], nth("ot_lo", a, g))
                else:
                    pe.wait_ge(s["xt1_lo"], nth("xt1_lo", a, 1))
                for i in range(2):
                    for dk in range(ND):
                        c0 = i * 512 + g * P
                        last = three(ps[:, 0, i * S:(i + 1) * S], both(W["wqk"], full, dk, slice(c0, c0 + P)),
                                     both(XT, full, dk), dk == 0, dk == ND - 1)
                last.then_inc(s["qk_ps"], 1)

            def scores(a, h):
                g, r = divmod(h, R)
                rows = slice(32 * r, 32 * r + 32)
                pe.wait_ge(s["qk_lo"], nth("qk_lo", a, g + 1))
                if h >= 2:
                    pe.wait_ge(s["ex"], nth("ex", a, h - 1))
                if h == 0:
                    pe.wait_ge(s["v_sb"], nth("v_sb", a, 1))
                for t in range(NT):
                    for k, keys in enumerate((qk_h, qk_l)):
                        last = te.matmul(ps[:, 1 + h % 2, t * S:(t + 1) * S], qk_l[rows, 0, t * P:(t + 1) * P],
                                         keys[rows, 1, :], start=k == 0, stop=k == 1)
                last.then_inc(s["s_ps"], 1)

            def transp(a, h):
                pe.wait_ge(s["pn"], nth("pn", a, h + 1))
                if h >= 2:
                    pe.wait_ge(s["pt_lo"], nth("pt_lo", a, h - 1))
                for j in range(NT):
                    for t in range(NT):
                        last = te.transpose(ps[:, 3 + h % 2, j * S + t * P:j * S + (t + 1) * P],
                                            p_sb[:, h % 2, t, j * P:(j + 1) * P], ident[:, :])
                last.then_inc(s["t_ps"], 1)

            def pv(a, h):
                g, r = divmod(h, R)
                pe.wait_ge(s["pt_lo"], nth("pt_lo", a, h + 1))
                if r == 0:
                    pe.wait_ge(s["vg_lo"], nth("vg_lo", a, g + 1))
                    pe.wait_ge(s["qk_sb"], nth("qk_sb", a, g + 1))
                for j in range(NT):
                    w = vg[:, j, :, :].rearrange("p r w -> p (r w)")[:, r * P:(r + 1) * P]
                    for k, pt in enumerate((pt_hi, pt_lo)):
                        last = te.matmul(ps[:, 0, 0:S], w, pt[:, h % 2, j, :], start=r == 0 and j == 0 and k == 0,
                                         stop=r == R - 1 and j == NT - 1 and k == 1)
                last.then_inc(s["pv"], 1)

            def project(a, w, signal):
                for t in range(NT):
                    for g in range(G):
                        last = three(ps[:, 0, t * D:(t + 1) * D], both(OT, full, g, slice(t * P, t * P + P)),
                                     both(W[w], full, g), g == 0, g == G - 1)
                last.then_inc(s[signal], 1)

            def oproj(a):
                pe.wait_ge(s["ot_lo"], nth("ot_lo", a, G))
                project(a, "wo", "o_ps")

            def kv(a):
                pe.wait_ge(s["ct_lo"], nth("ct_lo", a, 1))
                pe.wait_ge(s["ex"], nth("ex", a, H - 1))
                for dk in range(ND):
                    last = three(ps[0:CTX, 1, :], both(CX, full, dk), both(W["wkv2"], full, dk), dk == 0, dk == ND - 1)
                last.then_inc(s["kv_ps"], 1)

            def k2t(a):
                pe.wait_ge(s["kd_sb"], nth("kd_sb", a, 1))
                pe.wait_ge(s["ex"], nth("ex", a, H))
                for g in range(G):
                    kd = k2d[:, :, :, :].rearrange("p h e d -> p (h e d)")[:, g * P:(g + 1) * P]
                    last = te.transpose(ps[:, 2, g * CTX:(g + 1) * CTX], kd, ident[0:CTX, 0:CTX])
                last.then_inc(s["k2t_ps"], 1)

            def q2(a, g):
                if g:
                    pe.wait_ge(s["s2_sb"], nth("s2_sb", a, g))
                else:
                    pe.wait_ge(s["xt2_lo"], nth("xt2_lo", a, 1))
                    pe.wait_ge(s["x1"], nth("x1", a, 1))
                for dk in range(ND):
                    last = three(ps[:, 0, 0:S], both(W["wq2"], full, dk, slice(g * P, g * P + P)), both(XT, full, dk),
                                 dk == 0, dk == ND - 1)
                last.then_inc(s["q2_ps"], 1)

            def s2_step(a, g):
                pe.wait_ge(s["q2_a"], nth("q2_a", a, g + 1))
                pe.wait_ge(s["k2_lo"], nth("k2_lo", a, g + 1))
                if g:
                    pe.wait_ge(s["s2_sb"], nth("s2_sb", a, g))
                for t in range(NT):
                    for k, keys in enumerate((k2_hi, k2_lo)):
                        last = te.matmul(ps[:, t, 0:R * CTX], q2_a[:, g % 2, t * P:(t + 1) * P], keys[:, :],
                                         start=k == 0, stop=k == 1)
                last.then_inc(s["s2_ps"], 1)

            def t2(a, g, u):
                n = 2 * g + u
                pe.wait_ge(s["pn2"], nth("pn2", a, g + 1))
                if n >= 2:
                    pe.wait_ge(s["pt2_lo"], nth("pt2_lo", a, n - 1))
                else:
                    pe.wait_ge(s["pt_lo"], nth("pt_lo", a, H))
                for i in range(2):
                    for t in range(NT):
                        r = 2 * u + i
                        last = te.transpose(ps[0:CTX, 3 + u, i * S + t * P:i * S + (t + 1) * P],
                                            s2[:, g % 2, t, r * CTX:(r + 1) * CTX], ident[:, :])
                last.then_inc(s["t2_ps"], 1)

            def pv2(a, g, u):
                n = 2 * g + u
                pe.wait_ge(s["pt2_lo"], nth("pt2_lo", a, n + 1))
                if u == 0:
                    pe.wait_ge(s["vg2_lo"], nth("vg2_lo", a, g + 1))
                    if g:
                        pe.wait_ge(s["ot2_lo"], nth("ot2_lo", a, g))
                    else:
                        pe.wait_ge(s["k2_n"], nth("k2_n", a, 1))
                for i in range(2):
                    r = 2 * u + i
                    w = vg[0:CTX, g % 2, :, :].rearrange("p r w -> p (r w)")[:, r * P:(r + 1) * P]
                    for k, pt in enumerate((pt2_hi, pt2_lo)):
                        last = te.matmul(ps[:, 2, 0:S], w, pt[:, u, i, :], start=r == 0 and k == 0,
                                         stop=r == R - 1 and k == 1)
                last.then_inc(s["pv2"], 1)

            def oproj2(a):
                pe.wait_ge(s["ot2_lo"], nth("ot2_lo", a, G))
                pe.wait_ge(s["s2_sb"], nth("s2_sb", a, G))
                project(a, "wo2", "o2_ps")

            def logits(a, k):
                if k == 0:
                    pe.wait_ge(s["xt3_lo"], nth("xt3_lo", a, 1))
                if k == 3:
                    pe.wait_ge(s["x2"], nth("x2", a, 1))
                t, u = divmod(k, 2)
                for dk in range(ND):
                    last = three(ps[:, (2, 3, 4, 0)[k], :], both(XT, full, dk, slice(t * P, t * P + P)),
                                 both(W["se"], full, dk, slice(u * 512, u * 512 + 512)), dk == 0, dk == ND - 1)
                last.then_inc(s["lg_ps"], 1)

            def lt(b, c):
                if c == 0:
                    pe.wait_ge(s["lg_sb"], nth("lg_sb", b, 4))
                else:
                    pe.wait_ge(s["ge"], nth("ge", b, 4 * c - 1))
                for e in range(2):
                    for t in range(NT):
                        last = te.transpose(ps[:, 6, e * S + t * P:e * S + (t + 1) * P],
                                            lg[:, t, c * CHUNK + e * P:c * CHUNK + (e + 1) * P], ident[:, :])
                last.then_inc(s["lt_ps"], 1)

            def dispatch(b, c):
                pe.wait_ge(s["edn"], nth("edn", b, c + 1))
                for t in range(NT):
                    for e in range(2):
                        last = te.transpose(ps[:, 6, t * CHUNK + e * P:t * CHUNK + (e + 1) * P],
                                            edt[:, e, t * P:(t + 1) * P], ident[:, :])
                last.then_inc(s["ds_ps"], 1)

            def slots(b, c):
                pe.wait_ge(s["ds_lo"], nth("ds_lo", b, c + 1))
                if c:
                    pe.wait_ge(s["ge"], nth("ge", b, 4 * c))
                else:
                    pe.wait_ge(s["xs_lo"], nth("xs_lo", b, 1))
                for dk in range(ND):
                    for t in range(NT):
                        last = three(ps[:, 5, dk * CHUNK:(dk + 1) * CHUNK], both(XS, full, t, slice(dk * P, dk * P + P)),
                                     both(DS, full, t), t == 0, t == NT - 1)
                last.then_inc(s["sl_ps"], 1)

            def hidden(b, c, q):
                n = c * 4 + q
                if q == 0:
                    pe.wait_ge(s["sl_lo"], nth("sl_lo", b, c + 1))
                    if c:
                        pe.wait_ge(s["cb_lo"], nth("cb_lo", b, c))
                if q >= 2:
                    pe.wait_ge(s["ge"], nth("ge", b, n - 1))
                for i in range(2):
                    m = 2 * q + i
                    for dk in range(ND):
                        last = three(ps[:, 6 - q % 2, i * CHUNK:(i + 1) * CHUNK],
                                     both(W["w1"], full, dk, slice(m * P, m * P + P)), both(SL, full, dk),
                                     dk == 0, dk == ND - 1)
                last.then_inc(s["h_ps"], 1)

            def outer(b, c, e):
                if e == 0:
                    pe.wait_ge(s["h_lo"], nth("h_lo", b, 4 * c + 4))
                    if c:
                        pe.wait_ge(s["acc"], nth("acc", b, c))
                for k in range(NM):
                    last = three(ps[:, 7, e * D:(e + 1) * D], both(HH, full, k, slice(e * P, e * P + P)),
                                 both(W["w2"], full, k), k == 0, k == NM - 1)
                if e == 1:
                    last.then_inc(s["pr_ps"], 1)

            def comb(b, c):
                pe.wait_ge(s["ec"], nth("ec", b, c + 1))
                if c == NC - 1:
                    pe.wait_ge(s["ge"], nth("ge", b, 16))
                for e in range(2):
                    for t in range(NT):
                        last = te.transpose(ps[:, 6, e * S + t * P:e * S + (t + 1) * P],
                                            ecomb[:, t, e * P:(e + 1) * P], ident[:, :])
                last.then_inc(s["cb_ps"], 1)

            def combine(b, c):
                pe.wait_ge(s["pr_lo"], nth("pr_lo", b, c + 1))
                pe.wait_ge(s["cb_lo"], nth("cb_lo", b, c + 1))
                for t in range(NT):
                    for e in range(2):
                        last = three(ps[:, 7, t * D:(t + 1) * D], both(CB, full, e, slice(t * P, t * P + P)),
                                     both(PR, full, e), e == 0, e == 1)
                last.then_inc(s["d_ps"], 1)

            pe.wait_ge(s["i_const"], 16)
            pe.wait_ge(s["i_xn"], 1)
            for dk in range(ND):
                for e in range(NS):
                    last = te.transpose(ps[:, 2 * dk + e // 4, (e % 4) * P:(e % 4 + 1) * P],
                                        g_se[:, e, dk * P:(dk + 1) * P], ident[:, :])
            last.then_inc(s["i_sps"], 1)
            pe.wait_ge(s["i_slo"], 1)
            pe.wait_ge(s["i_lo"], len(WEIGHTS))

            steps = dict(xt=xt, v=v, qk=qk, scores=scores, transp=transp, pv=pv, oproj=oproj, kv=kv, k2t=k2t, q2=q2,
                         s2=s2_step, t2=t2, pv2=pv2, oproj2=oproj2, logits=logits, lt=lt, dispatch=dispatch, slots=slots,
                         hidden=hidden, outer=outer, comb=comb, combine=combine)
            run(steps, a=0)
            with pe.Fori(0, B - 1) as b:
                run(steps, a=b + 1, b=b)
            run(steps, b=B - 1)

        @block.scalar
        def _(act):
            def copy(o, i):
                return nc.scalar.activation(o, i, ACT.Copy)

            def halves(bank, rows=P):
                return ps[0:rows, bank, :].rearrange("p (k s) -> p k s", k=2)

            def xt(a, n):
                act.wait_ge(s[f"xt{n}_ps"], nth(f"xt{n}_ps", a, 1))
                copy(xt_hi[:, :, :], halves(0 if n == 1 else 1)).then_inc(s[f"xt{n}_hi"], 1)

            def qk(a, g):
                act.wait_ge(s["qk_ps"], nth("qk_ps", a, g + 1))
                if g:
                    act.wait_ge(s["s_ps"], nth("s_ps", a, 4 * g))
                nc.scalar.activation(qk_f[:, 0, :], ps[:, 0, 0:S], ACT.Identity, scale=ATTN_SCALE,
                                     bias=cols[:, BQ + g:BQ + g + 1])
                nc.scalar.activation(qk_f[:, 1, :], ps[:, 0, S:2 * S], ACT.Identity,
                                     bias=cols[:, BK + g:BK + g + 1]).then_inc(s["qk_sb"], 1)

            def scores(a, h):
                act.wait_ge(s["mx"], nth("mx", a, h + 1))
                if h >= 2:
                    act.wait_ge(s["t_ps"], nth("t_ps", a, h - 1))
                for t in range(NT):
                    last = nc.scalar.activation(p_sb[:, h % 2, t, :], ps[:, 1 + h % 2, t * S:(t + 1) * S], ACT.Exp,
                                                bias=mx[:, h, t:t + 1], accum_out=ls[:, h, t:t + 1])
                last.then_inc(s["ex"], 1)

            def normed(a, h):
                act.wait_ge(s["rl"], nth("rl", a, h + 1))
                for t in range(NT):
                    last = nc.scalar.activation(p_sb[:, h % 2, t, :], p_sb[:, h % 2, t, :], ACT.Copy,
                                                scale=rl[:, h, t:t + 1])
                last.then_inc(s["pn"], 1)

            def transp(a, h):
                act.wait_ge(s["t_ps"], nth("t_ps", a, h + 1))
                if h >= 2:
                    act.wait_ge(s["pv"], nth("pv", a, h - 1))
                copy(pt_hi[:, h % 2, :, :], halves(3 + h % 2)).then_inc(s["pt_hi"], 1)

            def ot(a, g):
                act.wait_ge(s["pv"], nth("pv", a, 4 * g + 4))
                copy(ot_hi[:, g, :], ps[:, 0, 0:S]).then_inc(s["ot_hi"], 1)

            def q2(a, g):
                act.wait_ge(s["q2_ps"], nth("q2_ps", a, g + 1))
                if g >= 2:
                    act.wait_ge(s["s2_ps"], nth("s2_ps", a, g - 1))
                nc.scalar.activation(q2_f[:, g % 2, :], ps[:, 0, 0:S], ACT.Identity, scale=XATTN_SCALE,
                                     bias=cols[:, BQ2 + g:BQ2 + g + 1]).then_inc(s["q2_sb"], 1)

            def s2_step(a, g):
                act.wait_ge(s["sh2"], nth("sh2", a, g + 1))
                nc.scalar.activation(s2[:, g % 2, :, :], s2[:, g % 2, :, :], ACT.Exp).then_inc(s["ex2"], 1)

            def t2(a, g, u):
                n = 2 * g + u
                act.wait_ge(s["t2_ps"], nth("t2_ps", a, n + 1))
                if n >= 2:
                    act.wait_ge(s["pv2"], nth("pv2", a, n - 1))
                copy(pt2_hi[:, u, :, :], halves(3 + u, CTX)).then_inc(s["pt2_hi"], 1)

            def pv2(a, g, u):
                if u == 0:
                    return
                act.wait_ge(s["pv2"], nth("pv2", a, 2 * g + 2))
                if g == 0:
                    act.wait_ge(s["o_ps"], nth("o_ps", a, 1))
                copy(ot_hi[:, g, :], ps[:, 2, 0:S]).then_inc(s["ot2_hi"], 1)

            def logits(a, k):
                act.wait_ge(s["lg_ps"], nth("lg_ps", a, k + 1))
                t, u = divmod(k, 2)
                copy(lg[:, t, u * 512:(u + 1) * 512], ps[:, (2, 3, 4, 0)[k], :]).then_inc(s["lg_sb"], 1)

            def edt_step(b, c):
                act.wait_ge(s["cm"], nth("cm", b, c + 1))
                for e in range(2):
                    k = 2 * c + e
                    last = nc.scalar.activation(edt[:, e, :], ps[:, 6, e * S:(e + 1) * S], ACT.Exp,
                                                bias=cm[:, k:k + 1], accum_out=csum[:, k:k + 1])
                last.then_inc(s["ed"], 1)

            def ec(b, c):
                if c == 0:
                    act.wait_ge(s["rm"], nth("rm", b, 2))
                else:
                    act.wait_ge(s["cb_ps"], nth("cb_ps", b, c))
                for t in range(NT):
                    last = nc.scalar.activation(ecomb[:, t, :], lg[:, t, c * CHUNK:(c + 1) * CHUNK], ACT.Exp,
                                                bias=rm[:, t:t + 1], accum_out=rsum[:, t, c:c + 1])
                last.then_inc(s["ec"], 1)

            def dispatch(b, c):
                act.wait_ge(s["ds_ps"], nth("ds_ps", b, c + 1))
                if c >= 2:
                    act.wait_ge(s["d_ps"], nth("d_ps", b, c - 1))
                copy(ds_hi[:, :, :], halves(6)).then_inc(s["ds_hi"], 1)

            def slots(b, c):
                act.wait_ge(s["sl_ps"], nth("sl_ps", b, c + 1))
                if c:
                    act.wait_ge(s["h_ps"], nth("h_ps", b, 4 * c))
                copy(sl_hi[:, :, :], halves(5)).then_inc(s["sl_hi"], 1)

            def hidden(b, c, q):
                n = 4 * c + q
                act.wait_ge(s["h_ps"], nth("h_ps", b, n + 1))
                if c and q == 0:
                    act.wait_ge(s["pr_ps"], nth("pr_ps", b, c))
                nc.scalar.activation(h_f[:, 2 * q:2 * q + 2, :], halves(6 - q % 2), ACT.Gelu).then_inc(s["ge"], 1)

            def outer(b, c, e):
                if e == 0:
                    return
                act.wait_ge(s["pr_ps"], nth("pr_ps", b, c + 1))
                copy(pr_hi[:, :, :], halves(7)).then_inc(s["pr_hi"], 1)

            def comb(b, c):
                act.wait_ge(s["cb_ps"], nth("cb_ps", b, c + 1))
                if c < NC - 1:
                    act.wait_ge(s["sl_ps"], nth("sl_ps", b, c + 2))
                copy(cb_hi[:, :, :], halves(6)).then_inc(s["cb_hi"], 1)

            for name in WEIGHTS:
                act.wait_ge(s["i_" + name], 16)
                if name == "w1":
                    act.wait_ge(s["i_w1g"], 1)
                copy(W[name][0][:, :, :], stage[name][:, :, :]).then_inc(s["i_hi"], 1)
            act.wait_ge(s["i_sg"], 2)
            copy(W["se"][0][:, :, :], se_t[:, :, :]).then_inc(s["i_shi"], 1)
            act.wait_ge(s["i_cols"], 1)

            steps = dict(xt=xt, qk=qk, scores=scores, normed=normed, transp=transp, ot=ot, q2=q2, s2=s2_step, t2=t2,
                         pv2=pv2, logits=logits, edt=edt_step, ec=ec, dispatch=dispatch, slots=slots, hidden=hidden,
                         outer=outer, comb=comb)
            run(steps, a=0)
            with act.Fori(0, B - 1) as b:
                run(steps, a=b + 1, b=b)
            run(steps, b=B - 1)

        @block.vector
        def _(dve):
            V = nc.vector

            def minus(o, a, hi):
                return V.tensor_tensor(o, a, hi.bitcast(f32), ALU.subtract)

            def halves(bank, rows=P):
                return ps[0:rows, bank, :].rearrange("p (k s) -> p k s", k=2)

            def norm(a, n):
                src = (x, x1, x2)[n - 1]
                if n == 1:
                    dve.wait_ge(s["x_in"], nth("x_in", a, 16))
                else:
                    dve.wait_ge(s[f"x{n - 1}"], nth(f"x{n - 1}", a, 1))
                for t in range(NT):
                    last = V.bn_stats(st[:, t, :], src[:, t, :])
                last.then_inc(s[f"ln{n}_st"], 1)
                dve.wait_ge(s[f"ln{n}_st"], nth(f"ln{n}_st", a, 1))
                dve.sem_inc(s["dve_held"], 1)
                for t in range(NT):
                    last = V.bn_aggr(mv[:, t, :], st[:, t, :])
                last.then_inc(s[f"ln{n}_mv"], 1)
                dve.wait_ge(s[f"ln{n}_mv"], nth(f"ln{n}_mv", a, 1))
                V.tensor_scalar(ve[:, 0, :], mv[:, :, 1], LN_EPS, None, ALU.add)
                V.tensor_scalar(ve[:, 1, :], mv[:, :, 1], 1.0, None, ALU.mult).then_inc(s[f"ln{n}_ve"], 1)
                dve.wait_ge(s[f"ln{n}_pw"], nth(f"ln{n}_pw", a, 1))
                scale = pw[:, 0, :]
                if n == 3:
                    V.tensor_tensor(sc3[:, 0, :], pw[:, 0, :], pw[:, 1, :], ALU.mult).then_inc(s["ln3_sc"], 1)
                    dve.wait_ge(s["ln3_sc"], nth("ln3_sc", a, 1))
                    V.tensor_scalar(sc3[:, 1, :], sc3[:, 0, :], float(D) ** 0.5, RMS_EPS, ALU.mult, ALU.max)\
                        .then_inc(s["ln3_sc"], 1)
                    dve.wait_ge(s["ln3_sc"], nth("ln3_sc", a, 2))
                    V.reciprocal(sc3[:, 2, :], sc3[:, 1, :]).then_inc(s["ln3_sc"], 1)
                    dve.wait_ge(s["ln3_sc"], nth("ln3_sc", a, 3))
                    V.scalar_tensor_tensor(sc3[:, 3, :], sc3[:, 2, :], float(D) ** 0.5, pw[:, 0, :], ALU.mult, ALU.mult)\
                        .then_inc(s["ln3_sc"], 1)
                    dve.wait_ge(s["ln3_sc"], nth("ln3_sc", a, 4))
                    scale = sc3[:, 3, :]
                for t in range(NT):
                    last = V.tensor_scalar(xh[:, t, :], src[:, t, :], mv[:, t, 0:1], scale[:, t:t + 1],
                                           ALU.subtract, ALU.mult)
                last.then_inc(s[f"ln{n}_xh"], 1)

            def xt(a, n):
                dve.wait_ge(s[f"xt{n}_hi"], nth(f"xt{n}_hi", a, 1))
                minus(xt_lo[:, :, :], halves(0 if n == 1 else 1), xt_hi[:, :, :]).then_inc(s[f"xt{n}_lo"], 1)

            def v(a):
                dve.wait_ge(s["v_ps"], nth("v_ps", a, 1))
                V.tensor_tensor(v_f[:, :, :], halves(1), bv[:, :].unsqueeze(1).broadcast_to([P, NT, D]), ALU.add)\
                    .then_inc(s["v_sb"], 1)

            def qk(a, g):
                dve.wait_ge(s["qk_sb"], nth("qk_sb", a, g + 1))
                V.tensor_copy(qk_h[:, :, :], qk_f[:, :, :]).then_inc(s["qk_hi"], 1)
                dve.wait_ge(s["qk_hi"], nth("qk_hi", a, g + 1))
                V.scalar_tensor_tensor(qk_l[:, 0, :], qk_h[:, 0, :].bitcast(f32), cols[:, NMASK:NMASK + 1],
                                       qk_f[:, 0, :], ALU.mult, ALU.add)
                minus(qk_l[:, 1, :], qk_f[:, 1, :], qk_h[:, 1, :]).then_inc(s["qk_lo"], 1)

            def scores(a, h):
                dve.wait_ge(s["s_ps"], nth("s_ps", a, h + 1))
                V.tensor_reduce(mx[:, h, :], halves(1 + h % 2), AX, ALU.max, negate=True).then_inc(s["mx"], 1)

            def normed(a, h):
                dve.wait_ge(s["ex"], nth("ex", a, h + 1))
                V.reciprocal(rl[:, h, :], ls[:, h, :]).then_inc(s["rl"], 1)

            def transp(a, h):
                dve.wait_ge(s["pt_hi"], nth("pt_hi", a, h + 1))
                minus(pt_lo[:, h % 2, :, :], halves(3 + h % 2), pt_hi[:, h % 2, :, :]).then_inc(s["pt_lo"], 1)

            def ot(a, g):
                dve.wait_ge(s["ot_hi"], nth("ot_hi", a, g + 1))
                minus(ot_lo[:, g, :], ps[:, 0, 0:S], ot_hi[:, g, :]).then_inc(s["ot_lo"], 1)

            def oproj(a):
                dve.wait_ge(s["o_ps"], nth("o_ps", a, 1))
                dve.wait_ge(s["x_bo"], nth("x_bo", a, 1))
                V.tensor_tensor(x1[:, :, :], halves(0), x[:, :, :], ALU.add).then_inc(s["x1"], 1)

            def kv(a):
                dve.wait_ge(s["kv_ps"], nth("kv_ps", a, 1))
                dve.wait_ge(s["vg_lo"], nth("vg_lo", a, G))
                kin = ps[0:CTX, 1, 0:D].rearrange("p (h d) -> p h d", h=H)
                kb = bkv2[:, 0:D].rearrange("p (h d) -> p h d", h=H)
                for e in range(2):
                    last = V.tensor_tensor(k2d[:, :, e, :], kin, kb, ALU.add)
                last.then_inc(s["kd_sb"], 1)
                V.tensor_tensor(v2_f[:, :], ps[0:CTX, 1, D:2 * D], bkv2[:, D:2 * D], ALU.add).then_inc(s["v2_sb"], 1)
                dve.wait_ge(s["mask_in"], nth("mask_in", a, 16))
                V.tensor_scalar(mk_f[:, :], mk_i[:, :], 0.0, -3.0e38, ALU.is_equal, ALU.mult).then_inc(s["mk"], 1)
                dve.wait_ge(s["mk"], nth("mk", a, 1))
                V.tensor_scalar(mk_f[:, :], mk_f[:, :], 4.0, None, ALU.mult).then_inc(s["mk"], 1)

            def k2t(a):
                dve.wait_ge(s["k2t_ps"], nth("k2t_ps", a, 1))
                V.tensor_copy(k2_n[:, :, :], ps[:, 2, 0:G * CTX].rearrange("p (g c) -> p g c", g=G))\
                    .then_inc(s["k2_n"], 1)

            def q2(a, g):
                dve.wait_ge(s["q2_sb"], nth("q2_sb", a, g + 1))
                V.tensor_copy(qk_h[:, g % 2, :], q2_f[:, g % 2, :]).then_inc(s["q2_hi"], 1)
                dve.wait_ge(s["q2_hi"], nth("q2_hi", a, g + 1))
                V.scalar_tensor_tensor(q2_a[:, g % 2, :], qk_h[:, g % 2, :].bitcast(f32), cols[:, NMASK:NMASK + 1],
                                       q2_f[:, g % 2, :], ALU.mult, ALU.add).then_inc(s["q2_a"], 1)

            def by_head(g, t):
                return s2[:, g % 2, t, :].rearrange("p (r c) -> p r c", r=R)

            def s2_step(a, g):
                dve.wait_ge(s["s2_ps"], nth("s2_ps", a, g + 1))
                if g == 0:
                    dve.wait_ge(s["mk"], nth("mk", a, 2))
                if g >= 2:
                    dve.wait_ge(s["t2_ps"], nth("t2_ps", a, 2 * g - 2))
                for t in range(NT):
                    last = V.tensor_tensor(by_head(g, t), ps[:, t, 0:R * CTX].rearrange("p (r c) -> p r c", r=R),
                                           mk_f[:, :].unsqueeze(1).broadcast_to([P, R, CTX]), ALU.add)
                last.then_inc(s["s2_sb"], 1)
                dve.wait_ge(s["s2_sb"], nth("s2_sb", a, g + 1))
                V.tensor_reduce(mx2[:, g, :, :], s2[:, g % 2, :, :].rearrange("p t (r c) -> p (t r) c", r=R), AX,
                                ALU.max, negate=True).then_inc(s["mx2"], 1)
                dve.wait_ge(s["mx2"], nth("mx2", a, g + 1))
                w = s2[:, g % 2, :, :].rearrange("p t (r c) -> p (t r) c", r=R)
                V.tensor_tensor(w, w, mx2[:, g, :, :].rearrange("p t r -> p (t r)").unsqueeze(2)
                                .broadcast_to([P, NT * R, CTX]), ALU.add).then_inc(s["sh2"], 1)

            def n2(a, g):
                dve.wait_ge(s["ex2"], nth("ex2", a, g + 1))
                w = s2[:, g % 2, :, :].rearrange("p t (r c) -> p (t r) c", r=R)
                V.tensor_reduce(ls2[:, g, :, :], w, AX, ALU.add).then_inc(s["sm2"], 1)
                dve.wait_ge(s["sm2"], nth("sm2", a, g + 1))
                V.reciprocal(rl2[:, g, :, :], ls2[:, g, :, :]).then_inc(s["rl2"], 1)
                dve.wait_ge(s["rl2"], nth("rl2", a, g + 1))
                V.tensor_tensor(w, w, rl2[:, g, :, :].rearrange("p t r -> p (t r)").unsqueeze(2)
                                .broadcast_to([P, NT * R, CTX]), ALU.mult).then_inc(s["pn2"], 1)

            def t2(a, g, u):
                dve.wait_ge(s["pt2_hi"], nth("pt2_hi", a, 2 * g + u + 1))
                minus(pt2_lo[:, u, :, :], halves(3 + u, CTX), pt2_hi[:, u, :, :]).then_inc(s["pt2_lo"], 1)

            def pv2(a, g, u):
                if u == 0:
                    return
                dve.wait_ge(s["ot2_hi"], nth("ot2_hi", a, g + 1))
                minus(ot_lo[:, g, :], ps[:, 2, 0:S], ot_hi[:, g, :]).then_inc(s["ot2_lo"], 1)

            def oproj2(a):
                dve.wait_ge(s["o2_ps"], nth("o2_ps", a, 1))
                dve.wait_ge(s["x1_bo"], nth("x1_bo", a, 1))
                V.tensor_tensor(x2[:, :, :], halves(0), x1[:, :, :], ALU.add).then_inc(s["x2"], 1)

            def xs(a):
                V.tensor_copy(xs_hi[:, :, :], xh[:, :, :]).then_inc(s["xs_hi"], 1)
                dve.wait_ge(s["xs_hi"], nth("xs_hi", a, 1))
                minus(xs_lo[:, :, :], xh[:, :, :], xs_hi[:, :, :]).then_inc(s["xs_lo"], 1)

            def begin(b):
                dve.wait_ge(s["x2"], nth("x2", b, 1))
                V.tensor_copy(res[:, :, :], x2[:, :, :]).then_inc(s["res"], 1)
                dve.wait_ge(s["lg_sb"], nth("lg_sb", b, 4))
                for t in range(NT):
                    V.tensor_reduce(rm[:, t:t + 1], lg[:, t, :], AX, ALU.max, negate=True).then_inc(s["rm"], 1)

            def lt(b, c):
                dve.wait_ge(s["lt_ps"], nth("lt_ps", b, c + 1))
                V.tensor_reduce(cm[:, 2 * c:2 * c + 2], halves(6), AX, ALU.max, negate=True).then_inc(s["cm"], 1)

            def edt_step(b, c):
                dve.wait_ge(s["ed"], nth("ed", b, c + 1))
                V.reciprocal(crec[:, 2 * c:2 * c + 2], csum[:, 2 * c:2 * c + 2]).then_inc(s["rc"], 1)
                dve.wait_ge(s["rc"], nth("rc", b, c + 1))
                for e in range(2):
                    last = V.tensor_scalar(edt[:, e, :], edt[:, e, :], crec[:, 2 * c + e:2 * c + e + 1], None, ALU.mult)
                last.then_inc(s["edn"], 1)

            def dispatch(b, c):
                dve.wait_ge(s["ds_hi"], nth("ds_hi", b, c + 1))
                minus(ds_lo[:, :, :], halves(6), ds_hi[:, :, :]).then_inc(s["ds_lo"], 1)

            def slots(b, c):
                dve.wait_ge(s["sl_hi"], nth("sl_hi", b, c + 1))
                minus(sl_lo[:, :, :], halves(5), sl_hi[:, :, :]).then_inc(s["sl_lo"], 1)

            def hidden(b, c, q):
                n = 4 * c + q
                dve.wait_ge(s["ge"], nth("ge", b, n + 1))
                V.tensor_copy(h_hi[:, 2 * q:2 * q + 2, :], h_f[:, 2 * q:2 * q + 2, :]).then_inc(s["h_hi"], 1)
                dve.wait_ge(s["h_hi"], nth("h_hi", b, n + 1))
                minus(h_lo[:, 2 * q:2 * q + 2, :], h_f[:, 2 * q:2 * q + 2, :], h_hi[:, 2 * q:2 * q + 2, :])\
                    .then_inc(s["h_lo"], 1)

            def outer(b, c, e):
                if e == 0:
                    return
                dve.wait_ge(s["pr_hi"], nth("pr_hi", b, c + 1))
                minus(pr_lo[:, :, :], halves(7), pr_hi[:, :, :]).then_inc(s["pr_lo"], 1)

            def comb(b, c):
                dve.wait_ge(s["cb_hi"], nth("cb_hi", b, c + 1))
                minus(cb_lo[:, :, :], halves(6), cb_hi[:, :, :]).then_inc(s["cb_lo"], 1)

            def combine(b, c):
                dve.wait_ge(s["d_ps"], nth("d_ps", b, c + 1))
                if c == 0:
                    dve.wait_ge(s["out"], nth("out", b, 16))
                    V.tensor_copy(acc[:, :, :], halves(7)).then_inc(s["acc"], 1)
                else:
                    dve.wait_ge(s["acc"], nth("acc", b, c))
                    V.tensor_tensor(acc[:, :, :], halves(7), acc[:, :, :], ALU.add).then_inc(s["acc"], 1)

            def finish(b):
                dve.wait_ge(s["ec"], nth("ec", b, NC))
                V.tensor_reduce(rtot[:, :], rsum[:, :, :], AX, ALU.add).then_inc(s["rs_sum"], 1)
                dve.wait_ge(s["rs_sum"], nth("rs_sum", b, 1))
                V.reciprocal(rrec[:, :], rtot[:, :]).then_inc(s["rr"], 1)
                dve.wait_ge(s["rr"], nth("rr", b, 1))
                dve.wait_ge(s["acc"], nth("acc", b, NC))
                dve.wait_ge(s["res"], nth("res", b, 1))
                for t in range(NT):
                    last = V.scalar_tensor_tensor(acc[:, t, :], acc[:, t, :], rrec[:, t:t + 1], res[:, t, :],
                                                  ALU.mult, ALU.add)
                last.then_inc(s["y"], 1)

            dve.wait_ge(s["i_const"], 16)
            V.tensor_scalar(cols[:, BQ:BQ + G], cols[:, BQ:BQ + G], ATTN_SCALE, None, ALU.mult)
            V.tensor_scalar(cols[:, BQ2:BQ2 + G], cols[:, BQ2:BQ2 + G], XATTN_SCALE, None, ALU.mult)\
                .then_inc(s["i_cols"], 1)
            dve.wait_ge(s["i_bias"], 16)
            dve.wait_ge(s["i_se"], 16)
            V.tensor_tensor(se_sq[:, :, :], g_se[:, :, :], g_se[:, :, :], ALU.mult).then_inc(s["i_sq"], 1)
            dve.wait_ge(s["i_sq"], 1)
            V.tensor_reduce(se_ss[:, :], se_sq[:, :, :], AX, ALU.add).then_inc(s["i_st"], 1)
            dve.wait_ge(s["i_sr"], 4)
            for e in range(NS):
                last = V.tensor_scalar(g_se[:, e, :], g_se[:, e, :], se_sc[:, e:e + 1], None, ALU.mult)
            last.then_inc(s["i_xn"], 1)
            dve.wait_ge(s["i_gam"], 16)
            V.tensor_tensor(gxs[:, :], gam[:, 0, :], gam[:, 1, :], ALU.mult).then_inc(s["i_gxs"], 1)
            dve.wait_ge(s["i_w1"], 16)
            for dk in range(ND):
                last = V.tensor_scalar(stage["w1"][:, dk, :], stage["w1"][:, dk, :], gam[:, 0, dk:dk + 1], None, ALU.mult)
            last.then_inc(s["i_w1g"], 1)
            for n, name in enumerate(WEIGHTS):
                dve.wait_ge(s["i_hi"], n + 1)
                minus(W[name][1][:, :, :], stage[name][:, :, :], W[name][0][:, :, :]).then_inc(s["i_lo"], 1)
            dve.wait_ge(s["i_sps"], 1)
            dve.wait_ge(s["i_gxs"], 1)
            for dk in range(ND):
                V.tensor_scalar(se_t[:, dk, :], ps[:, 2 * dk:2 * dk + 2, :].rearrange("p u n -> p (u n)"),
                                gxs[:, dk:dk + 1], None, ALU.mult).then_inc(s["i_sg"], 1)
            dve.wait_ge(s["i_sg"], 2)
            dve.wait_ge(s["i_shi"], 1)
            minus(W["se"][1][:, :, :], se_t[:, :, :], W["se"][0][:, :, :]).then_inc(s["i_slo"], 1)

            steps = dict(norm=norm, xt=xt, v=v, qk=qk, scores=scores, normed=normed, transp=transp, ot=ot, oproj=oproj,
                         kv=kv, k2t=k2t, q2=q2, s2=s2_step, n2=n2, t2=t2, pv2=pv2, oproj2=oproj2, xs=xs, begin=begin,
                         lt=lt, edt=edt_step, dispatch=dispatch, slots=slots, hidden=hidden, outer=outer, comb=comb,
                         combine=combine, finish=finish)
            run(steps, a=0)
            with dve.Fori(0, B - 1) as b:
                run(steps, a=b + 1, b=b)
            run(steps, b=B - 1)

        @block.gpsimd
        def _(pool):
            Q = nc.gpsimd

            def copy(o, i):
                return Q.tensor_scalar(o, i, 1.0, None, ALU.mult)

            def power(o, i, col, w):
                return Q.tensor_tensor(o, i, cols[:, col:col + 1].broadcast_to([P, w]), ALU.pow)

            def norm(a, n):
                pool.wait_ge(s[f"ln{n}_ve"], nth(f"ln{n}_ve", a, 1))
                w = 2 if n < 3 else 4
                Q.tensor_tensor(pw[:, :, :].rearrange("p a b -> p (a b)")[:, 0:w],
                                ve[:, :, :].rearrange("p a b -> p (a b)")[:, 0:w],
                                cols[:, EXPO:EXPO + w], ALU.pow).then_inc(s[f"ln{n}_pw"], 1)
                if n < 3:
                    o, bias, signal = ((x, bo, "x_bo"), (x1, bo2, "x1_bo"))[n - 1]
                    pool.wait_ge(s[f"ln{n}_xh"], nth(f"ln{n}_xh", a, 1))
                    Q.tensor_tensor(o[:, :, :], o[:, :, :], bias[:, :].unsqueeze(1).broadcast_to([P, NT, D]), ALU.add)\
                        .then_inc(s[signal], 1)

            def context(a):
                pool.wait_ge(s["ctx_in"], nth("ctx_in", a, 16))
                pool.sem_inc(s["pool_held"], 1)
                copy(cx_hi[:, :, :], cx[:, :, :]).then_inc(s["ct_hi"], 1)
                pool.wait_ge(s["ct_hi"], nth("ct_hi", a, 1))
                Q.tensor_tensor(cx_lo[:, :, :], cx[:, :, :], cx_hi[:, :, :].bitcast(f32), ALU.subtract)\
                    .then_inc(s["ct_lo"], 1)

            def qk(a, g):
                pool.wait_ge(s["v_sb"], nth("v_sb", a, 1))
                if g:
                    pool.wait_ge(s["pv"], nth("pv", a, 4 * g))
                elif later(a):
                    pool.wait_ge(s["pv2"], nth("pv2", a - 1, 8))
                pool.sem_inc(s["pool_held"], 1)
                src = v_f[:, :, g * R * HD:(g + 1) * R * HD].rearrange("p t (r d) -> p t r d", r=R)
                copy(vg[:, :, :, 0:HD], src).then_inc(s["vg_hi"], 1)
                pool.wait_ge(s["vg_hi"], nth("vg_hi", a, g + 1))
                Q.tensor_tensor(vg[:, :, :, HD:2 * HD], src, vg[:, :, :, 0:HD].bitcast(f32), ALU.subtract)\
                    .then_inc(s["vg_lo"], 1)

            def k2(a, g):
                pool.wait_ge(s["k2_n"], nth("k2_n", a, 1))
                if g:
                    pool.wait_ge(s["s2_ps"], nth("s2_ps", a, g))
                Q.tensor_tensor(k2_f[:, :, :], k2_n[:, g, :].unsqueeze(1).broadcast_to([P, R, CTX]),
                                cols[:, BM:BM + R].unsqueeze(2).broadcast_to([P, R, CTX]), ALU.mult)\
                    .then_inc(s["k2_f"], 1)
                pool.wait_ge(s["k2_f"], nth("k2_f", a, g + 1))
                pool.sem_inc(s["pool_held"], 1)
                flat = k2_f[:, :, :].rearrange("p r c -> p (r c)")
                copy(k2_hi[:, :], flat).then_inc(s["k2_hi"], 1)
                pool.wait_ge(s["k2_hi"], nth("k2_hi", a, g + 1))
                Q.tensor_tensor(k2_lo[:, :], flat, k2_hi[:, :].bitcast(f32), ALU.subtract).then_inc(s["k2_lo"], 1)

            def v2(a, g):
                pool.wait_ge(s["v2_sb"], nth("v2_sb", a, 1))
                if g >= 2:
                    pool.wait_ge(s["pv2"], nth("pv2", a, 2 * (g - 1)))
                else:
                    pool.wait_ge(s["pv"], nth("pv", a, H))
                pool.sem_inc(s["pool_held"], 1)
                src = v2_f[:, g * R * HD:(g + 1) * R * HD].rearrange("p (r d) -> p r d", r=R)
                copy(vg[0:CTX, g % 2, :, 0:HD], src).then_inc(s["vg2_hi"], 1)
                pool.wait_ge(s["vg2_hi"], nth("vg2_hi", a, g + 1))
                Q.tensor_tensor(vg[0:CTX, g % 2, :, HD:2 * HD], src, vg[0:CTX, g % 2, :, 0:HD].bitcast(f32),
                                ALU.subtract).then_inc(s["vg2_lo"], 1)

            Q.memset(vg[:, :, :, :].bitcast(f32), 0.0).then_inc(s["i_vz"], 1)
            pool.wait_ge(s["i_vz"], 1)
            pool.wait_ge(s["i_const"], 16)
            pool.wait_ge(s["i_st"], 1)
            power(se_n[:, :], se_ss[:, :], EXPO + 2, NS).then_inc(s["i_sr"], 1)
            pool.wait_ge(s["i_sr"], 1)
            Q.tensor_scalar(se_n[:, :], se_n[:, :], RMS_EPS, None, ALU.max).then_inc(s["i_sr"], 1)
            pool.wait_ge(s["i_sr"], 2)
            power(se_i[:, :], se_n[:, :], EXPO + 4, NS).then_inc(s["i_sr"], 1)
            pool.wait_ge(s["i_sr"], 3)
            Q.tensor_scalar(se_sc[:, :], se_i[:, :], float(D) ** 0.5, None, ALU.mult).then_inc(s["i_sr"], 1)
            pool.wait_ge(s["i_bias"], 16)

            steps = dict(norm=norm, context=context, qk=qk, k2=k2, v2=v2)
            run(steps, a=0)
            with pool.Fori(0, B - 1) as b:
                run(steps, a=b + 1, b=b)

        @block.sync
        def _(sp):
            def tokens(t, b):
                return t[bass.ds(b, 1), :, :].rearrange("o (t p) d -> p (o t) d", p=P)

            def load_x(b):
                if later(b):
                    sp.wait_ge(s["x1"], nth("x1", b - 1, 1))
                sp.dma_start(x[:, :, :], tokens(t_in["x"], b)).then_inc(s["x_in"], 16)

            def load_ctx(b):
                if later(b):
                    sp.wait_ge(s["kv_ps"], nth("kv_ps", b - 1, 1))
                    sp.wait_ge(s["mk"], nth("mk", b - 1, 2))
                sp.dma_start(cx[:, :, :], t_in["ctxT"][bass.ds(b, 1), :, :].rearrange("o (k p) c -> p (o k) c", p=P))\
                    .then_inc(s["ctx_in"], 16)
                sp.dma_start(mk_i[:, :], t_in["mask"][bass.ds(b, 1), :].broadcast_to([P, CTX])).then_inc(s["mask_in"], 16)

            def store(b):
                sp.wait_ge(s["y"], nth("y", b, 1))
                sp.dma_start(tokens(out, b), acc[:, :, :]).then_inc(s["out"], 16)

            def load(name):
                sp.dma_start(stage[name][:, :, :], t_in[name]).then_inc(s["i_" + name], 16)

            sp.sem_inc(s["out"], 16)
            sp.dma_start(consts[:, :], t_in["consts"]).then_inc(s["i_const"], 16)
            sp.dma_start(g_se[:, :, :], t_in["se"].rearrange("(e p) d -> p e d", p=P)).then_inc(s["i_se"], 16)
            sp.dma_start(biases[:, :], t_in["bias"].broadcast_to([P, 5 * D])).then_inc(s["i_bias"], 16)
            sp.dma_start(gam[:, :, :], t_in["gam"]).then_inc(s["i_gam"], 16)
            load("w1")
            for name in WEIGHTS:
                if name != "w1":
                    load(name)
            load_ctx(0)
            sp.wait_ge(s["i_xn"], 1)
            sp.wait_ge(s["i_sps"], 1)
            load_x(0)
            load_x(1)
            load_ctx(1)
            with sp.Fori(1, B - 1) as b:
                load_x(b + 1)
                load_ctx(b + 1)
                store(b - 1)
            store(B - 2)
            store(B - 1)
            sp.wait_ge(s["out"], 16 * (B + 1))


def kernel(**inputs):
    import numpy as _np
    import concourse.bacc as _bacc
    from concourse import mybir as _mybir
    from concourse.bass_utils import run_bass_kernel_spmd as _run

    a = {n: _np.asarray(v) for n, v in inputs.items()}
    sa, xa, ff = "L0_attn_", "L0_xattn_", "L0_ffn_"

    def twice(w, axis):
        shape = w.shape[:axis] + (H, HD) + w.shape[axis + 1:]
        w = w.reshape(shape)
        return _np.concatenate([w, w], axis=axis + 1).reshape(w.shape[:axis] + (2 * H * HD,) + w.shape[axis + 2:])

    def on_partitions(w):
        return w.reshape(-1, P, w.shape[-1]).transpose(1, 0, 2)

    def by_group(v):
        return twice(v, 0).reshape(G, P).T

    rows = _np.arange(P)
    consts = _np.zeros((P, P + NCOLS), _np.float32)
    consts[:, :P] = _np.eye(P, dtype=_np.float32)
    for r in range(R):
        consts[32 * r:32 * r + 32, P + BM + r] = 1.0
    consts[rows % 32 >= HD, P + NMASK] = -1.0
    consts[:, P + EXPO:P + EXPO + 5] = _np.array([-0.5, -0.5, 0.5, 0.5, -1.0], _np.float32)
    consts[:, P + BQ:P + BQ + G] = by_group(a[sa + "bq"])
    consts[:, P + BK:P + BK + G] = by_group(a[sa + "bk"])
    consts[:, P + BQ2:P + BQ2 + G] = by_group(a[xa + "bq"])
    host = {
        "x": a["x"],
        "ctxT": a["ctx_1024"].transpose(0, 2, 1),
        "mask": a["mask_Bx1x1xS2_if1"].reshape(B, CTX),
        "consts": consts,
        "bias": _np.concatenate([a[sa + "bv"], a[sa + "bo"], a[xa + "bk"], a[xa + "bv"], a[xa + "bo"]])[None, :],
        "gam": _np.stack([a[ff + "gamma_x"], a[ff + "gamma_slot"]]).reshape(2, ND, P).transpose(2, 0, 1),
        "se": a[ff + "slot_embeds"].reshape(SLOTS, D),
        "wqk": on_partitions(_np.concatenate([twice(a[sa + "Wq"].T, 1), twice(a[sa + "Wk"].T, 1)], axis=1)),
        "wv": on_partitions(a[sa + "Wv"].T),
        "wo": on_partitions(twice(a[sa + "Wo"].T, 0)),
        "wkv2": on_partitions(_np.concatenate([a[xa + "Wk"].T, a[xa + "Wv"].T], axis=1)),
        "wq2": on_partitions(twice(a[xa + "Wq"].T, 1)),
        "wo2": on_partitions(twice(a[xa + "Wo"].T, 0)),
        "w1": on_partitions(a[ff + "w1"]),
        "w2": on_partitions(a[ff + "w2"]),
    }
    nc = _bacc.Bacc("TRN2", target_bir_lowering=False, num_devices=1)
    arrays, t_in = {}, {}
    for name, v in host.items():
        v = _np.ascontiguousarray(v)
        arrays["in_" + name] = v
        t_in[name] = nc.dram_tensor("in_" + name, v.shape, _mybir.dt.from_np(v.dtype), kind="ExternalInput").ap()
    out = nc.dram_tensor("out_0", (B, S, D), _mybir.dt.float32, kind="ExternalOutput").ap()
    decoder_layer(nc, t_in, out)
    r = _run(nc, [arrays], core_ids=[0])
    return r.results[0]["out_0"]
```

```python
import concourse.bass as bass
from concourse import mybir
from concourse.alu_op_type import AluOpType as ALU
from contextlib import ExitStack
import numpy as np

B, S, D = 16, 256, 256
H, HD = 16, 16
CTX = 77
E, TS, HID = 8, 128, 1024
SLOTS = E * TS
P = 128
NT = S // P
ND = D // P
G, R = 4, 4
PADW = 160
CHUNK = 256
NC = SLOTS // CHUNK
NM = HID // P
NS = SLOTS // P
LN_EPS, RMS_EPS = 1e-5, 1e-12
BM, NMASK, EXPO, BQ, BK, BQ2, NCOLS = 0, 4, 5, 10, 14, 18, 22
ATTN_SCALE, XATTN_SCALE = 1.0 / 16.0, 1.0 / 4.0

PER = dict(
    x_in=16, ctx_in=16, mask_in=16, out=16,
    ln1_st=1, ln1_mv=1, ln1_ve=1, ln1_pw=1, ln1_xh=1, xt1_ps=1, xt1_hi=1, xt1_lo=1,
    ln2_st=1, ln2_mv=1, ln2_ve=1, ln2_pw=1, ln2_xh=1, xt2_ps=1, xt2_hi=1, xt2_lo=1,
    ln3_st=1, ln3_mv=1, ln3_ve=1, ln3_pw=1, ln3_sc=4, ln3_xh=1, xt3_ps=1, xt3_hi=1, xt3_lo=1,
    x_bo=1, v_ps=1, v_sb=1, vg_hi=16, vg_lo=16, qk_ps=4, qk_sb=4, qk_hi=4, qk_lo=4,
    s_ps=16, mx=16, ex=16, rl=16, pn=16, t_ps=16, pt_hi=16, pt_lo=16, pv=16, ot_hi=4, ot_lo=4,
    o_ps=1, x1=1, x1_bo=1, ct_hi=1, ct_lo=1, kv_ps=1, kd_sb=1, v2_sb=1, k2t_ps=1, k2_n=1, mk=2,
    k2_f=4, k2_hi=4, k2_lo=4, vg2_hi=4, vg2_lo=4, q2_ps=4, q2_sb=4, q2_hi=4, q2_a=4,
    s2_ps=4, s2_sb=4, mx2=4, sh2=4, ex2=4, sm2=4, rl2=4, pn2=4,
    t2_ps=8, pt2_hi=8, pt2_lo=8, pv2=8, ot2_hi=4, ot2_lo=4,
    o2_ps=1, x2=1, xs_hi=1, xs_lo=1, lg_ps=4, lg_sb=4,
    res=1, rm=2, lt_ps=4, cm=4, ed=4, rc=4, edn=4, ds_ps=4, ds_hi=4, ds_lo=4, sl_ps=4, sl_hi=4, sl_lo=4,
    ec=4, cb_ps=4, cb_hi=4, cb_lo=4, h_ps=16, ge=16, h_hi=16, h_lo=16, pr_ps=4, pr_hi=4, pr_lo=4,
    d_ps=4, acc=4, rs_sum=1, rr=1, y=1,
)

WEIGHTS = ("wqk", "wv", "wo", "wkv2", "wq2", "wo2", "w1", "w2")

ORDER = dict(
    pe="""
        m.lt.0 c.xt.1 l.outer.3.0 c.v c.qk.0 m.dispatch.0 l.outer.3.1 c.scores.0 c.scores.1 m.slots.0 l.comb.3 c.qk.1
        c.transp.0 c.scores.2 m.hidden.0.0 m.hidden.0.1 c.transp.1 c.scores.3 m.hidden.0.2 m.hidden.0.3 c.pv.0 m.lt.1
        c.transp.2 c.scores.4 l.combine.3 c.pv.1 c.scores.5 c.qk.2 c.transp.3 m.outer.0.0 c.transp.4 c.pv.2
        m.dispatch.1 c.scores.6 c.scores.7 c.pv.3 c.transp.5 m.outer.0.1 c.scores.8 c.scores.9 c.transp.6 c.pv.4
        c.pv.5 c.transp.7 m.slots.1 m.comb.0 c.qk.3 c.scores.10 c.transp.8 c.pv.6 c.pv.7 c.scores.11 c.transp.9
        m.hidden.1.0 m.hidden.1.1 c.transp.10 c.pv.8 c.scores.12 m.hidden.1.2 c.scores.13 c.transp.11 c.pv.9 c.pv.10
        m.lt.2 m.hidden.1.3 c.scores.14 c.scores.15 c.transp.12 m.combine.0 c.transp.13 c.pv.11 c.kv c.transp.14
        c.pv.12 c.pv.13 c.transp.15 m.dispatch.2 c.pv.14 c.pv.15 m.comb.1 c.k2t c.oproj m.slots.2 m.outer.1.0 c.xt.2
        m.outer.1.1 c.q2.0 m.hidden.2.0 c.s2.0 m.hidden.2.1 m.hidden.2.2 c.q2.1 m.lt.3 m.hidden.2.3 c.s2.1 m.combine.1
        c.t2.0.0 c.t2.0.1 c.q2.2 m.dispatch.3 c.s2.2 c.pv2.0.0 c.t2.1.0 c.t2.1.1 c.pv2.0.1 c.q2.3 c.pv2.1.0 c.pv2.1.1
        c.s2.3 m.outer.2.0 c.t2.2.0 c.t2.2.1 m.outer.2.1 c.pv2.2.0 c.pv2.2.1 c.t2.3.0 c.t2.3.1 m.slots.3 c.pv2.3.0
        c.pv2.3.1 m.comb.2 c.oproj2 m.hidden.3.0 m.hidden.3.1 m.combine.2 m.hidden.3.2 c.xt.3 m.hidden.3.3 c.logits.0
        c.logits.1 c.logits.2 c.logits.3
    """,
    act="""
        c.xt.1 m.ed.0 c.qk.0 m.ds.0 c.ex.0 m.sl.0 l.cb.3 c.ex.1 c.qk.1 l.pr.3 c.ex.2 m.ge.0.0 m.ge.0.1 c.pt.0 c.pt.1
        m.ge.0.2 m.ge.0.3 c.ex.3 c.ex.4 c.pt.2 c.qk.2 m.ed.1 c.ex.5 c.pt.3 m.ds.1 c.pt.4 c.ex.6 c.ot.0 c.ex.7 c.pt.5
        m.ec.0 c.ex.8 c.pt.6 c.ex.9 c.pt.7 m.sl.1 m.cb.0 c.qk.3 c.ex.10 c.pt.8 c.ot.1 c.ex.11 m.ge.1.0 m.ge.1.1 c.pt.9
        c.pt.10 m.pr.0 m.ge.1.2 c.ex.12 c.ex.13 c.pt.11 m.ed.2 c.ex.14 c.pt.12 c.ex.15 c.ot.2 c.pt.13 m.ec.1 c.pt.14
        c.pt.15 m.ds.2 c.ot.3 m.ge.1.3 m.cb.1 m.ec.2 c.xt.2 m.sl.2 c.q2.0 m.ge.2.0 m.ge.2.1 m.pr.1 m.ge.2.2 c.q2.1
        c.ex2.0 m.ed.3 c.ex2.1 c.q2.2 c.t2.0.0 c.t2.0.1 m.ge.2.3 c.t2.1.0 c.t2.1.1 c.ot2.0 c.q2.3 c.ex2.2 c.ot2.1
        c.ex2.3 c.t2.2.0 c.t2.2.1 m.ds.3 c.ot2.2 c.t2.3.0 c.t2.3.1 m.sl.3 c.ot2.3 m.cb.2 m.pr.2 m.ge.3.0 m.ge.3.1
        c.xt.3 m.ge.3.2 m.ge.3.3 m.ec.3 c.logits.0 c.logits.1 c.logits.2 c.logits.3
    """,
    dve="""
        c.stats.1 c.mask c.xh.1 m.row_max c.xt.1 m.cm.0 m.edn.0 c.v c.qk.0 m.ds.0 c.mx.0 c.mx.1 c.rl.0 m.sl.0 l.cb.3
        c.rl.1 c.mx.2 c.qk.1 c.rl.2 c.mx.3 m.hid.0.0 m.hid.0.1 c.pt.0 c.pt.1 m.hid.0.2 l.pr.3 m.hid.0.3 m.cm.1 c.mx.4
        c.rl.3 c.mx.5 l.acc.3 l.finish c.rl.4 c.pt.2 m.edn.1 c.rl.5 c.pt.3 c.qk.2 m.ds.1 c.mx.6 c.mx.7 c.pt.4 c.rl.6
        c.rl.7 c.ot.0 c.pt.5 c.mx.8 c.mx.9 c.rl.8 c.rl.9 c.pt.6 m.sl.1 c.pt.7 c.mx.10 m.cb.0 c.mx.11 c.pt.8 c.rl.10
        c.rl.11 c.ot.1 c.qk.3 c.pt.9 c.mx.12 c.pt.10 c.mx.13 m.keep m.hid.1.0 m.pr.0 c.rl.12 m.hid.1.1 m.cm.2 c.rl.13
        c.mx.14 c.pt.11 c.mx.15 c.rl.14 m.edn.2 c.pt.12 c.rl.15 c.ot.2 c.pt.13 c.kv c.pt.14 c.pt.15 m.ds.2 m.acc.0
        c.ot.3 m.hid.1.2 m.hid.1.3 c.k2t c.x1 c.stats.2 c.xh.2 m.cb.1 c.xt.2 m.sl.2 c.q2.0 c.s2.0 m.pr.1 m.hid.2.0
        m.hid.2.1 m.hid.2.2 m.cm.3 c.q2.1 c.n2.0 c.s2.1 m.edn.3 c.n2.1 c.q2.2 c.t2.0.0 c.t2.0.1 c.s2.2 c.t2.1.0
        c.ot2.0 c.t2.1.1 m.hid.2.3 c.q2.3 m.acc.1 c.n2.2 c.s2.3 c.ot2.1 c.n2.3 c.t2.2.0 c.t2.2.1 m.ds.3 c.ot2.2
        c.t2.3.0 c.t2.3.1 c.ot2.3 m.cb.2 m.sl.3 m.pr.2 c.x2 c.stats.3 c.xh.3 m.hid.3.0 m.hid.3.1 c.xt.3 m.hid.3.2
        m.hid.3.3 c.xs m.acc.2
    """,
    pool="""
        c.context c.rstd.1 c.vg.0 c.pn.0 c.vg.1 c.vg.2 c.pn.1 c.pn.2 m.hid.0.0 m.hid.0.1 c.vg.3 m.hid.0.2 m.hid.0.3
        c.pn.3 c.pn.4 c.pn.5 c.vg.4 c.vg.5 c.vg.6 c.pn.6 c.pn.7 c.pn.8 c.vg.7 c.vg.8 c.pn.9 c.pn.10 c.pn.11 c.vg.9
        c.vg.10 c.vg.11 c.vg.12 c.vg.13 c.vg.14 c.pn.12 c.pn.13 c.pn.14 c.vg.15 c.pn.15 m.hid.1.0 m.hid.1.1 c.v2.0
        c.bias.1 m.hid.1.2 m.hid.1.3 c.rstd.2 c.k2.0 c.k2.1 m.hid.2.0 m.hid.2.1 m.hid.2.2 c.nm.0 c.k2.2 c.nm.1 c.k2.3
        c.v2.1 m.hid.2.3 c.nm.2 c.v2.2 c.nm.3 c.v2.3 c.bias.2 c.rstd.3 m.hid.3.0 m.hid.3.1 m.hid.3.2 m.hid.3.3
    """,
)


RING = [("v", 0), ("qk", 0)]
for _h in range(H):
    RING.append(("head", _h))
    if _h % R == 1 and _h // R + 1 < G:
        RING.append(("qk", _h // R + 1))
RING += [("kv", 0), ("k2t", 0)]


def ring_bank(name, k=0):
    return 1 + RING.index((name, k)) % 2


def run(engine, steps, a=None, b=None, late=None):
    batches = dict(c=a, m=b, l=late)
    for entry in ORDER[engine].split():
        kind, name, *k = entry.split(".")
        if batches[kind] is not None:
            steps[name](batches[kind], *(int(i) for i in k))


def decoder_layer(nc, t_in, out):
    f32, f32r, i32 = mybir.dt.float32, mybir.dt.float32r, mybir.dt.int32
    ACT = mybir.ActivationFunctionType
    AX = mybir.AxisListType.X
    KB = 1024

    ctx = ExitStack()
    with ctx:
        base = [nc.sbuf_base + (-nc.sbuf_base) % 64]
        end = nc.sbuf_usable_end

        def region(nbytes):
            at = base[0]
            base[0] = at + nbytes + (-nbytes) % 32
            assert base[0] <= end, (base[0], end)
            return at

        def at(name, shape, dt, offset):
            return nc.alloc_sbuf_tensor_at(name, shape, dt, offset=offset)

        def sb(name, shape, dt=f32):
            return at(name, shape, dt, region(4 * int(np.prod(shape[1:]))))

        def pair(name, shape):
            return sb(name + "_hi", shape, f32r), sb(name + "_lo", shape, f32r)

        W = dict(
            wqk=pair("wqk", [P, ND, 2 * 512]), wv=pair("wv", [P, ND, D]), wo=pair("wo", [P, G, D]),
            wkv2=pair("wkv2", [P, ND, 2 * D]), wq2=pair("wq2", [P, ND, 512]), wo2=pair("wo2", [P, G, D]),
            w1=pair("w1", [P, ND, HID]), w2=pair("w2", [P, NM, D]), se=pair("se", [P, ND, SLOTS]),
        )
        r_lg = region(8 * KB)
        lg = at("lg", [P, NT, SLOTS], f32, r_lg)
        r_exp = region(4 * KB)
        edt = at("edt", [P, 2, S], f32, r_exp)
        ecomb = at("ecomb", [P, NT, CHUNK], f32, r_exp + 2 * KB)
        xs_hi, xs_lo = pair("xs", [P, NT, D])
        r_dc = region(4 * KB)
        ds_hi = at("ds_hi", [P, NT, CHUNK], f32r, r_dc)
        ds_lo = at("ds_lo", [P, NT, CHUNK], f32r, r_dc + 2 * KB)
        cb_hi = at("cb_hi", [P, 2, S], f32r, r_dc)
        cb_lo = at("cb_lo", [P, 2, S], f32r, r_dc + 2 * KB)
        sl_hi, sl_lo = pair("sl", [P, ND, CHUNK])
        r_hid = region(16 * KB)
        h_hi = at("h_hi", [P, NM, CHUNK], f32r, r_hid)
        h_lo = at("h_lo", [P, NM, CHUNK], f32r, r_hid + 8 * KB)
        h_f = at("h_f", [P, NM, CHUNK], f32, r_hid + 8 * KB)
        pr_hi, pr_lo = pair("pr", [P, 2, D])
        r_acc = region(2 * KB)
        acc = at("acc", [P, NT, D], f32, r_acc)
        res = sb("res", [P, NT, D])
        x = sb("x", [P, NT, D])
        x2 = sb("x2", [P, NT, D])
        xt_hi, xt_lo = pair("xt", [P, ND, S])
        r_qk = region(4 * KB)
        r_s2 = region(2 * NT * 4 * R * CTX)
        qk_f = [at(f"qk_f{i}", [P, 2, S], f32, r) for i, r in enumerate((r_qk, r_s2))]
        qk_l = [at(f"qk_l{i}", [P, 2, S], f32r, r) for i, r in enumerate((r_qk, r_s2))]
        qk_h = [at(f"qk_h{i}", [P, 2, S], f32r, r + 2 * KB) for i, r in enumerate((r_qk, r_s2))]
        q2_f = at("q2_f", [P, 2, S], f32, r_qk)
        q2_a = at("q2_a", [P, 2, S], f32r, r_qk)
        r_v = region(2 * KB)
        v_f = at("v_f", [P, NT, D], f32, r_v)
        k2d = at("k2d", [CTX, H, 2, HD], f32, r_v)
        vg = sb("vg", [P, NT, R, PADW], f32r)
        r_p = region(4 * KB)
        p_sb = at("p_sb", [P, 2, NT, S], f32, r_p)
        x1 = at("x1", [P, NT, D], f32, r_p)
        xh = at("xh", [P, NT, D], f32, r_p + 2 * KB)
        r_pt = region(8 * KB)
        pt_hi = at("pt_hi", [P, 2, NT, S], f32r, r_pt)
        pt_lo = at("pt_lo", [P, 2, NT, S], f32r, r_pt + 4 * KB)
        pt2_hi = at("pt2_hi", [CTX, 2, 2, S], f32r, r_pt)
        pt2_lo = at("pt2_lo", [CTX, 2, 2, S], f32r, r_pt + 4 * KB)
        r_ot = region(8 * KB)
        ot_hi = at("ot_hi", [P, G, S], f32r, r_ot)
        ot_lo = at("ot_lo", [P, G, S], f32r, r_ot + 4 * KB)
        s2 = at("s2", [P, 2, NT, R * CTX], f32, r_s2)
        v2_f = sb("v2_f", [CTX, D])
        k2_n = sb("k2_n", [P, G, CTX])
        r_k2 = region(4 * R * CTX)
        k2_f = at("k2_f", [P, R, CTX], f32, r_k2)
        k2_lo = at("k2_lo", [P, R * CTX], f32r, r_k2)
        k2_hi = sb("k2_hi", [P, R * CTX], f32r)
        r_cx = region(4 * ND * CTX)
        cx = at("cx", [P, ND, CTX], f32, r_cx)
        cx_lo = at("cx_lo", [P, ND, CTX], f32r, r_cx)
        cx_hi = sb("cx_hi", [P, ND, CTX], f32r)
        mk_i = sb("mk_i", [P, CTX], i32)
        mk_f = sb("mk_f", [P, CTX])
        consts = sb("consts", [P, P + NCOLS])
        ident = consts[:, 0:P]
        cols = consts[:, P:P + NCOLS]
        biases = sb("biases", [P, 5 * D])
        bv, bo, bo2 = (biases[:, i * D:(i + 1) * D] for i in (0, 1, 4))
        bkv2 = biases[0:CTX, 2 * D:4 * D]
        st = sb("st", [P, NT, 6])
        mv = sb("mv", [P, NT, 2])
        ve = sb("ve", [P, 2, NT])
        pw = sb("pw", [P, 2, NT])
        sc3 = sb("sc3", [P, 4, NT])
        mx = sb("mx", [P, H, NT])
        ls = sb("ls", [P, H, NT])
        rl = sb("rl", [P, H, NT])
        mx2 = sb("mx2", [P, G, NT, R])
        ls2 = sb("ls2", [P, G, NT, R])
        rl2 = sb("rl2", [P, G, NT, R])
        rm = sb("rm", [P, NT])
        rsum = sb("rsum", [P, NT, NC])
        rtot = sb("rtot", [P, NT])
        rrec = sb("rrec", [P, NT])
        cm = sb("cm", [P, NS])
        csum = sb("csum", [P, NS])
        crec = sb("crec", [P, NS])
        gam = sb("gam", [P, 2, ND])
        gxs = sb("gxs", [P, ND])
        stage = dict(
            wqk=at("g_wqk", [P, ND, 1024], f32, r_lg), w1=at("g_w1", [P, ND, HID], f32, r_hid),
            w2=at("g_w2", [P, NM, D], f32, r_hid + 8 * KB), wo2=at("g_wo2", [P, G, D], f32, r_ot),
            wq2=at("g_wq2", [P, ND, 512], f32, r_ot + 4 * KB), wv=at("g_wv", [P, ND, D], f32, r_exp),
            wo=at("g_wo", [P, G, D], f32, r_dc), wkv2=at("g_wkv2", [P, ND, 512], f32, r_p),
        )
        g_se = at("g_se", [P, NS, D], f32, r_acc)
        se_t = at("se_t", [P, ND, SLOTS], f32, r_pt)
        se_sq = at("se_sq", [P, NS, D], f32, r_pt)
        se_ss, se_n, se_i, se_sc = (sb(n, [P, NS]) for n in ("se_ss", "se_n", "se_i", "se_sc"))
        ps = ctx.enter_context(nc.psum_tensor("ps", [P, 8, 512], f32))

        s = {n: ctx.enter_context(nc.semaphore("s_" + n)) for n in PER}
        for n in ("i_const", "i_bias", "pool_held", "dve_held", "i_cols", "i_vz", "i_se", "i_gam", "i_gxs", "i_hi",
                  "i_lo", "i_w1g", "i_st", "i_sq", "i_sr", "i_xn", "i_sps", "i_sg", "i_shi", "i_slo"):
            s[n] = ctx.enter_context(nc.semaphore("s_" + n))
        for n in WEIGHTS:
            s["i_" + n] = ctx.enter_context(nc.semaphore("s_i_" + n))

        def nth(name, b, k):
            return b * PER[name] + k

        def later(b):
            return not isinstance(b, int) or b > 0

        def more(b):
            return not isinstance(b, int) or b < B - 1

        block = ctx.enter_context(nc.Block())

        @block.tensor
        def _(pe):
            te = nc.tensor
            full = slice(None)
            XT, OT, SL, CB, DS = (xt_hi, xt_lo), (ot_hi, ot_lo), (sl_hi, sl_lo), (cb_hi, cb_lo), (ds_hi, ds_lo)
            HH, PR, XS, CX = (h_hi, h_lo), (pr_hi, pr_lo), (xs_hi, xs_lo), (cx_hi, cx_lo)

            def three(o, lhs, rhs, first, last):
                te.matmul(o, lhs[0], rhs[0], start=first, stop=False)
                te.matmul(o, lhs[1], rhs[0], start=False, stop=False)
                return te.matmul(o, lhs[0], rhs[1], start=False, stop=last)

            def both(t, *ix):
                return tuple(u.__getitem__(ix) for u in t)

            def ring_free(a, name, k=0):
                at = RING.index((name, k))
                if at < 2:
                    return
                before, n = RING[at - 2]
                signal = dict(v="v_sb", qk="qk_sb", head="ex", kv="v2_sb")[before]
                pe.wait_ge(s[signal], nth(signal, a, n + 1))

            def xt(a, n):
                pe.wait_ge(s[f"ln{n}_xh"], nth(f"ln{n}_xh", a, 1))
                bank = 0 if n == 1 else 1
                if n == 1 and later(a):
                    pe.wait_ge(s["lg_sb"], nth("lg_sb", a - 1, 4))
                if n == 2:
                    pe.wait_ge(s["k2_n"], nth("k2_n", a, 1))
                if n == 3:
                    pe.wait_ge(s["s2_sb"], nth("s2_sb", a, G))
                for dk in range(ND):
                    for t in range(NT):
                        last = te.transpose(ps[:, bank, dk * S + t * P:dk * S + (t + 1) * P],
                                            xh[:, t, dk * P:(dk + 1) * P], ident[:, :])
                last.then_inc(s[f"xt{n}_ps"], 1)

            def v(a):
                pe.wait_ge(s["xt1_lo"], nth("xt1_lo", a, 1))
                for t in range(NT):
                    for dk in range(ND):
                        last = three(ps[:, ring_bank("v"), t * D:(t + 1) * D], both(XT, full, dk, slice(t * P, t * P + P)),
                                     both(W["wv"], full, dk), dk == 0, dk == ND - 1)
                last.then_inc(s["v_ps"], 1)

            def qk(a, g):
                pe.wait_ge(s["xt1_lo"], nth("xt1_lo", a, 1))
                if g == 0 and later(a):
                    pe.wait_ge(s["lg_sb"], nth("lg_sb", a - 1, 1))
                ring_free(a, "qk", g)
                for i in range(2):
                    for dk in range(ND):
                        c0 = i * 512 + g * P
                        last = three(ps[:, ring_bank("qk", g), i * S:(i + 1) * S],
                                     both(W["wqk"], full, dk, slice(c0, c0 + P)),
                                     both(XT, full, dk), dk == 0, dk == ND - 1)
                last.then_inc(s["qk_ps"], 1)

            def scores(a, h):
                g, r = divmod(h, R)
                rows = slice(32 * r, 32 * r + 32)
                pe.wait_ge(s["qk_lo"], nth("qk_lo", a, g + 1))
                ring_free(a, "head", h)
                for t in range(NT):
                    for k, keys in enumerate((qk_h, qk_l)):
                        last = te.matmul(ps[:, ring_bank("head", h), t * S:(t + 1) * S],
                                         qk_l[g % 2][rows, 0, t * P:(t + 1) * P],
                                         keys[g % 2][rows, 1, :], start=k == 0, stop=k == 1)
                last.then_inc(s["s_ps"], 1)

            def transp(a, h):
                pe.wait_ge(s["pn"], nth("pn", a, h + 1))
                if h >= 2:
                    pe.wait_ge(s["pt_lo"], nth("pt_lo", a, h - 1))
                for j in range(NT):
                    for t in range(NT):
                        last = te.transpose(ps[:, 3 + h % 2, j * S + t * P:j * S + (t + 1) * P],
                                            p_sb[:, h % 2, t, j * P:(j + 1) * P], ident[:, :])
                last.then_inc(s["t_ps"], 1)

            def pv(a, h):
                g, r = divmod(h, R)
                pe.wait_ge(s["pt_lo"], nth("pt_lo", a, h + 1))
                pe.wait_ge(s["vg_lo"], nth("vg_lo", a, h + 1))
                if r == 0:
                    if g:
                        pe.wait_ge(s["ot_lo"], nth("ot_lo", a, g))
                for j in range(NT):
                    w = vg[:, j, :, :].rearrange("p r w -> p (r w)")[:, r * P:(r + 1) * P]
                    for k, pt in enumerate((pt_hi, pt_lo)):
                        last = te.matmul(ps[:, 0, 0:S], w, pt[:, h % 2, j, :], start=r == 0 and j == 0 and k == 0,
                                         stop=r == R - 1 and j == NT - 1 and k == 1)
                last.then_inc(s["pv"], 1)

            def project(a, w, signal):
                for t in range(NT):
                    for g in range(G):
                        last = three(ps[:, 0, t * D:(t + 1) * D], both(OT, full, g, slice(t * P, t * P + P)),
                                     both(W[w], full, g), g == 0, g == G - 1)
                last.then_inc(s[signal], 1)

            def oproj(a):
                pe.wait_ge(s["ot_lo"], nth("ot_lo", a, G))
                project(a, "wo", "o_ps")

            def kv(a):
                pe.wait_ge(s["ct_lo"], nth("ct_lo", a, 1))
                ring_free(a, "kv")
                for dk in range(ND):
                    last = three(ps[0:CTX, ring_bank("kv"), :], both(CX, full, dk), both(W["wkv2"], full, dk), dk == 0, dk == ND - 1)
                last.then_inc(s["kv_ps"], 1)

            def k2t(a):
                pe.wait_ge(s["kd_sb"], nth("kd_sb", a, 1))
                ring_free(a, "k2t")
                for g in range(G):
                    kd = k2d[:, :, :, :].rearrange("p h e d -> p (h e d)")[:, g * P:(g + 1) * P]
                    last = te.transpose(ps[:, ring_bank("k2t"), g * CTX:(g + 1) * CTX], kd, ident[0:CTX, 0:CTX])
                last.then_inc(s["k2t_ps"], 1)

            def q2(a, g):
                if g:
                    pe.wait_ge(s["s2_sb"], nth("s2_sb", a, g))
                else:
                    pe.wait_ge(s["xt2_lo"], nth("xt2_lo", a, 1))
                    pe.wait_ge(s["x1"], nth("x1", a, 1))
                for dk in range(ND):
                    last = three(ps[:, 0, 0:S], both(W["wq2"], full, dk, slice(g * P, g * P + P)), both(XT, full, dk),
                                 dk == 0, dk == ND - 1)
                last.then_inc(s["q2_ps"], 1)

            def s2_step(a, g):
                pe.wait_ge(s["q2_a"], nth("q2_a", a, g + 1))
                pe.wait_ge(s["k2_lo"], nth("k2_lo", a, g + 1))
                if g:
                    pe.wait_ge(s["s2_sb"], nth("s2_sb", a, g))
                for t in range(NT):
                    for k, keys in enumerate((k2_hi, k2_lo)):
                        last = te.matmul(ps[:, t, 0:R * CTX], q2_a[:, g % 2, t * P:(t + 1) * P], keys[:, :],
                                         start=k == 0, stop=k == 1)
                last.then_inc(s["s2_ps"], 1)

            def t2(a, g, u):
                n = 2 * g + u
                pe.wait_ge(s["pn2"], nth("pn2", a, g + 1))
                if n >= 2:
                    pe.wait_ge(s["pt2_lo"], nth("pt2_lo", a, n - 1))
                else:
                    pe.wait_ge(s["pt_lo"], nth("pt_lo", a, H))
                for i in range(2):
                    for t in range(NT):
                        r = 2 * u + i
                        last = te.transpose(ps[0:CTX, 3 + u, i * S + t * P:i * S + (t + 1) * P],
                                            s2[:, g % 2, t, r * CTX:(r + 1) * CTX], ident[:, :])
                last.then_inc(s["t2_ps"], 1)

            def pv2(a, g, u):
                n = 2 * g + u
                pe.wait_ge(s["pt2_lo"], nth("pt2_lo", a, n + 1))
                if u == 0:
                    pe.wait_ge(s["vg2_lo"], nth("vg2_lo", a, g + 1))
                    if g:
                        pe.wait_ge(s["ot2_lo"], nth("ot2_lo", a, g))
                    else:
                        pe.wait_ge(s["v2_sb"], nth("v2_sb", a, 1))
                for i in range(2):
                    r = 2 * u + i
                    w = vg[0:CTX, g % 2, :, :].rearrange("p r w -> p (r w)")[:, r * P:(r + 1) * P]
                    for k, pt in enumerate((pt2_hi, pt2_lo)):
                        last = te.matmul(ps[:, 2, 0:S], w, pt[:, u, i, :], start=r == 0 and k == 0,
                                         stop=r == R - 1 and k == 1)
                last.then_inc(s["pv2"], 1)

            def oproj2(a):
                pe.wait_ge(s["ot2_lo"], nth("ot2_lo", a, G))
                pe.wait_ge(s["s2_sb"], nth("s2_sb", a, G))
                project(a, "wo2", "o2_ps")

            def logits(a, k):
                if k == 0:
                    pe.wait_ge(s["xt3_lo"], nth("xt3_lo", a, 1))
                if k == 3:
                    pe.wait_ge(s["x2"], nth("x2", a, 1))
                t, u = divmod(k, 2)
                for dk in range(ND):
                    last = three(ps[:, (2, 3, 4, 0)[k], :], both(XT, full, dk, slice(t * P, t * P + P)),
                                 both(W["se"], full, dk, slice(u * 512, u * 512 + 512)), dk == 0, dk == ND - 1)
                last.then_inc(s["lg_ps"], 1)

            def lt(b, c):
                if c == 0:
                    pe.wait_ge(s["lg_sb"], nth("lg_sb", b, 4))
                    if later(b):
                        pe.wait_ge(s["ge"], nth("ge", b - 1, 15))
                else:
                    pe.wait_ge(s["ge"], nth("ge", b, 4 * c - 1))
                for e in range(2):
                    for t in range(NT):
                        last = te.transpose(ps[:, 6, e * S + t * P:e * S + (t + 1) * P],
                                            lg[:, t, c * CHUNK + e * P:c * CHUNK + (e + 1) * P], ident[:, :])
                last.then_inc(s["lt_ps"], 1)

            def dispatch(b, c):
                pe.wait_ge(s["edn"], nth("edn", b, c + 1))
                for t in range(NT):
                    for e in range(2):
                        last = te.transpose(ps[:, 6, t * CHUNK + e * P:t * CHUNK + (e + 1) * P],
                                            edt[:, e, t * P:(t + 1) * P], ident[:, :])
                last.then_inc(s["ds_ps"], 1)

            def slots(b, c):
                pe.wait_ge(s["ds_lo"], nth("ds_lo", b, c + 1))
                if c:
                    pe.wait_ge(s["ge"], nth("ge", b, 4 * c))
                else:
                    pe.wait_ge(s["xs_lo"], nth("xs_lo", b, 1))
                    if later(b):
                        pe.wait_ge(s["ge"], nth("ge", b - 1, 16))
                for dk in range(ND):
                    for t in range(NT):
                        last = three(ps[:, 5, dk * CHUNK:(dk + 1) * CHUNK], both(XS, full, t, slice(dk * P, dk * P + P)),
                                     both(DS, full, t), t == 0, t == NT - 1)
                last.then_inc(s["sl_ps"], 1)

            def hidden(b, c, q):
                n = c * 4 + q
                if q == 0:
                    pe.wait_ge(s["sl_lo"], nth("sl_lo", b, c + 1))
                    if c or later(b):
                        pe.wait_ge(s["cb_lo"], nth("cb_lo", b, c))
                if q >= 2:
                    pe.wait_ge(s["ge"], nth("ge", b, n - 1))
                for i in range(2):
                    m = 2 * q + i
                    for dk in range(ND):
                        last = three(ps[:, 6 - q % 2, i * CHUNK:(i + 1) * CHUNK],
                                     both(W["w1"], full, dk, slice(m * P, m * P + P)), both(SL, full, dk),
                                     dk == 0, dk == ND - 1)
                last.then_inc(s["h_ps"], 1)

            def outer(b, c, e):
                if e == 0:
                    pe.wait_ge(s["h_lo"], nth("h_lo", b, 4 * c + 4))
                    if c or later(b):
                        pe.wait_ge(s["acc"], nth("acc", b, c))
                for k in range(NM):
                    last = three(ps[:, 7, e * D:(e + 1) * D], both(HH, full, k, slice(e * P, e * P + P)),
                                 both(W["w2"], full, k), k == 0, k == NM - 1)
                if e == 1:
                    last.then_inc(s["pr_ps"], 1)

            def comb(b, c):
                pe.wait_ge(s["ec"], nth("ec", b, c + 1))
                if c < NC - 1 or more(b):
                    pe.wait_ge(s["ds_lo"], nth("ds_lo", b, c + 2))
                else:
                    pe.wait_ge(s["ge"], nth("ge", b, 16))
                for e in range(2):
                    for t in range(NT):
                        last = te.transpose(ps[:, 6, e * S + t * P:e * S + (t + 1) * P],
                                            ecomb[:, t, e * P:(e + 1) * P], ident[:, :])
                last.then_inc(s["cb_ps"], 1)

            def combine(b, c):
                pe.wait_ge(s["pr_lo"], nth("pr_lo", b, c + 1))
                pe.wait_ge(s["cb_lo"], nth("cb_lo", b, c + 1))
                for t in range(NT):
                    for e in range(2):
                        last = three(ps[:, 7, t * D:(t + 1) * D], both(CB, full, e, slice(t * P, t * P + P)),
                                     both(PR, full, e), e == 0, e == 1)
                last.then_inc(s["d_ps"], 1)

            pe.wait_ge(s["i_const"], 16)
            pe.wait_ge(s["i_xn"], 1)
            for dk in range(ND):
                for e in range(NS):
                    last = te.transpose(ps[:, 2 * dk + e // 4, (e % 4) * P:(e % 4 + 1) * P],
                                        g_se[:, e, dk * P:(dk + 1) * P], ident[:, :])
            last.then_inc(s["i_sps"], 1)
            pe.wait_ge(s["i_slo"], 1)
            pe.wait_ge(s["i_lo"], len(WEIGHTS))

            steps = dict(xt=xt, v=v, qk=qk, scores=scores, transp=transp, pv=pv, oproj=oproj, kv=kv, k2t=k2t, q2=q2,
                         s2=s2_step, t2=t2, pv2=pv2, oproj2=oproj2, logits=logits, lt=lt, dispatch=dispatch, slots=slots,
                         hidden=hidden, outer=outer, comb=comb, combine=combine)
            run("pe", steps, a=0)
            run("pe", steps, a=1, b=0)
            with pe.Fori(1, B - 1) as b:
                run("pe", steps, a=b + 1, b=b, late=b - 1)
            run("pe", steps, b=B - 1, late=B - 2)
            run("pe", steps, late=B - 1)

        @block.scalar
        def _(act):
            def copy(o, i):
                return nc.scalar.activation(o, i, ACT.Copy)

            def halves(bank, rows=P):
                return ps[0:rows, bank, :].rearrange("p (k s) -> p k s", k=2)

            def xt(a, n):
                act.wait_ge(s[f"xt{n}_ps"], nth(f"xt{n}_ps", a, 1))
                copy(xt_hi[:, :, :], halves(0 if n == 1 else 1)).then_inc(s[f"xt{n}_hi"], 1)

            def qk(a, g):
                act.wait_ge(s["qk_ps"], nth("qk_ps", a, g + 1))
                if g >= 2:
                    act.wait_ge(s["s_ps"], nth("s_ps", a, 4 * (g - 1)))
                bank = ring_bank("qk", g)
                nc.scalar.activation(qk_f[g % 2][:, 0, :], ps[:, bank, 0:S], ACT.Identity, scale=ATTN_SCALE,
                                     bias=cols[:, BQ + g:BQ + g + 1])
                nc.scalar.activation(qk_f[g % 2][:, 1, :], ps[:, bank, S:2 * S], ACT.Identity,
                                     bias=cols[:, BK + g:BK + g + 1]).then_inc(s["qk_sb"], 1)

            def ex(a, h):
                act.wait_ge(s["mx"], nth("mx", a, h + 1))
                if h >= 2:
                    act.wait_ge(s["t_ps"], nth("t_ps", a, h - 1))
                for t in range(NT):
                    last = nc.scalar.activation(p_sb[:, h % 2, t, :], ps[:, ring_bank("head", h), t * S:(t + 1) * S],
                                                ACT.Exp, bias=mx[:, h, t:t + 1], accum_out=ls[:, h, t:t + 1])
                last.then_inc(s["ex"], 1)

            def pt(a, h):
                act.wait_ge(s["t_ps"], nth("t_ps", a, h + 1))
                if h >= 2:
                    act.wait_ge(s["pv"], nth("pv", a, h - 1))
                copy(pt_hi[:, h % 2, :, :], halves(3 + h % 2)).then_inc(s["pt_hi"], 1)

            def ot(a, g):
                act.wait_ge(s["pv"], nth("pv", a, 4 * g + 4))
                copy(ot_hi[:, g, :], ps[:, 0, 0:S]).then_inc(s["ot_hi"], 1)

            def q2(a, g):
                act.wait_ge(s["q2_ps"], nth("q2_ps", a, g + 1))
                if g >= 2:
                    act.wait_ge(s["s2_ps"], nth("s2_ps", a, g - 1))
                nc.scalar.activation(q2_f[:, g % 2, :], ps[:, 0, 0:S], ACT.Identity, scale=XATTN_SCALE,
                                     bias=cols[:, BQ2 + g:BQ2 + g + 1]).then_inc(s["q2_sb"], 1)

            def ex2(a, g):
                act.wait_ge(s["sh2"], nth("sh2", a, g + 1))
                nc.scalar.activation(s2[:, g % 2, :, :], s2[:, g % 2, :, :], ACT.Exp).then_inc(s["ex2"], 1)

            def t2(a, g, u):
                n = 2 * g + u
                act.wait_ge(s["t2_ps"], nth("t2_ps", a, n + 1))
                if n >= 2:
                    act.wait_ge(s["pv2"], nth("pv2", a, n - 1))
                copy(pt2_hi[:, u, :, :], halves(3 + u, CTX)).then_inc(s["pt2_hi"], 1)

            def ot2(a, g):
                act.wait_ge(s["pv2"], nth("pv2", a, 2 * g + 2))
                if g == 0:
                    act.wait_ge(s["o_ps"], nth("o_ps", a, 1))
                copy(ot_hi[:, g, :], ps[:, 2, 0:S]).then_inc(s["ot2_hi"], 1)

            def logits(a, k):
                act.wait_ge(s["lg_ps"], nth("lg_ps", a, k + 1))
                if later(a):
                    act.wait_ge(s["ec"], nth("ec", a - 1, NC))
                t, u = divmod(k, 2)
                copy(lg[:, t, u * 512:(u + 1) * 512], ps[:, (2, 3, 4, 0)[k], :]).then_inc(s["lg_sb"], 1)

            def ed(b, c):
                act.wait_ge(s["cm"], nth("cm", b, c + 1))
                for e in range(2):
                    k = 2 * c + e
                    last = nc.scalar.activation(edt[:, e, :], ps[:, 6, e * S:(e + 1) * S], ACT.Exp,
                                                bias=cm[:, k:k + 1], accum_out=csum[:, k:k + 1])
                last.then_inc(s["ed"], 1)

            def ec(b, c):
                if c == 0:
                    act.wait_ge(s["rm"], nth("rm", b, 2))
                    if later(b):
                        act.wait_ge(s["cb_ps"], nth("cb_ps", b - 1, NC))
                        act.wait_ge(s["rs_sum"], nth("rs_sum", b - 1, 1))
                else:
                    act.wait_ge(s["cb_ps"], nth("cb_ps", b, c))
                for t in range(NT):
                    last = nc.scalar.activation(ecomb[:, t, :], lg[:, t, c * CHUNK:(c + 1) * CHUNK], ACT.Exp,
                                                bias=rm[:, t:t + 1], accum_out=rsum[:, t, c:c + 1])
                last.then_inc(s["ec"], 1)

            def ds(b, c):
                act.wait_ge(s["ds_ps"], nth("ds_ps", b, c + 1))
                if c >= 2 or later(b):
                    act.wait_ge(s["d_ps"], nth("d_ps", b, c - 1))
                copy(ds_hi[:, :, :], halves(6)).then_inc(s["ds_hi"], 1)

            def sl(b, c):
                act.wait_ge(s["sl_ps"], nth("sl_ps", b, c + 1))
                if c or later(b):
                    act.wait_ge(s["h_ps"], nth("h_ps", b, 4 * c))
                copy(sl_hi[:, :, :], halves(5)).then_inc(s["sl_hi"], 1)

            def ge(b, c, q):
                n = 4 * c + q
                act.wait_ge(s["h_ps"], nth("h_ps", b, n + 1))
                if (c or later(b)) and q == 0:
                    act.wait_ge(s["pr_ps"], nth("pr_ps", b, c))
                nc.scalar.activation(h_f[:, 2 * q:2 * q + 2, :], halves(6 - q % 2), ACT.Gelu).then_inc(s["ge"], 1)

            def pr(b, c):
                act.wait_ge(s["pr_ps"], nth("pr_ps", b, c + 1))
                copy(pr_hi[:, :, :], halves(7)).then_inc(s["pr_hi"], 1)

            def cb(b, c):
                act.wait_ge(s["cb_ps"], nth("cb_ps", b, c + 1))
                if c < NC - 1 or more(b):
                    act.wait_ge(s["sl_ps"], nth("sl_ps", b, c + 2))
                copy(cb_hi[:, :, :], halves(6)).then_inc(s["cb_hi"], 1)

            for name in WEIGHTS:
                act.wait_ge(s["i_" + name], 16)
                if name == "w1":
                    act.wait_ge(s["i_w1g"], 1)
                copy(W[name][0][:, :, :], stage[name][:, :, :]).then_inc(s["i_hi"], 1)
            act.wait_ge(s["i_sg"], 2)
            copy(W["se"][0][:, :, :], se_t[:, :, :]).then_inc(s["i_shi"], 1)
            act.wait_ge(s["i_cols"], 1)

            steps = dict(xt=xt, qk=qk, ex=ex, pt=pt, ot=ot, q2=q2, ex2=ex2, t2=t2, ot2=ot2, logits=logits, ed=ed,
                         ec=ec, ds=ds, sl=sl, ge=ge, pr=pr, cb=cb)
            run("act", steps, a=0)
            run("act", steps, a=1, b=0)
            with act.Fori(1, B - 1) as b:
                run("act", steps, a=b + 1, b=b, late=b - 1)
            run("act", steps, b=B - 1, late=B - 2)
            run("act", steps, late=B - 1)

        @block.vector
        def _(dve):
            V = nc.vector

            def minus(o, a, hi):
                return V.tensor_tensor(o, a, hi.bitcast(f32), ALU.subtract)

            def halves(bank, rows=P):
                return ps[0:rows, bank, :].rearrange("p (k s) -> p k s", k=2)

            def stats(a, n):
                src = (x, x1, x2)[n - 1]
                if n == 1:
                    dve.wait_ge(s["x_in"], nth("x_in", a, 16))
                else:
                    dve.wait_ge(s[f"x{n - 1}"], nth(f"x{n - 1}", a, 1))
                for t in range(NT):
                    last = V.bn_stats(st[:, t, :], src[:, t, :])
                last.then_inc(s[f"ln{n}_st"], 1)
                dve.wait_ge(s[f"ln{n}_st"], nth(f"ln{n}_st", a, 1))
                dve.sem_inc(s["dve_held"], 1)
                for t in range(NT):
                    last = V.bn_aggr(mv[:, t, :], st[:, t, :])
                last.then_inc(s[f"ln{n}_mv"], 1)
                dve.wait_ge(s[f"ln{n}_mv"], nth(f"ln{n}_mv", a, 1))
                V.tensor_scalar(ve[:, 0, :], mv[:, :, 1], LN_EPS, None, ALU.add)
                V.tensor_scalar(ve[:, 1, :], mv[:, :, 1], 1.0, None, ALU.mult).then_inc(s[f"ln{n}_ve"], 1)

            def xh_step(a, n):
                src = (x, x1, x2)[n - 1]
                dve.wait_ge(s[f"ln{n}_pw"], nth(f"ln{n}_pw", a, 1))
                scale = pw[:, 0, :]
                if n == 3:
                    V.tensor_tensor(sc3[:, 0, :], pw[:, 0, :], pw[:, 1, :], ALU.mult).then_inc(s["ln3_sc"], 1)
                    dve.wait_ge(s["ln3_sc"], nth("ln3_sc", a, 1))
                    V.tensor_scalar(sc3[:, 1, :], sc3[:, 0, :], float(D) ** 0.5, RMS_EPS, ALU.mult, ALU.max)\
                        .then_inc(s["ln3_sc"], 1)
                    dve.wait_ge(s["ln3_sc"], nth("ln3_sc", a, 2))
                    V.reciprocal(sc3[:, 2, :], sc3[:, 1, :]).then_inc(s["ln3_sc"], 1)
                    dve.wait_ge(s["ln3_sc"], nth("ln3_sc", a, 3))
                    V.scalar_tensor_tensor(sc3[:, 3, :], sc3[:, 2, :], float(D) ** 0.5, pw[:, 0, :], ALU.mult, ALU.mult)\
                        .then_inc(s["ln3_sc"], 1)
                    dve.wait_ge(s["ln3_sc"], nth("ln3_sc", a, 4))
                    scale = sc3[:, 3, :]
                for t in range(NT):
                    last = V.tensor_scalar(xh[:, t, :], src[:, t, :], mv[:, t, 0:1], scale[:, t:t + 1],
                                           ALU.subtract, ALU.mult)
                last.then_inc(s[f"ln{n}_xh"], 1)

            def xt(a, n):
                dve.wait_ge(s[f"xt{n}_hi"], nth(f"xt{n}_hi", a, 1))
                minus(xt_lo[:, :, :], halves(0 if n == 1 else 1), xt_hi[:, :, :]).then_inc(s[f"xt{n}_lo"], 1)

            def v(a):
                dve.wait_ge(s["v_ps"], nth("v_ps", a, 1))
                V.tensor_tensor(v_f[:, :, :], halves(ring_bank("v")), bv[:, :].unsqueeze(1).broadcast_to([P, NT, D]), ALU.add)\
                    .then_inc(s["v_sb"], 1)

            def qk(a, g):
                dve.wait_ge(s["qk_sb"], nth("qk_sb", a, g + 1))
                f, h, lo = qk_f[g % 2], qk_h[g % 2], qk_l[g % 2]
                V.tensor_copy(h[:, :, :], f[:, :, :]).then_inc(s["qk_hi"], 1)
                dve.wait_ge(s["qk_hi"], nth("qk_hi", a, g + 1))
                V.scalar_tensor_tensor(lo[:, 0, :], h[:, 0, :].bitcast(f32), cols[:, NMASK:NMASK + 1],
                                       f[:, 0, :], ALU.mult, ALU.add)
                minus(lo[:, 1, :], f[:, 1, :], h[:, 1, :]).then_inc(s["qk_lo"], 1)

            def mx_step(a, h):
                dve.wait_ge(s["s_ps"], nth("s_ps", a, h + 1))
                V.tensor_reduce(mx[:, h, :], halves(ring_bank("head", h)), AX, ALU.max, negate=True).then_inc(s["mx"], 1)

            def rl_step(a, h):
                dve.wait_ge(s["ex"], nth("ex", a, h + 1))
                V.reciprocal(rl[:, h, :], ls[:, h, :]).then_inc(s["rl"], 1)

            def pt(a, h):
                dve.wait_ge(s["pt_hi"], nth("pt_hi", a, h + 1))
                minus(pt_lo[:, h % 2, :, :], halves(3 + h % 2), pt_hi[:, h % 2, :, :]).then_inc(s["pt_lo"], 1)

            def ot(a, g):
                dve.wait_ge(s["ot_hi"], nth("ot_hi", a, g + 1))
                minus(ot_lo[:, g, :], ps[:, 0, 0:S], ot_hi[:, g, :]).then_inc(s["ot_lo"], 1)

            def x1_step(a):
                dve.wait_ge(s["o_ps"], nth("o_ps", a, 1))
                dve.wait_ge(s["x_bo"], nth("x_bo", a, 1))
                V.tensor_tensor(x1[:, :, :], halves(0), x[:, :, :], ALU.add).then_inc(s["x1"], 1)

            def kv(a):
                dve.wait_ge(s["kv_ps"], nth("kv_ps", a, 1))
                dve.wait_ge(s["vg_lo"], nth("vg_lo", a, H))
                kin = ps[0:CTX, ring_bank("kv"), 0:D].rearrange("p (h d) -> p h d", h=H)
                kb = bkv2[:, 0:D].rearrange("p (h d) -> p h d", h=H)
                for e in range(2):
                    last = V.tensor_tensor(k2d[:, :, e, :], kin, kb, ALU.add)
                last.then_inc(s["kd_sb"], 1)
                V.tensor_tensor(v2_f[:, :], ps[0:CTX, ring_bank("kv"), D:2 * D], bkv2[:, D:2 * D], ALU.add).then_inc(s["v2_sb"], 1)

            def mask(a):
                dve.wait_ge(s["mask_in"], nth("mask_in", a, 16))
                V.tensor_scalar(mk_f[:, :], mk_i[:, :], 0.0, -3.0e38, ALU.is_equal, ALU.mult).then_inc(s["mk"], 1)
                dve.wait_ge(s["mk"], nth("mk", a, 1))
                V.tensor_scalar(mk_f[:, :], mk_f[:, :], 4.0, None, ALU.mult).then_inc(s["mk"], 1)

            def k2t(a):
                dve.wait_ge(s["k2t_ps"], nth("k2t_ps", a, 1))
                V.tensor_copy(k2_n[:, :, :], ps[:, ring_bank("k2t"), 0:G * CTX].rearrange("p (g c) -> p g c", g=G))\
                    .then_inc(s["k2_n"], 1)

            def q2(a, g):
                dve.wait_ge(s["q2_sb"], nth("q2_sb", a, g + 1))
                V.tensor_copy(qk_h[0][:, g % 2, :], q2_f[:, g % 2, :]).then_inc(s["q2_hi"], 1)
                dve.wait_ge(s["q2_hi"], nth("q2_hi", a, g + 1))
                V.scalar_tensor_tensor(q2_a[:, g % 2, :], qk_h[0][:, g % 2, :].bitcast(f32), cols[:, NMASK:NMASK + 1],
                                       q2_f[:, g % 2, :], ALU.mult, ALU.add).then_inc(s["q2_a"], 1)

            def s2_step(a, g):
                dve.wait_ge(s["s2_ps"], nth("s2_ps", a, g + 1))
                if g == 0:
                    dve.wait_ge(s["mk"], nth("mk", a, 2))
                if g >= 2:
                    dve.wait_ge(s["t2_ps"], nth("t2_ps", a, 2 * g - 2))
                V.tensor_tensor(s2[:, g % 2, :, :].rearrange("p t (r c) -> p t r c", r=R),
                                ps[:, 0:NT, 0:R * CTX].rearrange("p t (r c) -> p t r c", r=R),
                                mk_f[:, :].unsqueeze(1).unsqueeze(1).broadcast_to([P, NT, R, CTX]), ALU.add)\
                    .then_inc(s["s2_sb"], 1)
                dve.wait_ge(s["s2_sb"], nth("s2_sb", a, g + 1))
                V.tensor_reduce(mx2[:, g, :, :], s2[:, g % 2, :, :].rearrange("p t (r c) -> p (t r) c", r=R), AX,
                                ALU.max, negate=True).then_inc(s["mx2"], 1)
                dve.wait_ge(s["mx2"], nth("mx2", a, g + 1))
                w = s2[:, g % 2, :, :].rearrange("p t (r c) -> p (t r) c", r=R)
                V.tensor_tensor(w, w, mx2[:, g, :, :].rearrange("p t r -> p (t r)").unsqueeze(2)
                                .broadcast_to([P, NT * R, CTX]), ALU.add).then_inc(s["sh2"], 1)

            def n2(a, g):
                dve.wait_ge(s["ex2"], nth("ex2", a, g + 1))
                w = s2[:, g % 2, :, :].rearrange("p t (r c) -> p (t r) c", r=R)
                V.tensor_reduce(ls2[:, g, :, :], w, AX, ALU.add).then_inc(s["sm2"], 1)
                dve.wait_ge(s["sm2"], nth("sm2", a, g + 1))
                V.reciprocal(rl2[:, g, :, :], ls2[:, g, :, :]).then_inc(s["rl2"], 1)

            def t2(a, g, u):
                dve.wait_ge(s["pt2_hi"], nth("pt2_hi", a, 2 * g + u + 1))
                minus(pt2_lo[:, u, :, :], halves(3 + u, CTX), pt2_hi[:, u, :, :]).then_inc(s["pt2_lo"], 1)

            def ot2(a, g):
                dve.wait_ge(s["ot2_hi"], nth("ot2_hi", a, g + 1))
                minus(ot_lo[:, g, :], ps[:, 2, 0:S], ot_hi[:, g, :]).then_inc(s["ot2_lo"], 1)

            def x2_step(a):
                dve.wait_ge(s["o2_ps"], nth("o2_ps", a, 1))
                dve.wait_ge(s["x1_bo"], nth("x1_bo", a, 1))
                if later(a):
                    dve.wait_ge(s["res"], nth("res", a - 1, 1))
                V.tensor_tensor(x2[:, :, :], halves(0), x1[:, :, :], ALU.add).then_inc(s["x2"], 1)

            def xs(a):
                dve.wait_ge(s["ln3_xh"], nth("ln3_xh", a, 1))
                V.tensor_copy(xs_hi[:, :, :], xh[:, :, :]).then_inc(s["xs_hi"], 1)
                dve.wait_ge(s["xs_hi"], nth("xs_hi", a, 1))
                minus(xs_lo[:, :, :], xh[:, :, :], xs_hi[:, :, :]).then_inc(s["xs_lo"], 1)

            def keep(b):
                dve.wait_ge(s["x2"], nth("x2", b, 1))
                if later(b):
                    dve.wait_ge(s["y"], nth("y", b - 1, 1))
                V.tensor_copy(res[:, :, :], x2[:, :, :]).then_inc(s["res"], 1)

            def row_max(b):
                dve.wait_ge(s["lg_sb"], nth("lg_sb", b, 4))
                for t in range(NT):
                    V.tensor_reduce(rm[:, t:t + 1], lg[:, t, :], AX, ALU.max, negate=True).then_inc(s["rm"], 1)

            def cm_step(b, c):
                dve.wait_ge(s["lt_ps"], nth("lt_ps", b, c + 1))
                V.tensor_reduce(cm[:, 2 * c:2 * c + 2], halves(6), AX, ALU.max, negate=True).then_inc(s["cm"], 1)

            def edn(b, c):
                dve.wait_ge(s["ed"], nth("ed", b, c + 1))
                V.reciprocal(crec[:, 2 * c:2 * c + 2], csum[:, 2 * c:2 * c + 2]).then_inc(s["rc"], 1)
                dve.wait_ge(s["rc"], nth("rc", b, c + 1))
                for e in range(2):
                    last = V.tensor_scalar(edt[:, e, :], edt[:, e, :], crec[:, 2 * c + e:2 * c + e + 1], None, ALU.mult)
                last.then_inc(s["edn"], 1)

            def ds(b, c):
                dve.wait_ge(s["ds_hi"], nth("ds_hi", b, c + 1))
                minus(ds_lo[:, :, :], halves(6), ds_hi[:, :, :]).then_inc(s["ds_lo"], 1)

            def sl(b, c):
                dve.wait_ge(s["sl_hi"], nth("sl_hi", b, c + 1))
                minus(sl_lo[:, :, :], halves(5), sl_hi[:, :, :]).then_inc(s["sl_lo"], 1)

            def hid(b, c, q):
                n = 4 * c + q
                dve.wait_ge(s["ge"], nth("ge", b, n + 1))
                V.tensor_copy(h_hi[:, 2 * q:2 * q + 2, :], h_f[:, 2 * q:2 * q + 2, :]).then_inc(s["h_hi"], 1)

            def pr(b, c):
                dve.wait_ge(s["pr_hi"], nth("pr_hi", b, c + 1))
                minus(pr_lo[:, :, :], halves(7), pr_hi[:, :, :]).then_inc(s["pr_lo"], 1)

            def cb(b, c):
                dve.wait_ge(s["cb_hi"], nth("cb_hi", b, c + 1))
                minus(cb_lo[:, :, :], halves(6), cb_hi[:, :, :]).then_inc(s["cb_lo"], 1)

            def acc_step(b, c):
                dve.wait_ge(s["d_ps"], nth("d_ps", b, c + 1))
                if c == 0:
                    dve.wait_ge(s["out"], nth("out", b, 16))
                    V.tensor_copy(acc[:, :, :], halves(7)).then_inc(s["acc"], 1)
                else:
                    dve.wait_ge(s["acc"], nth("acc", b, c))
                    V.tensor_tensor(acc[:, :, :], halves(7), acc[:, :, :], ALU.add).then_inc(s["acc"], 1)

            def finish(b):
                dve.wait_ge(s["ec"], nth("ec", b, NC))
                V.tensor_reduce(rtot[:, :], rsum[:, :, :], AX, ALU.add).then_inc(s["rs_sum"], 1)
                dve.wait_ge(s["rs_sum"], nth("rs_sum", b, 1))
                V.reciprocal(rrec[:, :], rtot[:, :]).then_inc(s["rr"], 1)
                dve.wait_ge(s["rr"], nth("rr", b, 1))
                dve.wait_ge(s["acc"], nth("acc", b, NC))
                dve.wait_ge(s["res"], nth("res", b, 1))
                for t in range(NT):
                    last = V.scalar_tensor_tensor(acc[:, t, :], acc[:, t, :], rrec[:, t:t + 1], res[:, t, :],
                                                  ALU.mult, ALU.add)
                last.then_inc(s["y"], 1)

            dve.wait_ge(s["i_const"], 16)
            V.tensor_scalar(cols[:, BQ:BQ + G], cols[:, BQ:BQ + G], ATTN_SCALE, None, ALU.mult)
            V.tensor_scalar(cols[:, BQ2:BQ2 + G], cols[:, BQ2:BQ2 + G], XATTN_SCALE, None, ALU.mult)\
                .then_inc(s["i_cols"], 1)
            dve.wait_ge(s["i_bias"], 16)
            dve.wait_ge(s["i_se"], 16)
            V.tensor_tensor(se_sq[:, :, :], g_se[:, :, :], g_se[:, :, :], ALU.mult).then_inc(s["i_sq"], 1)
            dve.wait_ge(s["i_sq"], 1)
            V.tensor_reduce(se_ss[:, :], se_sq[:, :, :], AX, ALU.add).then_inc(s["i_st"], 1)
            dve.wait_ge(s["i_sr"], 4)
            for e in range(NS):
                last = V.tensor_scalar(g_se[:, e, :], g_se[:, e, :], se_sc[:, e:e + 1], None, ALU.mult)
            last.then_inc(s["i_xn"], 1)
            dve.wait_ge(s["i_gam"], 16)
            V.tensor_tensor(gxs[:, :], gam[:, 0, :], gam[:, 1, :], ALU.mult).then_inc(s["i_gxs"], 1)
            dve.wait_ge(s["i_w1"], 16)
            for dk in range(ND):
                last = V.tensor_scalar(stage["w1"][:, dk, :], stage["w1"][:, dk, :], gam[:, 0, dk:dk + 1], None, ALU.mult)
            last.then_inc(s["i_w1g"], 1)
            for n, name in enumerate(WEIGHTS):
                dve.wait_ge(s["i_hi"], n + 1)
                minus(W[name][1][:, :, :], stage[name][:, :, :], W[name][0][:, :, :]).then_inc(s["i_lo"], 1)
            dve.wait_ge(s["i_sps"], 1)
            dve.wait_ge(s["i_gxs"], 1)
            for dk in range(ND):
                V.tensor_scalar(se_t[:, dk, :], ps[:, 2 * dk:2 * dk + 2, :].rearrange("p u n -> p (u n)"),
                                gxs[:, dk:dk + 1], None, ALU.mult).then_inc(s["i_sg"], 1)
            dve.wait_ge(s["i_sg"], 2)
            dve.wait_ge(s["i_shi"], 1)
            minus(W["se"][1][:, :, :], se_t[:, :, :], W["se"][0][:, :, :]).then_inc(s["i_slo"], 1)

            steps = dict(stats=stats, xh=xh_step, xt=xt, v=v, qk=qk, mx=mx_step, rl=rl_step, pt=pt, ot=ot, x1=x1_step,
                         kv=kv, mask=mask, k2t=k2t, q2=q2, s2=s2_step, n2=n2, t2=t2, ot2=ot2, x2=x2_step, xs=xs,
                         keep=keep, row_max=row_max, cm=cm_step, edn=edn, ds=ds, sl=sl, hid=hid, pr=pr, cb=cb,
                         acc=acc_step, finish=finish)
            run("dve", steps, a=0)
            run("dve", steps, a=1, b=0)
            with dve.Fori(1, B - 1) as b:
                run("dve", steps, a=b + 1, b=b, late=b - 1)
            run("dve", steps, b=B - 1, late=B - 2)
            run("dve", steps, late=B - 1)

        @block.gpsimd
        def _(pool):
            Q = nc.gpsimd

            def copy(o, i):
                return Q.tensor_scalar(o, i, 1.0, None, ALU.mult)

            def power(o, i, col, w):
                return Q.tensor_tensor(o, i, cols[:, col:col + 1].broadcast_to([P, w]), ALU.pow)

            def rstd(a, n):
                pool.wait_ge(s[f"ln{n}_ve"], nth(f"ln{n}_ve", a, 1))
                w = 2 if n < 3 else 4
                Q.tensor_tensor(pw[:, :, :].rearrange("p a b -> p (a b)")[:, 0:w],
                                ve[:, :, :].rearrange("p a b -> p (a b)")[:, 0:w],
                                cols[:, EXPO:EXPO + w], ALU.pow).then_inc(s[f"ln{n}_pw"], 1)

            def bias(a, n):
                o, row, signal = ((x, bo, "x_bo"), (x1, bo2, "x1_bo"))[n - 1]
                pool.wait_ge(s[f"ln{n}_xh"], nth(f"ln{n}_xh", a, 1))
                Q.tensor_tensor(o[:, :, :], o[:, :, :], row[:, :].unsqueeze(1).broadcast_to([P, NT, D]), ALU.add)\
                    .then_inc(s[signal], 1)

            def context(a):
                pool.wait_ge(s["ctx_in"], nth("ctx_in", a, 16))
                pool.sem_inc(s["pool_held"], 1)
                copy(cx_hi[:, :, :], cx[:, :, :]).then_inc(s["ct_hi"], 1)
                pool.wait_ge(s["ct_hi"], nth("ct_hi", a, 1))
                Q.tensor_tensor(cx_lo[:, :, :], cx[:, :, :], cx_hi[:, :, :].bitcast(f32), ALU.subtract)\
                    .then_inc(s["ct_lo"], 1)

            def hid(b, c, q):
                pool.wait_ge(s["h_hi"], nth("h_hi", b, 4 * c + q + 1))
                part = slice(2 * q, 2 * q + 2)
                Q.tensor_tensor(h_lo[:, part, :], h_f[:, part, :], h_hi[:, part, :].bitcast(f32), ALU.subtract)\
                    .then_inc(s["h_lo"], 1)

            def nm(a, g):
                pool.wait_ge(s["rl2"], nth("rl2", a, g + 1))
                w = s2[:, g % 2, :, :].rearrange("p t (r c) -> p (t r) c", r=R)
                Q.tensor_tensor(w, w, rl2[:, g, :, :].rearrange("p t r -> p (t r)").unsqueeze(2)
                                .broadcast_to([P, NT * R, CTX]), ALU.mult).then_inc(s["pn2"], 1)

            def pn(a, h):
                pool.wait_ge(s["rl"], nth("rl", a, h + 1))
                Q.tensor_tensor(p_sb[:, h % 2, :, :], p_sb[:, h % 2, :, :],
                                rl[:, h, :].unsqueeze(2).broadcast_to([P, NT, S]), ALU.mult).then_inc(s["pn"], 1)

            def vg_step(a, h):
                r = h % R
                pool.wait_ge(s["v_sb"], nth("v_sb", a, 1))
                if h >= R:
                    pool.wait_ge(s["pv"], nth("pv", a, h - R + 1))
                elif later(a):
                    pool.wait_ge(s["pv2"], nth("pv2", a - 1, 8))
                pool.sem_inc(s["pool_held"], 1)
                src = v_f[:, :, h * HD:(h + 1) * HD]
                copy(vg[:, :, r, 0:HD], src).then_inc(s["vg_hi"], 1)
                pool.wait_ge(s["vg_hi"], nth("vg_hi", a, h + 1))
                Q.tensor_tensor(vg[:, :, r, HD:2 * HD], src, vg[:, :, r, 0:HD].bitcast(f32), ALU.subtract)\
                    .then_inc(s["vg_lo"], 1)

            def k2(a, g):
                pool.wait_ge(s["k2_n"], nth("k2_n", a, 1))
                if g:
                    pool.wait_ge(s["s2_ps"], nth("s2_ps", a, g))
                Q.tensor_tensor(k2_f[:, :, :], k2_n[:, g, :].unsqueeze(1).broadcast_to([P, R, CTX]),
                                cols[:, BM:BM + R].unsqueeze(2).broadcast_to([P, R, CTX]), ALU.mult)\
                    .then_inc(s["k2_f"], 1)
                pool.wait_ge(s["k2_f"], nth("k2_f", a, g + 1))
                pool.sem_inc(s["pool_held"], 1)
                flat = k2_f[:, :, :].rearrange("p r c -> p (r c)")
                copy(k2_hi[:, :], flat).then_inc(s["k2_hi"], 1)
                pool.wait_ge(s["k2_hi"], nth("k2_hi", a, g + 1))
                Q.tensor_tensor(k2_lo[:, :], flat, k2_hi[:, :].bitcast(f32), ALU.subtract).then_inc(s["k2_lo"], 1)

            def v2(a, g):
                pool.wait_ge(s["v2_sb"], nth("v2_sb", a, 1))
                if g >= 2:
                    pool.wait_ge(s["pv2"], nth("pv2", a, 2 * (g - 1)))
                else:
                    pool.wait_ge(s["pv"], nth("pv", a, H))
                pool.sem_inc(s["pool_held"], 1)
                src = v2_f[:, g * R * HD:(g + 1) * R * HD].rearrange("p (r d) -> p r d", r=R)
                copy(vg[0:CTX, g % 2, :, 0:HD], src).then_inc(s["vg2_hi"], 1)
                pool.wait_ge(s["vg2_hi"], nth("vg2_hi", a, g + 1))
                Q.tensor_tensor(vg[0:CTX, g % 2, :, HD:2 * HD], src, vg[0:CTX, g % 2, :, 0:HD].bitcast(f32),
                                ALU.subtract).then_inc(s["vg2_lo"], 1)

            Q.memset(vg[:, :, :, :].bitcast(f32), 0.0).then_inc(s["i_vz"], 1)
            pool.wait_ge(s["i_vz"], 1)
            pool.wait_ge(s["i_const"], 16)
            pool.wait_ge(s["i_st"], 1)
            power(se_n[:, :], se_ss[:, :], EXPO + 2, NS).then_inc(s["i_sr"], 1)
            pool.wait_ge(s["i_sr"], 1)
            Q.tensor_scalar(se_n[:, :], se_n[:, :], RMS_EPS, None, ALU.max).then_inc(s["i_sr"], 1)
            pool.wait_ge(s["i_sr"], 2)
            power(se_i[:, :], se_n[:, :], EXPO + 4, NS).then_inc(s["i_sr"], 1)
            pool.wait_ge(s["i_sr"], 3)
            Q.tensor_scalar(se_sc[:, :], se_i[:, :], float(D) ** 0.5, None, ALU.mult).then_inc(s["i_sr"], 1)
            pool.wait_ge(s["i_bias"], 16)

            steps = dict(rstd=rstd, bias=bias, context=context, nm=nm, hid=hid, pn=pn, vg=vg_step, k2=k2, v2=v2)
            run("pool", steps, a=0)
            run("pool", steps, a=1, b=0)
            with pool.Fori(1, B - 1) as b:
                run("pool", steps, a=b + 1, b=b, late=b - 1)
            run("pool", steps, b=B - 1, late=B - 2)
            run("pool", steps, late=B - 1)

        @block.sync
        def _(sp):
            def tokens(t, b):
                return t[bass.ds(b, 1), :, :].rearrange("o (t p) d -> p (o t) d", p=P)

            def load_x(b):
                if later(b):
                    sp.wait_ge(s["x1"], nth("x1", b - 1, 1))
                sp.dma_start(x[:, :, :], tokens(t_in["x"], b)).then_inc(s["x_in"], 16)

            def load_ctx(b):
                if later(b):
                    sp.wait_ge(s["kv_ps"], nth("kv_ps", b - 1, 1))
                    sp.wait_ge(s["mk"], nth("mk", b - 1, 2))
                sp.dma_start(cx[:, :, :], t_in["ctxT"][bass.ds(b, 1), :, :].rearrange("o (k p) c -> p (o k) c", p=P))\
                    .then_inc(s["ctx_in"], 16)
                sp.dma_start(mk_i[:, :], t_in["mask"][bass.ds(b, 1), :].broadcast_to([P, CTX])).then_inc(s["mask_in"], 16)

            def store(b):
                sp.wait_ge(s["y"], nth("y", b, 1))
                sp.dma_start(tokens(out, b), acc[:, :, :]).then_inc(s["out"], 16)

            def load(name):
                sp.dma_start(stage[name][:, :, :], t_in[name]).then_inc(s["i_" + name], 16)

            sp.sem_inc(s["out"], 16)
            sp.dma_start(consts[:, :], t_in["consts"]).then_inc(s["i_const"], 16)
            sp.dma_start(g_se[:, :, :], t_in["se"].rearrange("(e p) d -> p e d", p=P)).then_inc(s["i_se"], 16)
            sp.dma_start(biases[:, :], t_in["bias"].broadcast_to([P, 5 * D])).then_inc(s["i_bias"], 16)
            sp.dma_start(gam[:, :, :], t_in["gam"]).then_inc(s["i_gam"], 16)
            load("w1")
            for name in WEIGHTS:
                if name != "w1":
                    load(name)
            load_ctx(0)
            sp.wait_ge(s["i_xn"], 1)
            sp.wait_ge(s["i_sps"], 1)
            load_x(0)
            load_x(1)
            load_ctx(1)
            with sp.Fori(1, B - 1) as b:
                load_x(b + 1)
                load_ctx(b + 1)
                store(b - 1)
            store(B - 2)
            store(B - 1)
            sp.wait_ge(s["out"], 16 * (B + 1))


def kernel(**inputs):
    import numpy as _np
    import concourse.bacc as _bacc
    from concourse import mybir as _mybir
    from concourse.bass_utils import run_bass_kernel_spmd as _run

    a = {n: _np.asarray(v) for n, v in inputs.items()}
    sa, xa, ff = "L0_attn_", "L0_xattn_", "L0_ffn_"

    def twice(w, axis):
        shape = w.shape[:axis] + (H, HD) + w.shape[axis + 1:]
        w = w.reshape(shape)
        return _np.concatenate([w, w], axis=axis + 1).reshape(w.shape[:axis] + (2 * H * HD,) + w.shape[axis + 2:])

    def on_partitions(w):
        return w.reshape(-1, P, w.shape[-1]).transpose(1, 0, 2)

    def by_group(v):
        return twice(v, 0).reshape(G, P).T

    rows = _np.arange(P)
    consts = _np.zeros((P, P + NCOLS), _np.float32)
    consts[:, :P] = _np.eye(P, dtype=_np.float32)
    for r in range(R):
        consts[32 * r:32 * r + 32, P + BM + r] = 1.0
    consts[rows % 32 >= HD, P + NMASK] = -1.0
    consts[:, P + EXPO:P + EXPO + 5] = _np.array([-0.5, -0.5, 0.5, 0.5, -1.0], _np.float32)
    consts[:, P + BQ:P + BQ + G] = by_group(a[sa + "bq"])
    consts[:, P + BK:P + BK + G] = by_group(a[sa + "bk"])
    consts[:, P + BQ2:P + BQ2 + G] = by_group(a[xa + "bq"])
    host = {
        "x": a["x"],
        "ctxT": a["ctx_1024"].transpose(0, 2, 1),
        "mask": a["mask_Bx1x1xS2_if1"].reshape(B, CTX),
        "consts": consts,
        "bias": _np.concatenate([a[sa + "bv"], a[sa + "bo"], a[xa + "bk"], a[xa + "bv"], a[xa + "bo"]])[None, :],
        "gam": _np.stack([a[ff + "gamma_x"], a[ff + "gamma_slot"]]).reshape(2, ND, P).transpose(2, 0, 1),
        "se": a[ff + "slot_embeds"].reshape(SLOTS, D),
        "wqk": on_partitions(_np.concatenate([twice(a[sa + "Wq"].T, 1), twice(a[sa + "Wk"].T, 1)], axis=1)),
        "wv": on_partitions(a[sa + "Wv"].T),
        "wo": on_partitions(twice(a[sa + "Wo"].T, 0)),
        "wkv2": on_partitions(_np.concatenate([a[xa + "Wk"].T, a[xa + "Wv"].T], axis=1)),
        "wq2": on_partitions(twice(a[xa + "Wq"].T, 1)),
        "wo2": on_partitions(twice(a[xa + "Wo"].T, 0)),
        "w1": on_partitions(a[ff + "w1"]),
        "w2": on_partitions(a[ff + "w2"]),
    }
    nc = _bacc.Bacc("TRN2", target_bir_lowering=False, num_devices=1)
    arrays, t_in = {}, {}
    for name, v in host.items():
        v = _np.ascontiguousarray(v)
        arrays["in_" + name] = v
        t_in[name] = nc.dram_tensor("in_" + name, v.shape, _mybir.dt.from_np(v.dtype), kind="ExternalInput").ap()
    out = nc.dram_tensor("out_0", (B, S, D), _mybir.dt.float32, kind="ExternalOutput").ap()
    decoder_layer(nc, t_in, out)
    r = _run(nc, [arrays], core_ids=[0])
    return r.results[0]["out_0"]
```
